# Optimizing a Trainium2 kernel written in Bass

```python
import numpy as np
import jax
import jax.numpy as jnp

def _softmax(x, axis=-1):
    return jax.nn.softmax(x, axis=axis)

def _gelu(x):
    return jax.nn.gelu(x, approximate=True)

def _silu(x):
    return jax.nn.silu(x)

def _sigmoid(x):
    return jax.nn.sigmoid(x)

def _layernorm(x, axis=-1, eps=1e-05):
    m = jnp.mean(x, axis=axis, keepdims=True)
    v = jnp.var(x, axis=axis, keepdims=True)
    return (x - m) / jnp.sqrt(v + eps)

def _scatter_add(tgt, idx, src, axis=0):
    return tgt.at[idx].add(src)

def _segment_sum(src, seg, n):
    return jax.ops.segment_sum(src, seg, n)
kernel_name = 'mk_flamingo_gated_d2_seqx_r8_1b48c5'

def setup_inputs(seed: int=0):
    np.random.seed(seed)
    _w = jnp.asarray

    def _rec_inputs():
        import jax
        import jax.numpy as jnp
        _rk = jax.random.key(seed)
        x = -0.0003929 + 0.9999 * jax.random.normal(jax.random.fold_in(_rk, 1), (8, 128, 128), jnp.float32)
        _lenS = 128 - jax.random.randint(jax.random.fold_in(_rk, 7), (8,), 0, max(1, 128 // 4) + 1, jnp.int32)
        _lenS2 = 77 - jax.random.randint(jax.random.fold_in(_rk, 8), (8,), 0, max(1, 77 // 4) + 1, jnp.int32)
        _ctx_1024P = jax.random.normal(jax.random.fold_in(_rk, 11), (8, 16, 128), jnp.float32)
        _ctx_1024c = jax.random.dirichlet(jax.random.fold_in(_rk, 511), 0.3 * jnp.ones((16,), jnp.float32), (8, 77))
        _ctx_1024t = jnp.einsum('bsk,bkd->bsd', _ctx_1024c, _ctx_1024P)
        _ctx_1024t = _ctx_1024t * jax.lax.rsqrt(jnp.mean(jnp.square(_ctx_1024t)) + 1e-12) * 0.953939
        ctx_1024 = -1.39393e-06 + 0.999914 * (_ctx_1024t + 0.3 * jax.random.normal(jax.random.fold_in(_rk, 611), (8, 77, 128), jnp.float32))
        _g = jax.random.normal(jax.random.fold_in(_rk, 9001), (2, 2), jnp.float32)
        _g = jnp.sign(_g) * jnp.maximum(jnp.abs(_g), 1.0) + (_g == 0) * 1.0
        g_xattn = _g[0]
        g_ffn = _g[1]
        return (x, ctx_1024, g_xattn, g_ffn)
    x, ctx_1024, g_xattn, g_ffn = _rec_inputs()

    def _L0_xattn_setup():
        import jax, jax.numpy as jnp
        import numpy as np
        EMBED_DIM = 128
        Q_HEADS = 16
        KV_HEADS = 8
        HEAD_DIM = EMBED_DIM // Q_HEADS
        KV_EMBED = HEAD_DIM * KV_HEADS
        GROUPS = Q_HEADS // KV_HEADS
        LN_EPS = 1e-05
        RMS_EPS = 1e-06

        def _rms_norm(x):
            return x * jax.lax.rsqrt(jnp.mean(jnp.square(x), axis=-1, keepdims=True) + RMS_EPS)

        def _act_quant(x):
            scale = 127.0 / jnp.maximum(jnp.max(jnp.abs(x), axis=-1, keepdims=True), 1e-05)
            return jnp.clip(jnp.round(x * scale), -128.0, 127.0) / scale

        def _weight_quant(w):
            scale = 1.0 / jnp.maximum(jnp.mean(jnp.abs(w)), 1e-05)
            return jnp.clip(jnp.round(w * scale), -1.0, 1.0) / scale

        def _ste(a, q):
            return a + jax.lax.stop_gradient(q - a)

        def bit_linear(x, w):
            xn = _rms_norm(x)
            xq = _ste(xn, _act_quant(xn))
            wq = _ste(w, _weight_quant(w))
            return jnp.einsum('bni,oi->bno', xq, wq)
        key = jax.random.key(seed)
        ks = jax.random.split(key, 6)
        B, N, S, D = (16, 128, 32, EMBED_DIM)
        s = D ** (-0.5)
        return {'x': jax.random.normal(ks[0], (B, N, D), jnp.float32), 'y': jax.random.normal(ks[1], (B, S, D), jnp.float32), 'wq': jax.random.normal(ks[2], (D, D), jnp.float32) * s, 'wk': jax.random.normal(ks[3], (KV_EMBED, D), jnp.float32) * s, 'wv': jax.random.normal(ks[4], (KV_EMBED, D), jnp.float32) * s, 'wo': jax.random.normal(ks[5], (D, D), jnp.float32) * s, 'ln_gamma': jnp.ones((D,), jnp.float32), 'ln_beta': jnp.zeros((D,), jnp.float32)}
    _L0_xattn_all = _L0_xattn_setup()
    _L0_xattn_in = {k: v for k, v in _L0_xattn_all.items() if k in ('wq', 'wk', 'wv', 'wo', 'ln_gamma', 'ln_beta')}
    del _L0_xattn_all

    def _L0_ffn_setup():
        import jax, jax.numpy as jnp
        import numpy as np
        EPS = 1e-09
        key = jax.random.key(seed)
        k0, k1, k2, k3 = jax.random.split(key, 4)
        B, S, H, F, E = (4, 256, 128, 256, 8)
        return {'hidden_states': jax.random.normal(k0, (B, S, H), dtype=jnp.float32), 'router_w': jax.random.normal(k1, (H, E), dtype=jnp.float32) * 0.02, 'w1': jax.random.normal(k2, (E, H, F), dtype=jnp.float32) * 0.02, 'w2': jax.random.normal(k3, (E, F, H), dtype=jnp.float32) * 0.02}
    _L0_ffn_all = _L0_ffn_setup()
    _L0_ffn_in = {k: v for k, v in _L0_ffn_all.items() if k in ('router_w', 'w1', 'w2')}
    del _L0_ffn_all

    def _L1_xattn_setup():
        import jax, jax.numpy as jnp
        import numpy as np
        EMBED_DIM = 128
        NUM_HEADS = 16
        HEAD_DIM = EMBED_DIM // NUM_HEADS
        B, S = (4, 256)
        key = jax.random.key(seed)
        ks = jax.random.split(key, 12)
        sc = 1.0 / np.sqrt(EMBED_DIM)
        inp = {'query': jax.random.normal(ks[0], (B, S, EMBED_DIM), jnp.float32), 'key': jax.random.normal(ks[1], (B, S, EMBED_DIM), jnp.float32), 'value': jax.random.normal(ks[2], (B, S, EMBED_DIM), jnp.float32), 'Wq': jax.random.normal(ks[3], (EMBED_DIM, EMBED_DIM), jnp.float32) * sc, 'bq': jax.random.normal(ks[4], (EMBED_DIM,), jnp.float32) * sc, 'Wk': jax.random.normal(ks[5], (EMBED_DIM, EMBED_DIM), jnp.float32) * sc, 'bk': jax.random.normal(ks[6], (EMBED_DIM,), jnp.float32) * sc, 'Wv': jax.random.normal(ks[7], (EMBED_DIM, EMBED_DIM), jnp.float32) * sc, 'bv': jax.random.normal(ks[8], (EMBED_DIM,), jnp.float32) * sc, 'Wo': jax.random.normal(ks[9], (EMBED_DIM, EMBED_DIM), jnp.float32) * sc, 'bo': jax.random.normal(ks[10], (EMBED_DIM,), jnp.float32) * sc}
        return inp
    _L1_xattn_all = _L1_xattn_setup()
    _L1_xattn_in = {k: v for k, v in _L1_xattn_all.items() if k in ('Wq', 'bq', 'Wk', 'bk', 'Wv', 'bv', 'Wo', 'bo')}
    del _L1_xattn_all

    def _L1_ffn_setup():
        import jax, jax.numpy as jnp
        import numpy as np
        B, S, H, F, E = (8, 256, 128, 512, 8)
        INIT_LAMBDA = 0.2
        key = jax.random.key(seed)
        ks = jax.random.split(key, 12)
        std = 0.02
        return {'hidden_states': jax.random.normal(ks[0], (B, S, H), jnp.float32), 'gate_w1': jax.random.normal(ks[1], (H, H), jnp.float32) * 0.01, 'gate_b1': jnp.zeros((H,), jnp.float32), 'gate_w2': jax.random.normal(ks[2], (E, H), jnp.float32) * 0.01, 'gate_b2': jnp.full((E,), INIT_LAMBDA, jnp.float32), 'W1': jax.random.normal(ks[3], (F, H), jnp.float32) * std, 'b1': jax.random.normal(ks[4], (F,), jnp.float32) * std, 'W2': jax.random.normal(ks[5], (H, F), jnp.float32) * std, 'b2': jax.random.normal(ks[6], (H,), jnp.float32) * std, 'TW1': jax.random.normal(ks[7], (E, F, H), jnp.float32) * std, 'Tb1': jax.random.normal(ks[8], (E, F), jnp.float32) * std, 'TW2': jax.random.normal(ks[9], (E, H, F), jnp.float32) * std, 'Tb2': jax.random.normal(ks[10], (E, H), jnp.float32) * std}
    _L1_ffn_all = _L1_ffn_setup()
    _L1_ffn_in = {k: v for k, v in _L1_ffn_all.items() if k in ('gate_w1', 'gate_b1', 'gate_w2', 'gate_b2', 'W1', 'b1', 'W2', 'b2', 'TW1', 'Tb1', 'TW2', 'Tb2')}
    del _L1_ffn_all
    return {'x': x, 'ctx_1024': ctx_1024, 'g_xattn': g_xattn, 'g_ffn': g_ffn, 'L0_xattn_wq': _L0_xattn_in['wq'], 'L0_xattn_wk': _L0_xattn_in['wk'], 'L0_xattn_wv': _L0_xattn_in['wv'], 'L0_xattn_wo': _L0_xattn_in['wo'], 'L0_xattn_ln_gamma': _L0_xattn_in['ln_gamma'], 'L0_xattn_ln_beta': _L0_xattn_in['ln_beta'], 'L0_ffn_router_w': _L0_ffn_in['router_w'], 'L0_ffn_w1': _L0_ffn_in['w1'], 'L0_ffn_w2': _L0_ffn_in['w2'], 'L1_xattn_Wq': _L1_xattn_in['Wq'], 'L1_xattn_bq': _L1_xattn_in['bq'], 'L1_xattn_Wk': _L1_xattn_in['Wk'], 'L1_xattn_bk': _L1_xattn_in['bk'], 'L1_xattn_Wv': _L1_xattn_in['Wv'], 'L1_xattn_bv': _L1_xattn_in['bv'], 'L1_xattn_Wo': _L1_xattn_in['Wo'], 'L1_xattn_bo': _L1_xattn_in['bo'], 'L1_ffn_gate_w1': _L1_ffn_in['gate_w1'], 'L1_ffn_gate_b1': _L1_ffn_in['gate_b1'], 'L1_ffn_gate_w2': _L1_ffn_in['gate_w2'], 'L1_ffn_gate_b2': _L1_ffn_in['gate_b2'], 'L1_ffn_W1': _L1_ffn_in['W1'], 'L1_ffn_b1': _L1_ffn_in['b1'], 'L1_ffn_W2': _L1_ffn_in['W2'], 'L1_ffn_b2': _L1_ffn_in['b2'], 'L1_ffn_TW1': _L1_ffn_in['TW1'], 'L1_ffn_Tb1': _L1_ffn_in['Tb1'], 'L1_ffn_TW2': _L1_ffn_in['TW2'], 'L1_ffn_Tb2': _L1_ffn_in['Tb2']}

def reference(x, ctx_1024, g_xattn, g_ffn, L0_xattn_wq, L0_xattn_wk, L0_xattn_wv, L0_xattn_wo, L0_xattn_ln_gamma, L0_xattn_ln_beta, L0_ffn_router_w, L0_ffn_w1, L0_ffn_w2, L1_xattn_Wq, L1_xattn_bq, L1_xattn_Wk, L1_xattn_bk, L1_xattn_Wv, L1_xattn_bv, L1_xattn_Wo, L1_xattn_bo, L1_ffn_gate_w1, L1_ffn_gate_b1, L1_ffn_gate_w2, L1_ffn_gate_b2, L1_ffn_W1, L1_ffn_b1, L1_ffn_W2, L1_ffn_b2, L1_ffn_TW1, L1_ffn_Tb1, L1_ffn_TW2, L1_ffn_Tb2):
    import jax
    import jax.numpy as jnp

    def _L0_xattn_ref(x, y, wq, wk, wv, wo, ln_gamma, ln_beta):
        import jax, jax.numpy as jnp
        import numpy as np
        EMBED_DIM = 128
        Q_HEADS = 16
        KV_HEADS = 8
        HEAD_DIM = EMBED_DIM // Q_HEADS
        KV_EMBED = HEAD_DIM * KV_HEADS
        GROUPS = Q_HEADS // KV_HEADS
        LN_EPS = 1e-05
        RMS_EPS = 1e-06

        def _rms_norm(x):
            return x * jax.lax.rsqrt(jnp.mean(jnp.square(x), axis=-1, keepdims=True) + RMS_EPS)

        def _act_quant(x):
            scale = 127.0 / jnp.maximum(jnp.max(jnp.abs(x), axis=-1, keepdims=True), 1e-05)
            return jnp.clip(jnp.round(x * scale), -128.0, 127.0) / scale

        def _weight_quant(w):
            scale = 1.0 / jnp.maximum(jnp.mean(jnp.abs(w)), 1e-05)
            return jnp.clip(jnp.round(w * scale), -1.0, 1.0) / scale

        def _ste(a, q):
            return a + jax.lax.stop_gradient(q - a)

        def bit_linear(x, w):
            xn = _rms_norm(x)
            xq = _ste(xn, _act_quant(xn))
            wq = _ste(w, _weight_quant(w))
            return jnp.einsum('bni,oi->bno', xq, wq)
        B, N, D = x.shape
        S = y.shape[1]
        q = bit_linear(x, wq).reshape(B, N, Q_HEADS, HEAD_DIM)
        k = bit_linear(y, wk).reshape(B, S, KV_HEADS, HEAD_DIM)
        v = bit_linear(y, wv).reshape(B, S, KV_HEADS, HEAD_DIM)
        q = jnp.transpose(q, (0, 2, 1, 3)) / HEAD_DIM ** 0.5
        q = q.reshape(B, KV_HEADS, GROUPS, N, HEAD_DIM)
        k = jnp.transpose(k, (0, 2, 1, 3))
        v = jnp.transpose(v, (0, 2, 1, 3))
        scores = jnp.einsum('bhgnd,bhsd->bhgns', q, k)
        attn = jax.nn.softmax(scores, axis=-1)
        out = jnp.einsum('bhgns,bhsd->bhgnd', attn, v)
        out = jnp.transpose(out, (0, 3, 1, 2, 4)).reshape(B, N, D)
        mu = jnp.mean(out, axis=-1, keepdims=True)
        var = jnp.mean(jnp.square(out - mu), axis=-1, keepdims=True)
        out = (out - mu) * jax.lax.rsqrt(var + LN_EPS) * ln_gamma + ln_beta
        return bit_linear(out, wo)

    def _L0_ffn_ref(hidden_states, router_w, w1, w2):
        import jax, jax.numpy as jnp
        import numpy as np
        EPS = 1e-09
        TOP_K = 2
        orig_shape = hidden_states.shape
        H = orig_shape[-1]
        E = router_w.shape[-1]
        flat = hidden_states.reshape(-1, H)
        T = flat.shape[0]
        gate_logits = flat @ router_w
        gate_probs = jax.nn.softmax(gate_logits, axis=-1)
        topk_w, topk_idx = jax.lax.top_k(gate_probs, TOP_K)
        topk_w = topk_w / jnp.clip(topk_w.sum(-1, keepdims=True), EPS)
        cw = jnp.zeros((T, E), dtype=flat.dtype).at[jnp.arange(T)[:, None], topk_idx].add(topk_w)
        h = jax.nn.silu(jnp.einsum('td,edf->etf', flat, w1))
        y = jnp.einsum('etf,efd->etd', h, w2)
        out = jnp.einsum('etd,te->td', y, cw)
        return out.reshape(orig_shape)

    def _L1_xattn_ref(query, key, value, Wq, bq, Wk, bk, Wv, bv, Wo, bo):
        import jax, jax.numpy as jnp
        import numpy as np
        EMBED_DIM = 128
        NUM_HEADS = 16
        HEAD_DIM = EMBED_DIM // NUM_HEADS
        B, S = (4, 256)
        b = query.shape[0]

        def proj(x, W, bias):
            y = x @ W.T + bias
            return y.reshape(b, -1, NUM_HEADS, HEAD_DIM).transpose(0, 2, 1, 3)
        Q = proj(query, Wq, bq)
        K = proj(key, Wk, bk)
        V = proj(value, Wv, bv)
        scale = 1.0 / jnp.sqrt(jnp.asarray(HEAD_DIM, Q.dtype))
        energy = jnp.einsum('bhqd,bhkd->bhqk', Q, K) * scale
        attn = jax.nn.softmax(energy, axis=-1)
        x = jnp.einsum('bhqk,bhkd->bhqd', attn, V)
        x = x.transpose(0, 2, 1, 3).reshape(b, -1, EMBED_DIM)
        return x @ Wo.T + bo

    def _L1_ffn_ref(hidden_states, gate_w1, gate_b1, gate_w2, gate_b2, W1, b1, W2, b2, TW1, Tb1, TW2, Tb2):
        import jax, jax.numpy as jnp
        import numpy as np
        B, S, H, F, E = (8, 256, 128, 512, 8)
        INIT_LAMBDA = 0.2
        x = hidden_states
        h = jax.nn.relu(jnp.einsum('bsh,oh->bso', x, gate_w1) + gate_b1)
        g = jnp.einsum('bso,eo->bse', h, gate_w2) + gate_b2
        g = g.mean(axis=1)
        mW1 = W1 + jnp.einsum('be,efh->bfh', g, TW1)
        mb1 = b1 + g @ Tb1
        mW2 = W2 + jnp.einsum('be,ehf->bhf', g, TW2)
        mb2 = b2 + g @ Tb2
        u = jax.nn.gelu(jnp.einsum('bsh,bfh->bsf', x, mW1) + mb1[:, None, :])
        out = jnp.einsum('bsf,bhf->bsh', u, mW2) + mb2[:, None, :]
        return out
    x = x + jnp.tanh(g_xattn[0]) * _L0_xattn_ref(_layernorm(x, axis=-1), ctx_1024, L0_xattn_wq, L0_xattn_wk, L0_xattn_wv, L0_xattn_wo, L0_xattn_ln_gamma, L0_xattn_ln_beta)
    x = x + jnp.tanh(g_ffn[0]) * _L0_ffn_ref(_layernorm(x, axis=-1), L0_ffn_router_w, L0_ffn_w1, L0_ffn_w2)
    x = x + jnp.tanh(g_xattn[1]) * _L1_xattn_ref(_layernorm(x, axis=-1), ctx_1024, ctx_1024, L1_xattn_Wq, L1_xattn_bq, L1_xattn_Wk, L1_xattn_bk, L1_xattn_Wv, L1_xattn_bv, L1_xattn_Wo, L1_xattn_bo)
    x = x + jnp.tanh(g_ffn[1]) * _L1_ffn_ref(_layernorm(x, axis=-1), L1_ffn_gate_w1, L1_ffn_gate_b1, L1_ffn_gate_w2, L1_ffn_gate_b2, L1_ffn_W1, L1_ffn_b1, L1_ffn_W2, L1_ffn_b2, L1_ffn_TW1, L1_ffn_Tb1, L1_ffn_TW2, L1_ffn_Tb2)
    return x

_drawn_inputs = setup_inputs


def setup_inputs(seed=0):
    import zlib

    import numpy as np

    out = dict(_drawn_inputs(seed))
    spreads = {'g_ffn': (-1.0, 0.6),
     'L0_xattn_ln_gamma': (1.0, 0.2),
     'L0_xattn_ln_beta': (0.0, 0.1),
     'L1_ffn_gate_b1': (0.0, 0.8),
     'L1_ffn_gate_b2': (0.20000000298023224, 0.6)}
    factors = {'L0_ffn_router_w': 3.998,
     'L0_ffn_w1': 3.484,
     'L0_ffn_w2': 3.481,
     'L1_xattn_bq': 3.271,
     'L1_xattn_bk': 8.0,
     'L1_ffn_gate_w1': 8.0,
     'L1_ffn_gate_w2': 8.0,
     'L1_ffn_b1': 8.0,
     'L1_ffn_b2': 3.965,
     'L1_ffn_Tb1': 8.0,
     'L1_ffn_Tb2': 6.948}
    for name, (base, spread) in spreads.items():
        noise = np.random.default_rng([zlib.crc32(name.encode()), seed]).standard_normal(out[name].shape)
        drawn = base * np.exp(spread * noise) if base else spread * noise
        out[name] = jnp.asarray(drawn.astype(out[name].dtype))
    for name, factor in factors.items():
        out[name] = (out[name] * factor).astype(out[name].dtype)
    return out
```

```python
from contextlib import ExitStack

import numpy as np

import concourse.bass as bass
from concourse import mybir

F32 = mybir.dt.float32
BF16 = mybir.dt.bfloat16
FP16 = mybir.dt.float16
ACT = mybir.ActivationFunctionType
ALU = mybir.AluOpType
AX = mybir.AxisListType

B, TOK, D = 8, 128, 128
NK = 77
H, HD, KVH = 16, 8, 8
E0, F0 = 8, 256
E1, F1 = 8, 512
R = D // E1
NJ = D // R
CK0, CK1 = F0 // 128, F1 // 128
WAVES = 2
WB = B // WAVES
WT = WB * TOK
PARTS = 3
PAIRS = [(0, 0), (0, 1), (1, 0), (1, 1), (0, 2), (2, 0)]
QK_ROWS = len(PAIRS) * HD
ST_ROWS = QK_ROWS + PARTS
VW = HD + 1
PGROUP = 4
NG = H // PGROUP
PRING = 3
MAGIC = 1.5 * 2.0 ** 23
ROWS = 3 * D + 4
A_SPLIT = [(0, 6), (6, 12), (12, 16)]

NORMS = (["ctx0"] + [("q0", w) for w in range(WAVES)]
         + [(k, w) for w in range(WAVES) for k in ("mid0", "rms0")]
         + [("moe", w) for w in range(WAVES)] + [("q1", w) for w in range(WAVES)]
         + [("ffn1", w) for w in range(WAVES)])
NORM_FORM = {"ctx0": (1.0 / D, 1e-6), "q0": (1.0 + 1e-6, 1e-11), "mid0": (1.0, 1e-5), "rms0": (1.0 / D, 1e-6),
             "moe": (1.0, 1e-5), "q1": (1.0, 1e-5), "ffn1": (1.0, 1e-5)}


def bank_uses():
    waves = range(WAVES)
    t = ["wsum"] + [(k, i) for i in range(2) for k in ("y0T",)] + [("k0", 0), ("k0", 1), ("v0", 0)]
    t += [(k, w) for w in waves for k in ("q0T", "q0")]
    t += [("max0T", w) for w in waves]
    t += [(k, w) for w in waves for k in ("post0T", "post0")]
    t += [("y1T", 0), ("y1T", 1), ("k1", 0), ("k1", 1), ("v1", 0), ("v1", 1)]
    t += [(k, w) for w in waves for k in ("moeT", "router")]
    t += [(k, w) for w in waves for k in ("q1T", "q1")]
    t += [("max1T", w) for w in waves]
    t += [(k, w) for w in waves for k in ("post1T", "post1")]
    t += [(k, w) for w in waves for k in ("ffnT", "gate")]
    t += ["gexp", "gaug", "mb1"]
    a = [("A0", b, c) for b in range(B) for c in range(3)] + [("y", w, e) for w in waves for e in range(E0)]
    a += [("A1", b, c) for b in range(B) for c in range(3)] + [("mix", c) for c in range(2 * NJ)]
    s = [("S0", b, g) for b in range(B) for g in range(NG)]
    s += [("h", w, e, c) for w in waves for e in range(E0) for c in range(CK0)]
    s += [("S1", b, g) for b in range(B) for g in range(NG)] + [("u", b) for b in range(B)]
    t += [("out", b) for b in range(B)]
    o = [("O0", b) for b in range(B)] + [("O1", b) for b in range(B)]
    return {"t": t, "a": a, "s": s, "o": o}


def build(nc, io):
    ctx = ExitStack()
    with ctx:
        def sb(name, shape, dt=F32):
            return ctx.enter_context(nc.sbuf_tensor(name, shape, dt))

        sems = {}

        def sem(name):
            if name not in sems:
                sems[name] = ctx.enter_context(nc.semaphore(name))
            return sems[name]

        rings = {r: [ctx.enter_context(nc.psum_tensor(f"ps_{r}{i}", [128, 512], F32)) for i in range(2)]
                 for r in "taso"}
        place = {}
        for r, uses in bank_uses().items():
            for i, key in enumerate(uses):
                assert key not in place
                place[key] = (r, i % 2, i // 2)

        def bank(key):
            r, i, _ = place[key]
            return rings[r][i]

        def bank_full(key):
            r, i, _ = place[key]
            return sem(f"full_{r}{i}")

        def bank_free(key):
            r, i, _ = place[key]
            return sem(f"free_{r}{i}")

        def wait_full(eng, key):
            eng.wait_ge(bank_full(key), place[key][2] + 1)

        def wait_read(eng, key):
            eng.wait_ge(bank_free(key), place[key][2] + 1)

        def wait_free(eng, key):
            if place[key][2]:
                eng.wait_ge(bank_free(key), place[key][2])

        x = sb("x", [128, B, D])
        y = sb("y", [NK, B, D])
        attn = sb("attn", [128, B, D])
        yq = attn[0:NK, :, :]
        yT = sb("yT", [128, B * NK])
        const = sb("const", [128, 128 + R + 8])
        ident, rowsel, rank = const[:, 0:128], const[:, 128:128 + R], const[:, 128 + R:]
        identb = sb("identb", [128, 128], BF16)
        ones = sb("ones", [128, 128])
        neghalf = sb("neghalf", [128, 8])
        rows = sb("rows", [128, ROWS])
        gamma, beta, bo = (rows[:, i * D:(i + 1) * D] for i in range(3))
        tg = sb("tg", [128, 4])
        w0 = sb("w0", [128, 448])
        w0q = sb("w0q", [128, 448])
        w0part = [(0, 128), (128, 256), (256, 384), (384, 448)]
        wsum = sb("wsum", [128, 4])
        wsc = sb("wsc", [128, 4])
        winv = sb("winv", [128, 4])
        w1 = sb("w1", [128, 512])
        bias1 = sb("bias1", [128, 3])
        router = sb("router", [128, E0])
        moe = sb("moe", [128, 2, E0, F0])
        moe1 = moe[:, 0, :, :]
        moe2 = moe[:, 1, :, :].rearrange("p e (c d) -> p e c d", c=CK0)
        gate1 = sb("gate1", [128, D])
        gatec = sb("gatec", [128, 2])
        gate2 = sb("gate2", [128, 128 + E1 + 1])
        gaug_b = sb("gaug_b", [E1 + 1, 1])
        tb = sb("tb", [E1 + 1, F1 + D])
        tw = [sb(f"tw{i}", [128, NJ, 512]) for i in range(2)]
        base = [moe[:, :, :, :].rearrange("p a e f -> p (a e f)").rearrange("p (j f) -> p j f", j=NJ),
                sb("base1", [128, NJ, 512])]
        mw = sb("mw", [128, 2, B, 512])
        qst = mw[0:64, :, :, :].rearrange("p a b f -> p (a b f)").bitcast(BF16).rearrange("p (h t) -> p h t", h=H)
        kst = sb("kst", [64, H, B * NK], BF16)
        vst = sb("vst", [NK, B, H, PARTS, VW], BF16)
        lin = sb("lin", [128, WT])
        lin2 = sb("lin2", [128, WT])
        linT = sb("linT", [128, B * TOK])
        proj = sb("proj", [128, 640])
        rest = sb("rest", [128, 640])
        rest2 = sb("rest2", [128, 640])
        parts = sb("parts", [128, PARTS, B * NK], BF16)
        nmax = sb("nmax", [128, B, H])
        mrest = sb("mrest", [128, WB, H])
        mrest2 = sb("mrest2", [128, WB, H])
        mparts = sb("mparts", [128, B, PARTS, H], BF16)
        maxT = sb("maxT", [PARTS * H, WT], BF16)
        p32 = sb("p32", [NK, PRING, 512])
        ph = sb("ph", [NK, PRING, 512], FP16)
        pl = sb("pl", [NK, PRING, 512], FP16)
        osum = sb("osum", [128, H, VW])
        rden = sb("rden", [128, H])
        st = sb("st", [128, WB, 6])
        mv = sb("mv", [128, len(NORMS), WB, 2])
        sq = sb("sq", [128, len(NORMS), 8])
        nin = sb("nin", [128, len(NORMS), 8])
        rstd = sb("rstd", [128, len(NORMS), 8])
        amax = sb("amax", [128, 8])
        am1 = sb("am1", [128, 8])
        am2 = sb("am2", [128, 8])
        comb = sb("comb", [128, 8])
        inv = sb("inv", [128, 8])
        logit = sb("logit", [128, WB, E0])
        lg2 = sb("lg2", [128, WB, E0])
        oh1 = sb("oh1", [128, WB, E0])
        oh2 = sb("oh2", [128, WB, E0])
        code = sb("code", [128, WB, E0])
        cw = sb("cw", [128, WAVES, WB, E0])
        mm = sb("mm", [128, 8, WB])
        ediff = sb("ediff", [128, WAVES, WB])
        gap = sb("gap", [128, WAVES, WB])
        hT = sb("hT", [128, 4, WT])
        mixed = hT
        hs = sb("hs", [128, B])
        relu_out = sb("relu_out", [128, WT])
        gexp = sb("gexp", [128, B])
        gmat = sb("gmat", [128, R, B])
        gaug = sb("gaug", [E1 + 1, B])
        gtok = sb("gtok", [E1 + 1, B, TOK])
        mb1 = sb("mb1", [128, CK1, B])
        uT = sb("uT", [128, 2, CK1, TOK])

        def prob_key(n):
            return f"S{n // (B * NG)}", n // NG % B, n % NG

        norm_no = {k: i for i, k in enumerate(NORMS)}
        block = ctx.enter_context(nc.Block())

        @block.sync
        def _(sp):
            def load(name, dst, src):
                sp.dma_start(dst, src).then_inc(sem("loaded_" + name), 16)

            load("y", y[:, :, :], io["ctx"].rearrange("b s d -> s b d"))
            load("w0", w0[:, :], io["w0"])
            load("const", const[:, :], io["const"])
            load("x", x[:, :, :], io["x"].rearrange("b t d -> t b d"))
            load("rows", rows[:, :], io["rows"].partition_broadcast(128))
            load("w1", w1[:, :], io["w1"])
            load("bias1", bias1[:, :], io["bias1"])
            load("router", router[:, :], io["router"])
            load("moe1", moe1[:, :, :], io["moe1"])
            load("moe2", moe2[:, :, :, :], io["moe2"])
            load("gate1", gate1[:, :], io["gate1"])
            load("gatec", gatec[:, :], io["gatec"])
            load("gate2", gate2[:, :], io["gate2"])
            load("gaug_b", gaug_b[:, :], io["gaug_b"])
            load("tb", tb[:, :], io["tb"])

            def stack_keys(layer):
                sp.wait_ge(sem("k_split"), layer + 1)
                if layer:
                    sp.wait_ge(sem("attn_done"), B)
                for r, (_, kp) in enumerate(PAIRS):
                    sp.dma_start(kst[HD * r:HD * (r + 1), :, :], parts[:, kp, :]).then_inc(sem("k_stacked"), 16)

            def stack_queries(layer, w):
                sp.wait_ge(sem("q_split"), layer * WAVES + w + 1)
                if layer:
                    sp.wait_ge(sem("attn_done"), B)
                for r, (qp, _) in enumerate(PAIRS):
                    sp.dma_start(qst[HD * r:HD * (r + 1), :, w * WT:(w + 1) * WT],
                                 parts[:, qp, 0:WT]).then_inc(sem("q_stacked"), 16)

            def stack_maxima(layer, w):
                wait_read(sp, (f"max{layer}T", w))
                if layer:
                    sp.wait_ge(sem("attn_done"), B)
                sp.dma_start(qst[QK_ROWS:ST_ROWS, :, w * WT:(w + 1) * WT], maxT[:, :]).then_inc(sem("max_stacked"), 16)

            for layer in range(2):
                if layer:
                    for i in (1, 0):
                        load(f"tw{i}", tw[i][:, :, :], io[f"tw{i}"])
                        if i == 0:
                            for e in (E0 - 2, E0 - 1):
                                wait_full(sp, ("y", WAVES - 1, e))
                        load(f"base{i}", base[i][:, :, :], io[f"base{i}"])
                stack_keys(layer)
                for w in range(WAVES):
                    stack_queries(layer, w)
                for w in range(WAVES):
                    stack_maxima(layer, w)
            for c in range(2 * NJ):
                i, j = c // NJ, c % NJ
                wait_read(sp, ("mix", c))
                sp.dma_start(mw[R * j:R * (j + 1), i, :, :], mixed[:, c % 4, :]).then_inc(
                    sem(f"regrouped{c % 4}_{i}"), 16)
            for b in range(B):
                wait_read(sp, ("out", b))
                sp.dma_start(io["out"][b], x[:, b, :]).then_inc(sem("stored"), 16)
            sp.wait_ge(sem("stored"), 16 * B)

        @block.gpsimd
        def _(pool):
            count = [0]

            def link(ins):
                count[0] += 1
                ins.then_inc(sem("pool_chain"), 1)
                pool.wait_ge(sem("pool_chain"), count[0])

            pool.memset(ones[:, :], 1.0)
            link(pool.memset(neghalf[:, :], -0.5))
            link(pool.memset(vst[:, :, :, 0, HD:VW], 1.0))
            link(pool.memset(vst[:, :, :, 1:PARTS, HD:VW], 0.0))
            pool.memset(kst[32:64, :, :], 1.0).then_inc(sem("constants"), 1)
            pool.wait_ge(sem("constants"), 1)

            def inverse_root(key):
                i = norm_no[key]
                kind = key if isinstance(key, str) else key[0]
                scale, eps = NORM_FORM[kind]
                n, p = (8, NK) if kind == "ctx0" else (WB, 128)
                src = sq[0:p, i, 0:n] if kind in ("ctx0", "rms0") else mv[0:p, i, 0:n, 1]
                pool.wait_ge(sem("variance"), i + 1)
                link(pool.tensor_scalar(nin[0:p, i, 0:n], src, scale, eps, ALU.mult, ALU.add))
                pool.tensor_tensor(rstd[0:p, i, 0:n], nin[0:p, i, 0:n], neghalf[0:p, 0:n],
                                   ALU.pow).then_inc(sem("rstd"), 1)

            def prob_rest(layer):
                for n in range(layer * B * NG, (layer + 1) * B * NG):
                    if n % 2:
                        wait_read(pool, prob_key(n))
                        if n >= PRING:
                            pool.wait_ge(sem("pv_done"), n - PRING + 1)
                        s = n % PRING
                        pool.tensor_tensor(pl[:, s, :], p32[:, s, :], ph[:, s, :], ALU.subtract).then_inc(
                            sem("prob_rest_pool"), 1)

            for key in NORMS:
                if key in (("mid0", 0), ("ffn1", 0)):
                    prob_rest(0 if key[0] == "mid0" else 1)
                inverse_root(key)
            wait_read(pool, "gaug")
            pool.tensor_copy(gtok[:, :, :], gaug[:, :].unsqueeze(2).to_broadcast([E1 + 1, B, TOK])).then_inc(
                sem("gtok"), 1)

        @block.scalar
        def _(act):
            count = [0]

            def link(ins):
                count[0] += 1
                ins.then_inc(sem("act_chain"), 1)
                act.wait_ge(sem("act_chain"), count[0])

            def move(key, dst, src, scale=1.0, bias=0.0):
                wait_full(act, key)
                act.activation(dst, src, ACT.Identity, bias=bias, scale=scale).then_inc(bank_free(key), 1)

            act.wait_ge(sem("loaded_rows"), 16)
            act.activation(tg[:, :], rows[:, 3 * D:3 * D + 4], ACT.Tanh).then_inc(sem("tanh_gates"), 1)

            def context(layer):
                wide = WB * NK
                for i in range(2):
                    move((f"y{layer}T", i), yT[:, i * wide:(i + 1) * wide], bank((f"y{layer}T", i))[:, 0:wide])
                if layer:
                    act.wait_ge(sem("loaded_bias1"), 16)
                for i in range(2):
                    if i == 0 and layer:
                        act.wait_ge(sem("v_split"), 1)
                    move((f"k{layer}", i), proj[:, i * wide:(i + 1) * wide], bank((f"k{layer}", i))[:, 0:wide],
                         bias=bias1[:, 1:2] if layer else 0.0)
                for i in range(layer + 1):
                    act.wait_ge(sem("k_split"), layer + 1)
                    if i:
                        act.wait_ge(sem("v_split"), 2)
                    move((f"v{layer}", i), proj[0:NK, 0:512], bank((f"v{layer}", i))[0:NK, :])

            def queries(layer, w):
                if not layer:
                    act.wait_ge(sem("v_split"), 1)
                move((f"q{layer}T", w), linT[:, w * WT:(w + 1) * WT], bank((f"q{layer}T", w))[:, :])
                if w:
                    act.wait_ge(sem("q_split"), layer * WAVES + w)
                if layer:
                    act.wait_ge(sem("scaled_bq"), 1)
                    move(("q1", w), proj[:, 0:WT], bank(("q1", w))[:, :], scale=HD ** -0.5,
                         bias=bias_q[:, 0:1])
                else:
                    move(("q0", w), proj[:, 0:WT], bank(("q0", w))[:, :])

            def maxima(layer, w):
                if w or layer:
                    act.wait_ge(sem("max_stacked"), 16 * (layer * WAVES + w))
                key = (f"max{layer}T", w)
                move(key, maxT[:, :], bank(key)[0:PARTS * H, 0:WT // 2].bitcast(BF16))

            def probs(layer):
                for b in range(B):
                    for g in range(NG):
                        n = (layer * B + b) * NG + g
                        key = (f"S{layer}", b, g)
                        if n >= PRING:
                            act.wait_ge(sem("pv_done"), n - PRING + 1)
                        wait_full(act, key)
                        s = n % PRING
                        act.activation(p32[:, s, :], bank(key)[0:NK, :], ACT.Exp)
                        act.activation(ph[:, s, :], bank(key)[0:NK, :], ACT.Exp).then_inc(bank_free(key), 1)

            bias_q = sb("bias_q", [128, 1])
            context(0)
            for w in range(WAVES):
                queries(0, w)
            for w in range(WAVES):
                maxima(0, w)
            probs(0)
            for w in range(WAVES):
                move(("post0T", w), linT[:, w * WT:(w + 1) * WT], bank(("post0T", w))[:, :])
            context(1)
            for w in range(WAVES):
                move(("moeT", w), linT[:, w * WT:(w + 1) * WT], bank(("moeT", w))[:, :])
                act.wait_ge(sem("gap"), w + 1)
                act.activation(ediff[:, w, :], gap[:, w, :], ACT.Exp).then_inc(sem("ediff"), 1)
                for e in range(E0):
                    for c in range(CK0):
                        n = (w * E0 + e) * CK0 + c
                        key = ("h", w, e, c)
                        if n >= 4:
                            wait_full(act, ("y", (n - 4) // CK0 // E0, (n - 4) // CK0 % E0))
                        wait_full(act, key)
                        act.activation(hT[:, n % 4, :], bank(key)[:, :], ACT.Silu).then_inc(bank_free(key), 1)
            act.wait_ge(sem("loaded_bias1"), 16)
            act.activation(bias_q[:, :], bias1[:, 0:1], ACT.Copy, scale=HD ** -0.5).then_inc(sem("scaled_bq"), 1)
            for w in range(WAVES):
                queries(1, w)
            for w in range(WAVES):
                maxima(1, w)
            probs(1)
            for w in range(WAVES):
                move(("post1T", w), linT[:, w * WT:(w + 1) * WT], bank(("post1T", w))[:, :],
                     bias=bias1[:, 2:3])
            for w in range(WAVES):
                move(("ffnT", w), linT[:, w * WT:(w + 1) * WT], bank(("ffnT", w))[:, :])
                act.wait_ge(sem("loaded_gatec"), 16)
                wait_full(act, ("gate", w))
                for i in range(WB):
                    b = w * WB + i
                    ins = act.activation(relu_out[:, i * TOK:(i + 1) * TOK],
                                         bank(("gate", w))[:, i * TOK:(i + 1) * TOK], ACT.Relu,
                                         bias=gatec[:, 0:1], accum_out=hs[:, b:b + 1])
                ins.then_inc(bank_free(("gate", w)), 1)
                wait_read(act, ("gate", w))
            for b in range(B):
                wait_read(act, "mb1")
                if b >= 2:
                    wait_full(act, ("out", b - 2))
                wait_full(act, ("u", b))
                for c in range(CK1):
                    ins = act.activation(uT[:, b % 2, c, :], bank(("u", b))[:, c * TOK:(c + 1) * TOK],
                                         ACT.Gelu_apprx_tanh, bias=mb1[:, c, b:b + 1])
                ins.then_inc(bank_free(("u", b)), 1)

        @block.tensor
        def _(pe):
            def turn(key, tiles, dt=F32):
                wait_free(pe, key)
                p = bank(key)
                for dst, src, n in tiles(p):
                    i = (identb if dt == BF16 else ident)[0:n, 0:n]
                    ins = pe.transpose(dst, src, i)
                ins.then_inc(bank_full(key), 1)

            def product(key, terms):
                wait_free(pe, key)
                for out, lhsT, rhs, first, last in terms:
                    ins = pe.matmul(out, lhsT, rhs, start=first, stop=last)
                ins.then_inc(bank_full(key), 1)

            wide = WB * NK

            def context(layer):
                src = y if layer else yq
                for i in range(2):
                    key = (f"y{layer}T", i)
                    if not layer:
                        pe.wait_ge(sem("yq"), i + 1)
                    turn(key, lambda p: [(p[:, k * NK:(k + 1) * NK], src[:, i * WB + k, :], NK) for k in range(WB)])
                weights = w1 if layer else w0q
                for i in range(2):
                    wait_read(pe, (f"y{layer}T", i))
                    key = (f"k{layer}", i)
                    product(key, [(bank(key)[:, 0:wide], weights[:, 128:256], yT[:, i * wide:(i + 1) * wide],
                                   True, True)])
                wv = w1[:, 256:384] if layer else w0q[:, 384:448]
                n = wv.shape[1]
                for i in range(layer + 1):
                    key = (f"v{layer}", i)
                    tiles = 512 // n
                    product(key, [(bank(key)[0:NK, k * n:(k + 1) * n], yT[:, (i * tiles + k) * NK:(i * tiles + k + 1) * NK],
                                   wv, True, True) for k in range(tiles)])

            def turn_wave(key, src):
                turn(key, lambda p: [(p[:, k * TOK:(k + 1) * TOK], src[:, k * TOK:(k + 1) * TOK], 128)
                                     for k in range(WB)])

            def queries(layer, w):
                pe.wait_ge(sem(f"lin_q{layer}"), w + 1)
                turn_wave((f"q{layer}T", w), lin)
                wait_read(pe, (f"q{layer}T", w))
                key = (f"q{layer}", w)
                weights = w1 if layer else w0q
                product(key, [(bank(key)[:, :], weights[:, 0:128], linT[:, w * WT:(w + 1) * WT], True, True)])

            def scores_for_max(layer, w):
                pe.wait_ge(sem("q_stacked"), 16 * len(PAIRS) * (layer * WAVES + w + 1))
                pe.wait_ge(sem("k_stacked"), 16 * len(PAIRS) * (layer + 1))
                for b in range(w * WB, (w + 1) * WB):
                    for c, (h0, h1) in enumerate(A_SPLIT):
                        key = (f"A{layer}", b, c)
                        product(key, [(bank(key)[:, (h - h0) * NK:(h - h0 + 1) * NK],
                                       qst[0:QK_ROWS, h, b * TOK:(b + 1) * TOK],
                                       kst[0:QK_ROWS, h, b * NK:(b + 1) * NK], True, True) for h in range(h0, h1)])

            def turn_maxima(layer, w):
                pe.wait_ge(sem("max_split"), layer * WAVES + w + 1)
                turn((f"max{layer}T", w),
                     lambda p: [(p[0:PARTS * H, k * TOK // 2:(k + 1) * TOK // 2].bitcast(BF16),
                                 mparts[:, w * WB + k, :, :].rearrange("t p h -> t (p h)"), 128)
                                for k in range(WB)], BF16)

            def scores(layer, b, g):
                pe.wait_ge(sem("max_stacked"), 16 * (layer * WAVES + b // WB + 1))
                key = (f"S{layer}", b, g)
                product(key, [(bank(key)[0:NK, k * TOK:(k + 1) * TOK],
                               kst[0:ST_ROWS, g * PGROUP + k, b * NK:(b + 1) * NK],
                               qst[0:ST_ROWS, g * PGROUP + k, b * TOK:(b + 1) * TOK], True, True)
                              for k in range(PGROUP)])

            def values(layer, b, g):
                n = (layer * B + b) * NG + g
                key = (f"O{layer}", b)
                if g == 0:
                    wait_free(pe, key)
                pe.wait_ge(sem("prob_rest_pool"), n // 2 + n % 2) if n % 2 else \
                    pe.wait_ge(sem("prob_rest"), n // 2 + 1)
                wait_read(pe, prob_key(n))
                o, s = bank(key), n % PRING
                for k in range(PGROUP):
                    h = g * PGROUP + k
                    col = h * PARTS * VW
                    v = vst[:, b, h if layer else h // 2, :, :].rearrange("s p d -> s (p d)")
                    pe.matmul(o[:, col:col + PARTS * VW], ph[:, s, k * TOK:(k + 1) * TOK], v, start=True, stop=False,
                              skip_group_check=True)
                    ins = pe.matmul(o[:, col:col + 2 * VW], pl[:, s, k * TOK:(k + 1) * TOK], v[:, 0:2 * VW],
                                    start=False, stop=True, skip_group_check=True)
                ins.then_inc(sem("pv_done"), 1)

            def attention(layer):
                for w in range(WAVES):
                    scores_for_max(layer, w)
                for w in range(WAVES):
                    turn_maxima(layer, w)
                pe.wait_ge(sem("v_split"), [1, 3][layer])
                steps = [(b, g) for b in range(B) for g in range(NG)]
                for i in range(len(steps) + 2):
                    if i < len(steps):
                        scores(layer, *steps[i])
                    if i >= 2:
                        values(layer, *steps[i - 2])

            def post(layer, w, weights, src):
                if layer:
                    pe.wait_ge(sem("attn_done"), B + (w + 1) * WB)
                else:
                    pe.wait_ge(sem("lin_post0"), w + 1)
                turn_wave((f"post{layer}T", w), src)
                wait_read(pe, (f"post{layer}T", w))
                key = (f"post{layer}", w)
                product(key, [(bank(key)[:, k * TOK:(k + 1) * TOK],
                               linT[:, (w * WB + k) * TOK:(w * WB + k + 1) * TOK], weights, True, True)
                              for k in range(WB)])

            pe.wait_ge(sem("constants"), 1)
            pe.wait_ge(sem("wsum"), 1)
            product("wsum", [(bank("wsum")[:, 0:4], ones[:, :], wsum[:, :], True, True)])
            pe.wait_ge(sem("loaded_const"), 16)
            pe.wait_ge(sem("w0q"), 1)
            context(0)
            for w in range(WAVES):
                queries(0, w)
            pe.wait_ge(sem("identb"), 1)
            attention(0)
            for w in range(WAVES):
                post(0, w, w0q[:, 256:384], lin)
            pe.wait_ge(sem("loaded_w1"), 16)
            context(1)
            pe.wait_ge(sem("loaded_router"), 16)
            pe.wait_ge(sem("loaded_moe1"), 16)
            pe.wait_ge(sem("loaded_moe2"), 16)
            for w in range(WAVES):
                pe.wait_ge(sem("lin_moe"), w + 1)
                turn_wave(("moeT", w), lin)
                wait_read(pe, ("moeT", w))
                p = bank(("router", w))
                product(("router", w), [(p[:, k * E0:(k + 1) * E0],
                                         linT[:, (w * WB + k) * TOK:(w * WB + k + 1) * TOK], router[:, :], True, True)
                                        for k in range(WB)])

                def hidden(e):
                    for c in range(CK0):
                        key = ("h", w, e, c)
                        product(key, [(bank(key)[:, :], moe1[:, e, c * 128:(c + 1) * 128],
                                       linT[:, w * WT:(w + 1) * WT], True, True)])

                hidden(0)
                for e in range(E0):
                    if e + 1 < E0:
                        hidden(e + 1)
                    n = w * E0 + e
                    for c in range(CK0):
                        wait_read(pe, ("h", w, e, c))
                    key = ("y", w, e)
                    wait_free(pe, key)
                    for k in range(WB):
                        for c in range(CK0):
                            ins = pe.matmul(bank(key)[:, k * D:(k + 1) * D],
                                            hT[:, (CK0 * n + c) % 4, k * TOK:(k + 1) * TOK], moe2[:, e, c, :],
                                            start=(c == 0), stop=(c == CK0 - 1))
                    ins.then_inc(bank_full(key), 1)
            for w in range(WAVES):
                queries(1, w)
            attention(1)
            for w in range(WAVES):
                post(1, w, w1[:, 384:512], attn[:, w * WB:(w + 1) * WB, :].rearrange("t b d -> t (b d)"))
            pe.wait_ge(sem("loaded_gate1"), 16)
            pe.wait_ge(sem("loaded_gate2"), 16)
            pe.wait_ge(sem("loaded_tb"), 16)
            for w in range(WAVES):
                pe.wait_ge(sem("lin_ffn1"), w + 1)
                turn_wave(("ffnT", w), lin)
                wait_read(pe, ("ffnT", w))
                product(("gate", w), [(bank(("gate", w))[:, :], gate1[:, :], linT[:, w * WT:(w + 1) * WT], True, True)])
            for w in range(WAVES):
                wait_read(pe, ("gate", w))
            product("gexp", [(bank("gexp")[:, 0:B], gate2[:, 0:128], hs[:, :], True, True)])
            product("gaug", [(bank("gaug")[0:E1 + 1, 0:B], gate2[:, 128:], hs[:, :], True, True)])
            wait_read(pe, "gaug")
            product("mb1", [(bank("mb1")[:, c * B:(c + 1) * B], tb[:, c * 128:(c + 1) * 128], gaug[:, :], True, True)
                            for c in range(CK1)])
            pe.wait_ge(sem("gmat"), 1)
            for c in range(2 * NJ):
                i, j = c // NJ, c % NJ
                pe.wait_ge(sem(f"loaded_tw{i}"), 16)
                product(("mix", c), [(bank(("mix", c))[:, :], gmat[:, :, :].rearrange("p r b -> p (r b)"),
                                      tw[i][:, j, :], True, True)])

            def ffn_up(b):
                key = ("u", b)
                product(key, [(bank(key)[:, c * TOK:(c + 1) * TOK], mw[:, 0, b, c * 128:(c + 1) * 128],
                               linT[:, b * TOK:(b + 1) * TOK], True, True) for c in range(CK1)])

            for q in range(4):
                pe.wait_ge(sem(f"regrouped{q}_0"), 16 * NJ // 4)
            ffn_up(0)
            pe.wait_ge(sem("gtok"), 1)
            for b in range(B):
                if b + 1 < B:
                    ffn_up(b + 1)
                wait_read(pe, ("u", b))
                if b == 0:
                    for q in range(4):
                        pe.wait_ge(sem(f"regrouped{q}_1"), 16 * NJ // 4)
                key = ("out", b)
                wait_free(pe, key)
                for c in range(CK1):
                    pe.matmul(bank(key)[:, 0:D], uT[:, b % 2, c, :], mw[:, 1, b, c * D:(c + 1) * D],
                              start=(c == 0), stop=False)
                ins = pe.matmul(bank(key)[:, 0:D], gtok[:, b, :], tb[:, F1:F1 + D], start=False, stop=True)
                ins.then_inc(bank_full(key), 1)

        @block.vector
        def _(dve):
            count = [0]

            def link(ins):
                count[0] += 1
                ins.then_inc(sem("dve_chain"), 1)
                dve.wait_ge(sem("dve_chain"), count[0])

            def split(src, d0, d1, d2, r0, r1, done):
                link(dve.tensor_copy(d0, src))
                link(dve.tensor_tensor(r0, src, d0, ALU.subtract))
                link(dve.tensor_copy(d1, r0))
                link(dve.tensor_tensor(r1, r0, d1, ALU.subtract))
                dve.tensor_copy(d2, r1).then_inc(sem(done), 1)

            def statistics(key, src):
                i = norm_no[key]
                for k in range(WB):
                    ins = dve.bn_stats(st[:, k, :], src(k))
                link(ins)
                for k in range(WB):
                    ins = dve.bn_aggr(mv[:, i, k, :], st[:, k, :])
                ins.then_inc(sem("variance"), 1)
                dve.wait_ge(sem("variance"), i + 1)

            def quant_scales(key, p, n):
                i = norm_no[key]
                dve.wait_ge(sem("rstd"), i + 1)
                link(dve.tensor_tensor(am1[0:p, 0:n], amax[0:p, 0:n], rstd[0:p, i, 0:n], ALU.mult))
                link(dve.tensor_scalar(am1[0:p, 0:n], am1[0:p, 0:n], 1e-5, None, ALU.max))
                link(dve.reciprocal(am2[0:p, 0:n], am1[0:p, 0:n]))
                dve.tensor_scalar(inv[0:p, 0:n], am1[0:p, 0:n], 1.0 / 127.0, None, ALU.mult)
                link(dve.scalar_tensor_tensor(out=comb[0:p, 0:n], in0=am2[0:p, 0:n], scalar=127.0,
                                              in1=rstd[0:p, i, 0:n], op0=ALU.mult, op1=ALU.mult))

            def quantise(dst, src, p, n, k0=0):
                for k in range(n):
                    ins = dve.tensor_scalar(dst(k), src(k), comb[0:p, k0 + k:k0 + k + 1], MAGIC, ALU.mult, ALU.add)
                link(ins)
                for k in range(n):
                    ins = dve.tensor_scalar(dst(k), dst(k), -MAGIC, inv[0:p, k0 + k:k0 + k + 1], ALU.add, ALU.mult)
                return ins

            dve.wait_ge(sem("loaded_w0"), 16)
            for i, (a, b) in enumerate(w0part):
                ins = dve.tensor_reduce(wsum[:, i:i + 1], w0[:, a:b], AX.X, ALU.add, apply_absolute_value=True)
            ins.then_inc(sem("wsum"), 1)
            dve.wait_ge(sem("loaded_y"), 16)
            link(dve.tensor_tensor(yq[:, :, :], y[:, :, :], y[:, :, :], ALU.mult))
            dve.tensor_reduce(sq[0:NK, 0, 0:8], yq[:, :, :], AX.X, ALU.add).then_inc(sem("variance"), 1)
            link(dve.tensor_reduce(amax[0:NK, 0:8], y[:, :, :], AX.X, ALU.max, apply_absolute_value=True))
            wait_full(dve, "wsum")
            dve.tensor_scalar(wsc[:, 0:3], bank("wsum")[:, 0:3], 1.0 / (D * D), 1e-5, ALU.mult, ALU.max)
            link(dve.tensor_scalar(wsc[:, 3:4], bank("wsum")[:, 3:4], 1.0 / (D * KVH * HD), 1e-5, ALU.mult, ALU.max))
            dve.reciprocal(winv[:, :], wsc[:, :]).then_inc(bank_free("wsum"), 1)
            dve.wait_ge(bank_free("wsum"), 1)
            link(dve.tensor_scalar(wsc[:, 0:1], wsc[:, 0:1], HD ** -0.5, None, ALU.mult))
            for i, (a, b) in enumerate(w0part):
                ins = dve.tensor_scalar(w0q[:, a:b], w0[:, a:b], winv[:, i:i + 1], MAGIC, ALU.mult, ALU.add)
            link(ins)
            link(dve.tensor_scalar(w0q[:, :], w0q[:, :], -MAGIC, -1.0, ALU.add, ALU.max))
            for i, (a, b) in enumerate(w0part):
                ins = dve.tensor_scalar(w0q[:, a:b], w0q[:, a:b], 1.0, wsc[:, i:i + 1], ALU.min, ALU.mult)
            ins.then_inc(sem("w0q"), 1)
            quant_scales("ctx0", NK, 8)
            for i in range(2):
                quantise(lambda k: yq[:, i * WB + k, :], lambda k: y[:, i * WB + k, :], NK, WB, i * WB).then_inc(
                    sem("yq"), 1)
            dve.wait_ge(sem("loaded_const"), 16)
            dve.tensor_copy(identb[:, :], ident).then_inc(sem("identb"), 1)

            def split_context(layer):
                for i in range(2):
                    wait_read(dve, (f"k{layer}", i))
                if layer:
                    dve.wait_ge(sem("q_stacked"), 16 * len(PAIRS) * WAVES)
                n = B * NK
                split(proj[:, 0:n], *(parts[:, i, :] for i in range(PARTS)), rest[:, 0:n], rest2[:, 0:n], "k_split")
                dve.wait_ge(sem("constants"), 1)
                if layer:
                    dve.wait_ge(sem("attn_done"), B)
                    dve.wait_ge(sem("k_split"), 2)
                for i in range(layer + 1):
                    wait_read(dve, (f"v{layer}", i))
                    if layer == 0:
                        dve.wait_ge(sem("k_split"), 1)
                        dst = [vst[:, :, 0:KVH, p, 0:HD] for p in range(PARTS)]
                        shape = dict(b=B, h=KVH)
                    else:
                        dst = [vst[:, i * WB:(i + 1) * WB, :, p, 0:HD] for p in range(PARTS)]
                        shape = dict(b=WB, h=H)
                        if i:
                            dve.wait_ge(sem("v_split"), 2)

                    def view(t):
                        return t[0:NK, 0:512].rearrange("s (b h d) -> s b h d", **shape)

                    split(view(proj), *dst, view(rest), view(rest2), "v_split")

            def normalise(key, dst, src):
                i = norm_no[key]
                dve.wait_ge(sem("rstd"), i + 1)
                for k in range(WB):
                    ins = dve.tensor_scalar(dst(k), src(k), mv[:, i, k, 0:1], rstd[:, i, k:k + 1],
                                            ALU.subtract, ALU.mult)
                return ins

            def lin_tile(k):
                return lin[:, k * D:(k + 1) * D]

            def lin2_tile(k):
                return lin2[:, k * D:(k + 1) * D]

            def split_queries(layer, w):
                wait_read(dve, (f"q{layer}", w))
                dve.wait_ge(sem("k_stacked"), 16 * len(PAIRS) * (layer + 1))
                if w:
                    dve.wait_ge(sem("q_stacked"), 16 * len(PAIRS) * (layer * WAVES + w))
                split(proj[:, 0:WT], *(parts[:, i, 0:WT] for i in range(PARTS)), rest[:, 0:WT], rest2[:, 0:WT],
                      "q_split")

            def x_tile(w):
                return lambda k: x[:, w * WB + k, :]

            def maxima(layer, w):
                for b in range(w * WB, (w + 1) * WB):
                    for c, (h0, h1) in enumerate(A_SPLIT):
                        key = (f"A{layer}", b, c)
                        wait_full(dve, key)
                        v = bank(key)[:, 0:(h1 - h0) * NK].rearrange("t (h s) -> t h s", s=NK)
                        dve.tensor_reduce(nmax[:, b, h0:h1], v, AX.X, ALU.max, negate=True).then_inc(
                            bank_free(key), 1)
                wait_read(dve, key)
                if layer or w:
                    dve.wait_ge(sem("max_split"), layer * WAVES + w)
                bs = slice(w * WB, (w + 1) * WB)
                split(nmax[:, bs, :], *(mparts[:, bs, p, :] for p in range(PARTS)), mrest[:, :, :], mrest2[:, :, :],
                      "max_split")

            def outputs(layer, b):
                key = (f"O{layer}", b)
                dve.wait_ge(sem("pv_done"), NG * (layer * B + b + 1))
                v = bank(key)[:, 0:H * PARTS * VW].rearrange("t (h p d) -> t h d p", h=H, p=PARTS)
                dve.tensor_reduce(osum[:, :, :], v, AX.X, ALU.add).then_inc(bank_free(key), 1)
                wait_read(dve, key)
                link(dve.reciprocal(rden[:, :], osum[:, :, HD]))
                dve.tensor_tensor(attn[:, b, :].rearrange("t (h d) -> t h d", h=H), osum[:, :, 0:HD],
                                  rden[:, :].unsqueeze(2).to_broadcast([128, H, HD]), ALU.mult).then_inc(
                                      sem("attn_done"), 1)
                dve.wait_ge(sem("attn_done"), layer * B + b + 1)

            def attention(layer):
                for b in range(B):
                    for g in range(NG):
                        n = (layer * B + b) * NG + g
                        if n % 2 == 0:
                            wait_read(dve, prob_key(n))
                            s = n % PRING
                            dve.tensor_tensor(pl[:, s, :], p32[:, s, :], ph[:, s, :], ALU.subtract).then_inc(
                                sem("prob_rest"), 1)
                        if b and g == 2:
                            outputs(layer, b - 1)
                outputs(layer, B - 1)

            def residual(key, w, gate):
                wait_full(dve, key)
                xs = x[:, w * WB:(w + 1) * WB, :].rearrange("t b d -> t (b d)")
                link(dve.scalar_tensor_tensor(out=xs, in0=bank(key)[:, :], scalar=tg[:, gate:gate + 1], in1=xs,
                                              op0=ALU.mult, op1=ALU.add))

            split_context(0)
            dve.wait_ge(sem("loaded_x"), 16)
            for w in range(WAVES):
                key = ("q0", w)
                i = norm_no[key]
                statistics(key, x_tile(w))
                if w:
                    wait_full(dve, ("q0T", w - 1))
                for k in range(WB):
                    ins = dve.tensor_scalar(lin2_tile(k), x_tile(w)(k), mv[:, i, k, 0:1], None, ALU.subtract)
                link(ins)
                link(dve.tensor_reduce(amax[:, 0:WB], lin2[:, :].rearrange("t (b d) -> t b d", b=WB), AX.X, ALU.max,
                                       apply_absolute_value=True))
                quant_scales(key, 128, WB)
                quantise(lin_tile, lin2_tile, 128, WB).then_inc(sem("lin_q0"), 1)
                dve.wait_ge(sem("lin_q0"), w + 1)
                split_queries(0, w)
                dve.wait_ge(sem("q_split"), w + 1)
            for w in range(WAVES):
                maxima(0, w)
            attention(0)
            dve.wait_ge(sem("loaded_rows"), 16)
            dve.wait_ge(sem("tanh_gates"), 1)
            for w in range(WAVES):
                key = ("mid0", w)
                statistics(key, lambda k: attn[:, w * WB + k, :])
                if w:
                    wait_full(dve, ("post0T", w - 1))
                link(normalise(key, lin2_tile, lambda k: attn[:, w * WB + k, :]))
                v = lin2[:, :].rearrange("t (b d) -> t b d", b=WB)
                lv = lin[:, :].rearrange("t (b d) -> t b d", b=WB)
                link(dve.tensor_tensor(v, v, gamma.unsqueeze(1).to_broadcast([128, WB, D]), ALU.mult))
                link(dve.tensor_tensor(v, v, beta.unsqueeze(1).to_broadcast([128, WB, D]), ALU.add))
                link(dve.tensor_tensor(lv, v, v, ALU.mult))
                i = norm_no[("rms0", w)]
                dve.tensor_reduce(sq[:, i, 0:WB], lv, AX.X, ALU.add).then_inc(sem("variance"), 1)
                dve.wait_ge(sem("variance"), i + 1)
                link(dve.tensor_reduce(amax[:, 0:WB], v, AX.X, ALU.max, apply_absolute_value=True))
                quant_scales(("rms0", w), 128, WB)
                quantise(lin_tile, lin2_tile, 128, WB).then_inc(sem("lin_post0"), 1)
                dve.wait_ge(sem("lin_post0"), w + 1)
                wait_full(dve, ("post0", w))
                xs = x[:, w * WB:(w + 1) * WB, :].rearrange("t b d -> t (b d)")
                dve.scalar_tensor_tensor(out=xs, in0=bank(("post0", w))[:, :], scalar=tg[:, 0:1], in1=xs,
                                         op0=ALU.mult, op1=ALU.add).then_inc(bank_free(("post0", w)), 1)
                wait_read(dve, ("post0", w))
            split_context(1)
            for w in range(WAVES):
                key = ("moe", w)
                statistics(key, x_tile(w))
                if w:
                    wait_full(dve, ("moeT", w - 1))
                normalise(key, lin_tile, x_tile(w)).then_inc(sem("lin_moe"), 1)
                dve.wait_ge(sem("lin_moe"), w + 1)
                rk = ("router", w)
                wait_full(dve, rk)
                dve.tensor_copy(logit[:, :, :], bank(rk)[:, 0:WB * E0].rearrange("t (b e) -> t b e", b=WB)).then_inc(
                    bank_free(rk), 1)
                wait_read(dve, rk)

                def wide_e(v):
                    return v.unsqueeze(2).to_broadcast([128, WB, E0])

                rank_b = rank.unsqueeze(1).to_broadcast([128, WB, E0])
                for pick, (lg, oh) in enumerate(((logit, oh1), (lg2, oh2))):
                    m, r = mm[:, 2 * pick, :], mm[:, 2 * pick + 1, :]
                    link(dve.tensor_reduce(m, lg[:, :, :], AX.X, ALU.max))
                    link(dve.tensor_tensor(code[:, :, :], lg[:, :, :], wide_e(m), ALU.is_equal))
                    link(dve.tensor_tensor(code[:, :, :], code[:, :, :], rank_b, ALU.mult))
                    link(dve.tensor_reduce(r, code[:, :, :], AX.X, ALU.max))
                    link(dve.tensor_tensor(oh[:, :, :], code[:, :, :], wide_e(r), ALU.is_equal))
                    if pick == 0:
                        link(dve.scalar_tensor_tensor(out=lg2[:, :, :], in0=oh1[:, :, :], scalar=-3.0e38,
                                                      in1=logit[:, :, :], op0=ALU.mult, op1=ALU.add))
                dve.tensor_tensor(gap[:, w, :], mm[:, 2, :], mm[:, 0, :], ALU.subtract).then_inc(sem("gap"), 1)
                dve.wait_ge(sem("ediff"), w + 1)
                link(dve.tensor_scalar(mm[:, 4, :], ediff[:, w, :], 1.0, None, ALU.add))
                link(dve.reciprocal(mm[:, 5, :], mm[:, 4, :]))
                link(dve.tensor_scalar(mm[:, 5, :], mm[:, 5, :], tg[:, 2:3], None, ALU.mult))
                link(dve.tensor_tensor(mm[:, 6, :], mm[:, 5, :], ediff[:, w, :], ALU.mult))
                link(dve.tensor_tensor(oh1[:, :, :], oh1[:, :, :], wide_e(mm[:, 5, :]), ALU.mult))
                link(dve.tensor_tensor(oh2[:, :, :], oh2[:, :, :], wide_e(mm[:, 6, :]), ALU.mult))
                link(dve.tensor_tensor(cw[:, w, :, :], oh1[:, :, :], oh2[:, :, :], ALU.add))
                for e in range(E0):
                    key = ("y", w, e)
                    wait_full(dve, key)
                    for k in range(WB):
                        xt = x[:, w * WB + k, :]
                        ins = dve.scalar_tensor_tensor(out=xt, in0=bank(key)[:, k * D:(k + 1) * D],
                                                       scalar=cw[:, w, k, e:e + 1], in1=xt, op0=ALU.mult, op1=ALU.add)
                    ins.then_inc(bank_free(key), 1)
                    wait_read(dve, key)
            tgbo = sb("tgbo", [128, D])
            link(dve.tensor_scalar(tgbo[:, :], bo, tg[:, 1:2], None, ALU.mult))
            for w in range(WAVES):
                key = ("q1", w)
                statistics(key, x_tile(w))
                if w:
                    wait_full(dve, ("q1T", w - 1))
                normalise(key, lin_tile, x_tile(w)).then_inc(sem("lin_q1"), 1)
                dve.wait_ge(sem("lin_q1"), w + 1)
                xw = x[:, w * WB:(w + 1) * WB, :]
                link(dve.tensor_tensor(xw, xw, tgbo[:, :].unsqueeze(1).to_broadcast([128, WB, D]), ALU.add))
                split_queries(1, w)
                dve.wait_ge(sem("q_split"), WAVES + w + 1)
            for w in range(WAVES):
                maxima(1, w)
            attention(1)
            for w in range(WAVES):
                pk = ("post1", w)
                wait_full(dve, pk)
                xs = x[:, w * WB:(w + 1) * WB, :].rearrange("t b d -> t (b d)")
                dve.scalar_tensor_tensor(out=xs, in0=bank(pk)[:, :], scalar=tg[:, 1:2], in1=xs,
                                         op0=ALU.mult, op1=ALU.add).then_inc(bank_free(pk), 1)
                wait_read(dve, pk)
                key = ("ffn1", w)
                statistics(key, x_tile(w))
                if w:
                    wait_full(dve, ("ffnT", w - 1))
                normalise(key, lin_tile, x_tile(w)).then_inc(sem("lin_ffn1"), 1)
                dve.wait_ge(sem("lin_ffn1"), w + 1)
            dve.wait_ge(sem("loaded_gatec"), 16)
            dve.wait_ge(sem("loaded_gaug_b"), 16)
            wait_full(dve, "gexp")
            dve.tensor_scalar(gexp[:, :], bank("gexp")[:, 0:B], 1.0 / TOK, gatec[:, 1:2], ALU.mult,
                              ALU.add).then_inc(bank_free("gexp"), 1)
            wait_read(dve, "gexp")
            wait_full(dve, "gaug")
            ins = dve.tensor_scalar(gaug[:, :], bank("gaug")[0:E1 + 1, 0:B], 1.0 / TOK, gaug_b[:, 0:1], ALU.mult, ALU.add)
            ins.then_inc(bank_free("gaug"), 1)
            dve.tensor_tensor(gmat[:, :, :], rowsel.unsqueeze(2).to_broadcast([128, R, B]),
                              gexp[:, :].unsqueeze(1).to_broadcast([128, R, B]), ALU.mult).then_inc(sem("gmat"), 1)
            wait_full(dve, "mb1")
            ins = dve.tensor_copy(mb1[:, :, :], bank("mb1")[:, 0:CK1 * B].rearrange("p (c b) -> p c b", c=CK1))
            ins.then_inc(bank_free("mb1"), 1)
            for c in range(2 * NJ):
                i, j = c // NJ, c % NJ
                dve.wait_ge(sem(f"loaded_base{i}"), 16)
                if c >= 4:
                    d = c - 4
                    dve.wait_ge(sem(f"regrouped{d % 4}_{d // NJ}"), 16 * ((d % NJ) // 4 + 1))
                wait_full(dve, ("mix", c))
                dve.tensor_tensor(mixed[:, c % 4, :], bank(("mix", c))[:, :], base[i][:, j, :], ALU.add).then_inc(
                    bank_free(("mix", c)), 1)
            for b in range(B):
                wait_full(dve, ("out", b))
                ins = dve.scalar_tensor_tensor(out=x[:, b, :], in0=bank(("out", b))[:, 0:D], scalar=tg[:, 3:4],
                                               in1=x[:, b, :], op0=ALU.mult, op1=ALU.add)
                ins.then_inc(bank_free(("out", b)), 1)


def kernel(**inputs):
    import numpy as _np
    import concourse.bacc as _bacc
    from concourse import mybir as _mybir
    from concourse.bass_utils import run_bass_kernel_spmd as _run

    v = {k: _np.asarray(a) for k, a in inputs.items()}
    cat, c = _np.concatenate, _np.ascontiguousarray

    def by_dim(w, rep=1):
        n = w.shape[0] // HD
        w = _np.repeat(w.reshape(n, HD, -1), rep, axis=0)
        return w.transpose(2, 1, 0).reshape(w.shape[2], -1)

    def bias_by_dim(b):
        return b.reshape(H, HD).T.reshape(-1)

    const = _np.zeros((128, 128 + R + 8), _np.float32)
    const[:, :128] = _np.eye(128)
    const[:, 128:128 + R] = _np.tile(_np.eye(R), (E1, 1))
    const[:, 128 + R:] = _np.arange(8, 0, -1)
    one = _np.ones((1, 1), _np.float32)
    tw0 = v["L1_ffn_TW1"].transpose(0, 2, 1).reshape(E1, NJ, R, F1).transpose(0, 2, 1, 3)
    base0 = _np.repeat(v["L1_ffn_W1"].T.reshape(NJ, R, F1).transpose(1, 0, 2), B, axis=0)
    tw1 = v["L1_ffn_TW2"].reshape(E1, D, CK1, NJ, R).transpose(0, 4, 3, 2, 1)
    base1 = _np.repeat(v["L1_ffn_W2"].reshape(D, CK1, NJ, R).transpose(3, 2, 1, 0), B, axis=0)
    g2 = v["L1_ffn_gate_w2"]
    arrays = {
        "x": v["x"], "ctx": v["ctx_1024"], "const": const,
        "rows": cat([v["L0_xattn_ln_gamma"], v["L0_xattn_ln_beta"], v["L1_xattn_bo"], v["g_xattn"], v["g_ffn"]]),
        "w0": cat([by_dim(v["L0_xattn_wq"]), by_dim(v["L0_xattn_wk"], H // KVH), v["L0_xattn_wo"].T,
                   v["L0_xattn_wv"].T], 1),
        "w1": cat([by_dim(v["L1_xattn_Wq"]), by_dim(v["L1_xattn_Wk"]), v["L1_xattn_Wv"].T, v["L1_xattn_Wo"].T], 1),
        "bias1": _np.stack([bias_by_dim(v["L1_xattn_bq"]), bias_by_dim(v["L1_xattn_bk"]), v["L1_xattn_bv"]], 1),
        "router": v["L0_ffn_router_w"],
        "moe1": v["L0_ffn_w1"].transpose(1, 0, 2),
        "moe2": v["L0_ffn_w2"].reshape(E0, CK0, 128, D).transpose(2, 0, 1, 3),
        "gate1": v["L1_ffn_gate_w1"].T,
        "gatec": _np.stack([v["L1_ffn_gate_b1"], _np.repeat(v["L1_ffn_gate_b2"], R)], 1),
        "gate2": cat([_np.repeat(g2.T, R, axis=1), g2.T, _np.zeros((D, 1), _np.float32)], 1),
        "gaug_b": cat([v["L1_ffn_gate_b2"][:, None], one], 0),
        "tb": cat([cat([v["L1_ffn_Tb1"], v["L1_ffn_Tb2"]], 1),
                   cat([v["L1_ffn_b1"], v["L1_ffn_b2"]])[None]], 0),
        "tw0": tw0.reshape(128, NJ, 512), "base0": base0.reshape(128, NJ, 512),
        "tw1": tw1.reshape(128, NJ, 512), "base1": base1.reshape(128, NJ, 512),
    }
    arrays = {k: c(a) for k, a in arrays.items()}
    nc = _bacc.Bacc("TRN2", target_bir_lowering=False, num_devices=1)
    io = {k: nc.dram_tensor("in_" + k, a.shape, _mybir.dt.from_np(a.dtype), kind="ExternalInput").ap()
          for k, a in arrays.items()}
    io["out"] = nc.dram_tensor("out", (B, TOK, D), F32, kind="ExternalOutput").ap()
    build(nc, io)
    r = _run(nc, [{"in_" + k: a for k, a in arrays.items()}], core_ids=[0])
    return r.results[0]["out"]
```

```python
from contextlib import ExitStack

import concourse.bass as bass
from concourse import mybir

F32 = mybir.dt.float32
BF16 = mybir.dt.bfloat16
FP16 = mybir.dt.float16
ACT = mybir.ActivationFunctionType
ALU = mybir.AluOpType
AX = mybir.AxisListType

B, TOK, D = 8, 128, 128
NK = 77
H, HD, KVH = 16, 8, 8
E0, F0 = 8, 256
E1, F1 = 8, 512
R = D // E1
NJ = D // R
CK0, CK1 = F0 // 128, F1 // 128
WAVES = 2
WB = B // WAVES
WT = WB * TOK
PARTS = 3
PAIRS = [(0, 0), (0, 1), (1, 0), (1, 1), (0, 2), (2, 0)]
QK_ROWS = len(PAIRS) * HD
ST_ROWS = QK_ROWS + PARTS
VW = HD + 1
PGROUP = 4
NG = H // PGROUP
STEPS = B * NG
PRING = 7
LAG = 4
MB = 2
EXPERTS = WAVES * E0
AHEAD = 2
CHUNKS0 = list(range(18))
TURNS0 = {6: 1, 12: 2, 18: 3}
CHUNKS_E = [11, 11, 12, 12, 13, 13, 14, 14, 15, 15, 16, 16]
CHUNKS1 = [10, 10, 11, 11, 12, 12, 14, 15, 16, 17, 18, 19]
TURNS1 = {13: 2, 20: 3}
CTX_STEP = 2
POST_STEP = WB * NG + LAG
MAGIC = 1.5 * 2.0 ** 23
ROWS = 3 * D + 4
A_SPLIT = [(0, 6), (6, 12), (12, 16)]

NORMS = ["ctx0", ("q0", 0), ("q0", 1), ("mid0", 0), ("rms0", 0), ("moe", 0), ("mid0", 1), ("rms0", 1), ("moe", 1),
         ("q1", 0), ("q1", 1), ("ffn1", 0), ("ffn1", 1)]
NORM_FORM = {"ctx0": (1.0 / D, 1e-6), "q0": (1.0 + 1e-6, 1e-11), "mid0": (1.0, 1e-5), "rms0": (1.0 / D, 1e-6),
             "moe": (1.0, 1e-5), "q1": (1.0, 1e-5), "ffn1": (1.0, 1e-5)}


def build(nc, io):
    ctx = ExitStack()
    with ctx:
        def sb(name, shape, dt=F32):
            return ctx.enter_context(nc.sbuf_tensor(name, shape, dt))

        sems = {}

        def sem(name):
            if name not in sems:
                sems[name] = ctx.enter_context(nc.semaphore(name))
            return sems[name]

        rings = {r: [ctx.enter_context(nc.psum_tensor(f"ps_{r}{i}", [128, 512], F32)) for i in range(2)]
                 for r in "taso"}
        place = {}
        taken = {r: 0 for r in rings}
        fulls = {(r, i): 0 for r in rings for i in range(2)}

        def open_bank(pe, key, ring, signalled=True):
            i = taken[ring] % 2
            place[key] = (ring, i, taken[ring] // 2, fulls[ring, i])
            taken[ring] += 1
            fulls[ring, i] += signalled
            if place[key][2]:
                pe.wait_ge(bank_free(key), place[key][2])
            return bank(key)

        def bank(key):
            r, i, _, _ = place[key]
            return rings[r][i]

        def bank_full(key):
            r, i, _, _ = place[key]
            return sem(f"full_{r}{i}")

        def bank_free(key):
            r, i, _, _ = place[key]
            return sem(f"free_{r}{i}")

        def wait_full(eng, key):
            eng.wait_ge(bank_full(key), place[key][3] + 1)

        def wait_read(eng, key):
            eng.wait_ge(bank_free(key), place[key][2] + 1)

        x = sb("x", [128, B, D])
        y = sb("y", [NK, B, D])
        attn = sb("attn", [128, B, D])
        yq = attn[0:NK, :, :]
        yT = sb("yT", [128, B * NK])
        const = sb("const", [128, 128 + R + 8])
        ident, rowsel, rank = const[:, 0:128], const[:, 128:128 + R], const[:, 128 + R:]
        identb = sb("identb", [128, 128], BF16)
        ones = sb("ones", [128, 128])
        onesb = sb("onesb", [PARTS, B * NK], BF16)
        neghalf = sb("neghalf", [128, 8])
        rows = sb("rows", [128, ROWS])
        gamma, beta, bo = (rows[:, i * D:(i + 1) * D] for i in range(3))
        tg = sb("tg", [128, 4])
        w0 = sb("w0", [128, 448])
        w0q = sb("w0q", [128, 448])
        w0part = [(0, 128), (128, 256), (256, 384), (384, 448)]
        wsum = sb("wsum", [128, 4])
        wsc = sb("wsc", [128, 4])
        winv = sb("winv", [128, 4])
        w1 = sb("w1", [128, 512])
        bias1 = sb("bias1", [128, 3])
        router = sb("router", [128, E0])
        moe = sb("moe", [128, 2, E0, F0])
        moe1 = moe[:, 0, :, :]
        moe2 = moe[:, 1, :, :].rearrange("p e (c d) -> p e c d", c=CK0)
        gate1 = sb("gate1", [128, D])
        gatec = sb("gatec", [128, 2])
        gate2 = sb("gate2", [128, 128 + E1 + 1])
        gaug_b = sb("gaug_b", [E1 + 1, 1])
        tb = sb("tb", [E1 + 1, F1 + D])
        tw = [sb(f"tw{i}", [128, NJ, 512]) for i in range(2)]
        keyroom = sb("keyroom", [128, H * B * NK // 2])
        kst = keyroom[0:64, :].bitcast(BF16).rearrange("p (h s) -> p h s", h=H)
        base = [moe[:, :, :, :].rearrange("p a e f -> p (a e f)").rearrange("p (j f) -> p j f", j=NJ),
                keyroom[:, 0:NJ * 512].rearrange("p (j f) -> p j f", j=NJ)]
        mw = sb("mw", [128, 2, B, 512])
        qst = mw[0:64, :, :, :].rearrange("p a b f -> p (a b f)").bitcast(BF16).rearrange("p (h t) -> p h t", h=H)
        vst = [sb(f"vst{i}", [NK, B, n, PARTS, VW], BF16)
               for i, n in enumerate((KVH, H))]
        lin = sb("lin", [128, WAVES, WB, D])
        mid = sb("mid", [128, WAVES, WB, D])
        linT = sb("linT", [128, B * TOK])
        kproj = sb("kproj", [128, 640])
        qproj = sb("qproj", [128, WAVES, WT])
        rest = sb("rest", [128, 640])
        krest = qproj[:, :, :].rearrange("p w t -> p (w t)")
        kparts = sb("kparts", [128, PARTS, B * NK], BF16)
        qparts = sb("qparts", [128, WAVES, PARTS, WT], BF16)
        nmax = sb("nmax", [128, B, H])
        mrest = sb("mrest", [128, MB, H])
        mparts = sb("mparts", [128, B, PARTS, H], BF16)
        maxT = sb("maxT", [PARTS * H, B, TOK], BF16)
        ph = sb("ph", [NK, PRING, 512], FP16)
        pl = sb("pl", [NK, PRING, 512], FP16)
        osum = sb("osum", [128, H, VW])
        rden = sb("rden", [128, H])
        st = sb("st", [128, len(NORMS), WB, 6])
        mv = sb("mv", [128, len(NORMS), WB, 2])
        sq = sb("sq", [128, len(NORMS), 8])
        nin = sb("nin", [128, len(NORMS), 8])
        rstd = sb("rstd", [128, len(NORMS), 8])
        amax = sb("amax", [128, len(NORMS), 8])
        am1 = sb("am1", [128, 8])
        am2 = sb("am2", [128, 8])
        comb = sb("comb", [128, len(NORMS), 8])
        inv = sb("inv", [128, len(NORMS), 8])
        magic = sb("magic", [128, 1])
        logit = sb("logit", [128, WB, E0])
        lg2 = sb("lg2", [128, WB, E0])
        oh1 = sb("oh1", [128, WB, E0])
        oh2 = sb("oh2", [128, WB, E0])
        code = sb("code", [128, WB, E0])
        cw = sb("cw", [128, WAVES, WB, E0])
        mm = sb("mm", [128, 8, WB])
        ediff = sb("ediff", [128, WAVES, WB])
        gap = sb("gap", [128, WAVES, WB])
        hT = sb("hT", [128, 4, WT])
        p32 = [hT[0:NK, i, :] for i in range(4)] + [sb(f"p32_{i}", [NK, 512])[:, :] for i in range(4, PRING)]
        ys = [kproj[:, 0:WT], yT[:, 0:WT]]
        mixed = hT
        hs = sb("hs", [128, B])
        relu_out = mid[:, 0, :, :].rearrange("t b d -> t (b d)")
        tgbo = sb("tgbo", [128, D])
        bias_q = sb("bias_q", [128, 1])
        gexp = sb("gexp", [128, B])
        gmat = sb("gmat", [128, R, B])
        gaug = sb("gaug", [E1 + 1, B])
        gtok = y[0:E1 + 1, :, :]
        mb1 = sb("mb1", [128, CK1, B])
        uT = qproj[:, :, :].rearrange("p w (c t) -> p w c t", c=CK1)

        norm_no = {k: i for i, k in enumerate(NORMS)}
        block = ctx.enter_context(nc.Block())

        def prob_group(n):
            return f"S{n // (B * NG)}", n // NG % B, n % NG

        def batches(w):
            return range(w * WB, (w + 1) * WB)

        def flat(v):
            return v.rearrange("t b d -> t (b d)")

        wide = WB * NK

        @block.tensor
        def _(pe):
            def turn(key, ring, tiles, dt=F32):
                p = open_bank(pe, key, ring)
                for dst, src, n in tiles(p):
                    ins = pe.transpose(dst, src, (identb if dt == BF16 else ident)[0:n, 0:n])
                ins.then_inc(bank_full(key), 1)

            def product(key, ring, terms):
                p = open_bank(pe, key, ring)
                for out, lhsT, rhs in terms(p):
                    ins = pe.matmul(out, lhsT, rhs, start=True, stop=True)
                ins.then_inc(bank_full(key), 1)

            def turn_context(layer):
                src = y if layer else yq
                for i in range(2):
                    turn((f"y{layer}T", i), "t",
                         lambda p: [(p[:, k * NK:(k + 1) * NK], src[:, i * WB + k, :], NK) for k in range(WB)])

            def keys(layer):
                weights = w1 if layer else w0q
                for i in range(2):
                    wait_read(pe, (f"y{layer}T", i))
                    product((f"k{layer}", i), "t",
                            lambda p: [(p[:, 0:wide], weights[:, 128:256], yT[:, i * wide:(i + 1) * wide])])

            def context_values(layer, i):
                wv = w1[:, 256:384] if layer else w0q[:, 384:448]
                n = wv.shape[1]
                tiles = 512 // n
                product((f"v{layer}", i), "t",
                        lambda p: [(p[0:NK, k * n:(k + 1) * n],
                                    yT[:, (i * tiles + k) * NK:(i * tiles + k + 1) * NK], wv)
                                   for k in range(tiles)])

            def turn_wave(key, src, ring="t"):
                turn(key, ring, lambda p: [(p[:, k * TOK:(k + 1) * TOK], src[:, k, :], 128) for k in range(WB)])

            def turn_queries(layer, w, ring="t"):
                pe.wait_ge(sem(f"lin_q{layer}"), w + 1)
                turn_wave((f"q{layer}T", w), lin[:, w, :, :], ring)

            def queries(layer, w, ring="t"):
                wait_read(pe, (f"q{layer}T", w))
                weights = w1 if layer else w0q
                product((f"q{layer}", w), ring,
                        lambda p: [(p[:, :], weights[:, 0:128], linT[:, w * WT:(w + 1) * WT])])

            def scores_for_max(layer, n, ring="a"):
                b, c = n // len(A_SPLIT), n % len(A_SPLIT)
                h0, h1 = A_SPLIT[c]
                pe.wait_ge(sem(f"q_stacked{b // WB}"), 16 * len(PAIRS) * (layer + 1))
                pe.wait_ge(sem("k_stacked"), 16 * len(PAIRS) * (layer + 1))
                product((f"A{layer}", b, c), ring,
                        lambda p: [(p[:, (h - h0) * NK:(h - h0 + 1) * NK],
                                    qst[0:QK_ROWS, h, b * TOK:(b + 1) * TOK],
                                    kst[0:QK_ROWS, h, b * NK:(b + 1) * NK]) for h in range(h0, h1)])

            def turn_maxima(layer, m, ring="t"):
                pe.wait_ge(sem("max_split"), layer * B // MB + m + 1)
                turn((f"max{layer}T", m), ring,
                     lambda p: [(p[0:PARTS * H, k * TOK // 2:(k + 1) * TOK // 2].bitcast(BF16),
                                 mparts[:, m * MB + k, :, :].rearrange("t p h -> t (p h)"), 128)
                                for k in range(MB)], BF16)

            def scores(layer, b, g):
                pe.wait_ge(sem(f"max_stacked{b // MB}"), 16 * (layer + 1))
                pe.wait_ge(sem("ones_stacked"), 16)
                product((f"S{layer}", b, g), "s",
                        lambda p: [(p[0:NK, k * TOK:(k + 1) * TOK],
                                    kst[0:ST_ROWS, g * PGROUP + k, b * NK:(b + 1) * NK],
                                    qst[0:ST_ROWS, g * PGROUP + k, b * TOK:(b + 1) * TOK]) for k in range(PGROUP)])

            def values(layer, b, g):
                n = (layer * B + b) * NG + g
                key = (f"O{layer}", b)
                if g == 0:
                    open_bank(pe, key, "o", signalled=False)
                pe.wait_ge(sem("prob_rest_pool" if n % 2 else "prob_rest"), n // 2 + 1)
                o, s = bank(key), n % PRING
                for k in range(PGROUP):
                    h = g * PGROUP + k
                    col = h * PARTS * VW
                    v = vst[layer][:, b, h if layer else h // 2, :, :].rearrange("s p d -> s (p d)")
                    pe.matmul(o[:, col:col + PARTS * VW], ph[:, s, k * TOK:(k + 1) * TOK], v, start=True, stop=False,
                              skip_group_check=True)
                    ins = pe.matmul(o[:, col:col + 2 * VW], pl[:, s, k * TOK:(k + 1) * TOK], v[:, 0:2 * VW],
                                    start=False, stop=True, skip_group_check=True)
                ins.then_inc(sem("pv_done"), 1)

            def attention(layer, beside):
                pe.wait_ge(sem("v_split" if layer == 0 else "v1_split"), layer + 1)
                for i in range(STEPS + LAG):
                    if i < STEPS:
                        scores(layer, i // NG, i % NG)
                    beside(i)
                    if i >= LAG:
                        values(layer, (i - LAG) // NG, (i - LAG) % NG)

            def turn_post(layer, w, src, ring="t"):
                if layer:
                    pe.wait_ge(sem("attn_done"), B + (w + 1) * WB)
                else:
                    pe.wait_ge(sem("lin_post0"), w + 1)
                turn_wave((f"post{layer}T", w), src, ring)

            def post(layer, w, weights, ring="t"):
                wait_read(pe, (f"post{layer}T", w))
                product((f"post{layer}", w), ring,
                        lambda p: [(p[:, k * TOK:(k + 1) * TOK],
                                    linT[:, (w * WB + k) * TOK:(w * WB + k + 1) * TOK], weights) for k in range(WB)])

            def turn_experts(w, ring="t"):
                pe.wait_ge(sem("lin_moe"), w + 1)
                turn_wave(("moeT", w), lin[:, w, :, :], ring)

            def route(w):
                wait_read(pe, ("moeT", w))
                product(("router", w), "a",
                        lambda p: [(p[:, k * E0:(k + 1) * E0],
                                    linT[:, (w * WB + k) * TOK:(w * WB + k + 1) * TOK], router[:, :])
                                   for k in range(WB)])

            def hidden(n):
                w, e = n // E0, n % E0
                for c in range(CK0):
                    product(("h", n, c), "ts"[n % 2],
                            lambda p: [(p[:, :], moe1[:, e, c * 128:(c + 1) * 128], linT[:, w * WT:(w + 1) * WT])])

            def expert_out(n):
                for c in range(CK0):
                    wait_read(pe, ("h", n, c))
                p = open_bank(pe, ("y", n), "a")
                for k in range(WB):
                    for c in range(CK0):
                        ins = pe.matmul(p[:, k * D:(k + 1) * D], hT[:, (CK0 * n + c) % 4, k * TOK:(k + 1) * TOK],
                                        moe2[:, n % E0, c, :], start=(c == 0), stop=(c == CK0 - 1))
                ins.then_inc(bank_full(("y", n)), 1)

            def ffn_start(w):
                pe.wait_ge(sem("lin_ffn1"), w + 1)
                turn_wave(("ffnT", w), lin[:, w, :, :])
                wait_read(pe, ("ffnT", w))
                product(("gate", w), "t", lambda p: [(p[:, :], gate1[:, :], linT[:, w * WT:(w + 1) * WT])])

            pe.wait_ge(sem("constants"), 1)
            pe.wait_ge(sem("wsum"), 1)
            product("wsum", "t", lambda p: [(p[:, 0:4], ones[:, :], wsum[:, :])])
            pe.wait_ge(sem("loaded_const"), 16)
            pe.wait_ge(sem("yq"), 1)
            turn_context(0)
            turn_queries(0, 0)
            pe.wait_ge(sem("w0q"), 1)
            keys(0)
            queries(0, 0)
            context_values(0, 0)
            turn_queries(0, 1)
            queries(0, 1)
            pe.wait_ge(sem("identb"), 1)
            for n in range(MB * len(A_SPLIT)):
                scores_for_max(0, n)
            turn_maxima(0, 0)
            def beside_layer0(i):
                for j, step in enumerate(CHUNKS0):
                    if i == step:
                        scores_for_max(0, MB * len(A_SPLIT) + j)
                if i in TURNS0:
                    turn_maxima(0, TURNS0[i])
                if i == CTX_STEP:
                    turn_context(1)
                if i == CTX_STEP + 1:
                    pe.wait_ge(sem("loaded_w1"), 16)
                    keys(1)
                if i == CTX_STEP + 4:
                    context_values(1, 0)
                if i == CTX_STEP + 10:
                    context_values(1, 1)
                if i == POST_STEP + 8:
                    turn_post(0, 0, lin[:, 0, :, :])
                if i == POST_STEP + 9:
                    post(0, 0, w0q[:, 256:384])
                if i == POST_STEP + 13:
                    turn_experts(0)

            attention(0, beside_layer0)
            for name in ("router", "moe1", "moe2"):
                pe.wait_ge(sem("loaded_" + name), 16)
            route(0)
            for n in range(AHEAD):
                hidden(n)
            for n in range(EXPERTS):
                if n in CHUNKS_E:
                    scores_for_max(1, CHUNKS_E.index(n), "o")
                expert_out(n)
                if n + AHEAD < EXPERTS:
                    hidden(n + AHEAD)
                if n == 2:
                    turn_post(0, 1, lin[:, 1, :, :], "o")
                if n == 3:
                    post(0, 1, w0q[:, 256:384], "o")
                if n == 4:
                    turn_experts(1, "o")
                if n == 5:
                    route(1)
                if n == E0:
                    turn_queries(1, 0, "o")
                if n == E0 + 1:
                    queries(1, 0, "o")
                if n == 14:
                    turn_maxima(1, 0, "o")
                if n in CHUNKS_E:
                    scores_for_max(1, CHUNKS_E.index(n) + 1, "o")
            for j in range(CHUNKS_E.index(EXPERTS), len(CHUNKS_E)):
                scores_for_max(1, j, "o")
            turn_maxima(1, 1)
            for name in ("gate1", "gate2", "tb"):
                pe.wait_ge(sem("loaded_" + name), 16)

            def beside_layer1(i):
                if i == 3:
                    turn_queries(1, 1)
                if i == 5:
                    queries(1, 1)
                for j, step in enumerate(CHUNKS1):
                    if i == step:
                        scores_for_max(1, WB * len(A_SPLIT) + j)
                if i in TURNS1:
                    turn_maxima(1, TURNS1[i])
                if i == POST_STEP:
                    turn_post(1, 0, attn[:, 0:WB, :])
                if i == POST_STEP + 2:
                    post(1, 0, w1[:, 384:512])
                if i == POST_STEP + 7:
                    ffn_start(0)

            attention(1, beside_layer1)
            turn_post(1, 1, attn[:, WB:B, :])
            post(1, 1, w1[:, 384:512])
            ffn_start(1)
            for w in range(WAVES):
                wait_read(pe, ("gate", w))
            product("gexp", "t", lambda p: [(p[:, 0:B], gate2[:, 0:128], hs[:, :])])
            product("gaug", "t", lambda p: [(p[0:E1 + 1, 0:B], gate2[:, 128:], hs[:, :])])
            wait_read(pe, "gaug")
            product("mb1", "t", lambda p: [(p[:, c * B:(c + 1) * B], tb[:, c * 128:(c + 1) * 128], gaug[:, :])
                                           for c in range(CK1)])
            pe.wait_ge(sem("gmat"), 1)
            for c in range(2 * NJ):
                i, j = c // NJ, c % NJ
                pe.wait_ge(sem(f"loaded_tw{i}"), 16)
                product(("mix", c), "a", lambda p: [(p[:, :], gmat[:, :, :].rearrange("p r b -> p (r b)"),
                                                     tw[i][:, j, :])])

            def ffn_up(b):
                product(("u", b), "s", lambda p: [(p[:, c * TOK:(c + 1) * TOK], mw[:, 0, b, c * 128:(c + 1) * 128],
                                                   linT[:, b * TOK:(b + 1) * TOK]) for c in range(CK1)])

            def regrouped(i):
                for q in range(4):
                    pe.wait_ge(sem(f"regrouped{q}_{i}"), 16 * NJ // 4)

            regrouped(0)
            ffn_up(0)
            pe.wait_ge(sem("gtok"), 1)
            for b in range(B):
                if b + 1 < B:
                    ffn_up(b + 1)
                wait_read(pe, ("u", b))
                if b == 0:
                    regrouped(1)
                p = open_bank(pe, ("out", b), "t")
                for c in range(CK1):
                    pe.matmul(p[:, 0:D], uT[:, b % 2, c, :], mw[:, 1, b, c * D:(c + 1) * D], start=(c == 0), stop=False)
                pe.matmul(p[:, 0:D], gtok[:, b, :], tb[:, F1:F1 + D], start=False, stop=True).then_inc(
                    bank_full(("out", b)), 1)

        @block.sync
        def _(sp):
            def load(name, dst, src):
                sp.dma_start(dst, src).then_inc(sem("loaded_" + name), 16)

            load("y", y[:, :, :], io["ctx"].rearrange("b s d -> s b d"))
            load("w0", w0[:, :], io["w0"])
            load("x", x[:, :, :], io["x"].rearrange("b t d -> t b d"))
            load("const", const[:, :], io["const"])
            load("rows", rows[:, :], io["rows"].partition_broadcast(128))
            load("w1", w1[:, :], io["w1"])
            load("bias1", bias1[:, :], io["bias1"])
            sp.wait_ge(sem("constants"), 1)
            sp.dma_start(kst[QK_ROWS:ST_ROWS, :, :], onesb[:, :].unsqueeze(1).to_broadcast([PARTS, H, B * NK])).then_inc(
                sem("ones_stacked"), 16)

            def stack_keys(layer, first):
                if first:
                    for i in range(2):
                        wait_read(sp, (f"k{layer}", i))
                else:
                    sp.wait_ge(sem("k1_split" if layer else "k_split"), 1)
                if layer:
                    sp.wait_ge(sem("attn_done"), B)
                for r, (_, kp) in enumerate(PAIRS):
                    if (kp == 0) == first:
                        sp.dma_start(kst[HD * r:HD * (r + 1), :, :], kparts[:, kp, :]).then_inc(sem("k_stacked"), 16)

            def stack_queries(layer, w, first):
                if first:
                    wait_read(sp, (f"q{layer}", w))
                else:
                    sp.wait_ge(sem("q_split"), layer * WAVES + w + 1)
                for r, (qp, _) in enumerate(PAIRS):
                    if (qp == 0) == first:
                        sp.dma_start(qst[HD * r:HD * (r + 1), :, w * WT:(w + 1) * WT],
                                     qparts[:, w, qp, :]).then_inc(sem(f"q_stacked{w}"), 16)

            def stack_maxima(layer, m):
                wait_read(sp, (f"max{layer}T", m))
                sp.dma_start(qst[QK_ROWS:ST_ROWS, :, m * MB * TOK:(m + 1) * MB * TOK],
                             maxT[:, m * MB:(m + 1) * MB, :]).then_inc(sem(f"max_stacked{m}"), 16)

            stack_keys(0, True)
            stack_queries(0, 0, True)
            stack_keys(0, False)
            stack_queries(0, 0, False)
            stack_queries(0, 1, True)
            stack_queries(0, 1, False)
            stack_maxima(0, 0)
            load("router", router[:, :], io["router"])
            load("moe1", moe1[:, :, :], io["moe1"])
            load("moe2", moe2[:, :, :, :], io["moe2"])
            for m in range(1, B // MB):
                stack_maxima(0, m)
            load("gate1", gate1[:, :], io["gate1"])
            load("gatec", gatec[:, :], io["gatec"])
            load("gate2", gate2[:, :], io["gate2"])
            load("gaug_b", gaug_b[:, :], io["gaug_b"])
            load("tb", tb[:, :], io["tb"])
            load("tw0", tw[0][:, :, :], io["tw0"])
            load("tw1", tw[1][:, :, :], io["tw1"])
            stack_keys(1, True)
            stack_keys(1, False)
            stack_queries(1, 0, True)
            stack_queries(1, 0, False)
            stack_maxima(1, 0)
            stack_maxima(1, 1)
            stack_queries(1, 1, True)
            stack_queries(1, 1, False)
            wait_full(sp, ("y", EXPERTS - 2))
            wait_full(sp, ("y", EXPERTS - 1))
            load("base0", base[0][:, :, :], io["base0"])
            for m in range(WB // MB, B // MB):
                stack_maxima(1, m)
            sp.wait_ge(sem("attn_done"), 2 * B)
            load("base1", base[1][:, :, :], io["base1"])
            for c in range(2 * NJ):
                i, j = c // NJ, c % NJ
                wait_read(sp, ("mix", c))
                sp.dma_start(mw[R * j:R * (j + 1), i, :, :], mixed[:, c % 4, :]).then_inc(
                    sem(f"regrouped{c % 4}_{i}"), 16)
            for b in range(B):
                wait_read(sp, ("out", b))
                sp.dma_start(io["out"][b], x[:, b, :]).then_inc(sem("stored"), 16)
            sp.wait_ge(sem("stored"), 16 * B)

        @block.gpsimd
        def _(pool):
            count = [0]

            def link(ins):
                count[0] += 1
                ins.then_inc(sem("pool_chain"), 1)
                pool.wait_ge(sem("pool_chain"), count[0])

            given = {k: n + 1 for n, k in enumerate(k for k in NORMS if k[0] not in ("c", "rms0"))}

            def inverse_root(key):
                i = norm_no[key]
                kind = key if isinstance(key, str) else key[0]
                scale, eps = NORM_FORM[kind]
                n, p = (8, NK) if kind == "ctx0" else (WB, 128)
                if kind in ("ctx0", "rms0"):
                    pool.wait_ge(sem("squares"), 1 if kind == "ctx0" else 2 + key[1])
                    src = sq[0:p, i, 0:n]
                else:
                    pool.wait_ge(sem("variance"), given[key])
                    src = mv[0:p, i, 0:n, 1]
                link(pool.tensor_scalar(nin[0:p, i, 0:n], src, scale, eps, ALU.mult, ALU.add))
                pool.tensor_tensor(rstd[0:p, i, 0:n], nin[0:p, i, 0:n], neghalf[0:p, 0:n],
                                   ALU.pow).then_inc(sem("rstd"), 1)

            def prob_rests(layer, beside):
                for i in range(STEPS + LAG):
                    n = layer * STEPS + i
                    if i < STEPS and n % 2:
                        pool.wait_ge(sem("prob_first"), n + 1)
                        s = n % PRING
                        pool.tensor_tensor(pl[:, s, :], p32[s], ph[:, s, :], ALU.subtract).then_inc(
                            sem("prob_rest_pool"), 1)
                    beside(i)

            def split_rest(step, src, d0, d1, d2, r, done):
                if step == 0:
                    link(pool.tensor_tensor(r, src, d0, ALU.subtract))
                if step == 1:
                    link(pool.tensor_copy(d1, r))
                if step == 2:
                    pool.tensor_tensor(d2, r, d1, ALU.subtract).then_inc(sem(done), 1)
                    pool.wait_ge(sem(done), sum(splits.setdefault(done, [])) + 1)
                    splits[done].append(1)

            splits = {}

            def split_keys1(step):
                if step == 0:
                    pool.wait_ge(sem("q_split"), WAVES)
                    for i in range(2):
                        wait_read(pool, ("k1", i))
                n = B * NK
                split_rest(step, kproj[:, 0:n], *(kparts[:, i, :] for i in range(PARTS)), krest[:, 0:n], "k1_split")

            def split_values1(step, i):
                if step == 0:
                    wait_read(pool, ("v1", i))

                def view(t):
                    return t[0:NK, 0:512].rearrange("s (b h d) -> s b h d", b=WB, h=H)

                split_rest(step, view(kproj), *(vst[1][:, i * WB:(i + 1) * WB, :, p, 0:HD] for p in range(PARTS)),
                           view(krest), "v1_split")

            def add_expert(n):
                w = n // E0
                if n % E0 == 0:
                    pool.wait_ge(sem("lin_moe"), w + 1)
                wait_read(pool, ("y", n))
                xw = x[:, w * WB:(w + 1) * WB, :]
                pool.tensor_tensor(xw, xw, ys[n % 2].rearrange("t (b d) -> t b d", b=WB), ALU.add).then_inc(
                    sem("added"), 1)
                pool.wait_ge(sem("added"), n + 1)

            def add_bias(w):
                pool.wait_ge(sem("lin_q1"), w + 1)
                pool.wait_ge(sem("tgbo"), 1)
                xw = x[:, w * WB:(w + 1) * WB, :]
                pool.tensor_tensor(xw, xw, tgbo[:, :].unsqueeze(1).to_broadcast([128, WB, D]), ALU.add).then_inc(
                    sem("bias_added"), 1)

            pool.memset(magic[:, :], MAGIC)
            pool.memset(neghalf[:, :], -0.5)
            pool.memset(onesb[:, :], 1.0)
            pool.memset(ones[:, :], 1.0).then_inc(sem("constants"), 1)
            pool.wait_ge(sem("constants"), 1)
            inverse_root("ctx0")
            inverse_root(("q0", 0))
            inverse_root(("q0", 1))
            for v in vst:
                link(pool.memset(v[:, :, :, 0, HD:VW], 1.0))
                pool.memset(v[:, :, :, 1:PARTS, HD:VW], 0.0).then_inc(sem("ones_column"), 1)

            def beside_layer0(i):
                c = i - CTX_STEP - 2
                if c >= 0 and c % 2 == 0:
                    if c // 2 < 3:
                        split_keys1(c // 2)
                    elif c // 2 < 9:
                        split_values1(c // 2 % 3, c // 2 // 3 - 1)
                if i == POST_STEP + 1:
                    inverse_root(("mid0", 0))
                if i == POST_STEP + 4:
                    inverse_root(("rms0", 0))
                if i == POST_STEP + 12:
                    inverse_root(("moe", 0))

            prob_rests(0, beside_layer0)
            for n in range(-1, EXPERTS):
                if n >= 0:
                    add_expert(n)
                if n == -1:
                    inverse_root(("mid0", 1))
                if n == 0:
                    inverse_root(("rms0", 1))
                if n == 3:
                    inverse_root(("moe", 1))
                if n == E0 - 1:
                    inverse_root(("q1", 0))
                if n == E0:
                    add_bias(0)
            inverse_root(("q1", 1))

            def beside_layer1(i):
                if i == 4:
                    add_bias(1)
                if i == POST_STEP + 4:
                    inverse_root(("ffn1", 0))

            prob_rests(1, beside_layer1)
            inverse_root(("ffn1", 1))
            wait_read(pool, "gaug")
            pool.tensor_copy(gtok[:, :, :], gaug[:, :].unsqueeze(2).to_broadcast([E1 + 1, B, TOK])).then_inc(
                sem("gtok"), 1)

        @block.scalar
        def _(act):
            def move(key, dst, src, scale=1.0, bias=0.0, part=None):
                wait_full(act, key)
                ins = act.activation(dst, src, ACT.Identity, bias=bias, scale=scale)
                if part is not None:
                    ins = act.activation(part, src, ACT.Identity, bias=bias, scale=scale)
                ins.then_inc(bank_free(key), 1)

            def turned_context(layer):
                for i in range(2):
                    move((f"y{layer}T", i), yT[:, i * wide:(i + 1) * wide], bank((f"y{layer}T", i))[:, 0:wide])

            def keys(layer):
                if layer:
                    act.wait_ge(sem("v_split"), 1)
                    act.wait_ge(sem("k_stacked"), 16 * len(PAIRS))
                for i in range(2):
                    cols = slice(i * wide, (i + 1) * wide)
                    move((f"k{layer}", i), kproj[:, cols], bank((f"k{layer}", i))[:, 0:wide],
                         bias=bias1[:, 1:2] if layer else 0.0, part=kparts[:, 0, cols])

            def value_view(layer, i, t):
                shape = dict(b=WB, h=H) if layer else dict(b=B, h=KVH)
                return t[0:NK, 0:512].rearrange("s (b h d) -> s b h d", **shape)

            def context_values(layer, i):
                key = (f"v{layer}", i)
                if layer:
                    act.wait_ge(sem("v1_split" if i else "k1_split"), 1)
                    dst = vst[1][:, i * WB:(i + 1) * WB, :, 0, 0:HD]
                else:
                    act.wait_ge(sem("k_split"), 1)
                    dst = vst[0][:, :, :, 0, 0:HD]
                wait_full(act, key)
                act.activation(kproj[0:NK, 0:512], bank(key)[0:NK, :], ACT.Identity)
                act.activation(dst, value_view(layer, i, bank(key)), ACT.Identity).then_inc(bank_free(key), 1)

            def turned(key, w, bias=0.0):
                move((key, w), linT[:, w * WT:(w + 1) * WT], bank((key, w))[:, :], bias=bias)

            def queries(layer, w):
                if layer:
                    act.wait_ge(sem("scaled_bq"), 1)
                    act.wait_ge(sem("v1_split"), 2)
                move((f"q{layer}", w), qproj[:, w, :], bank((f"q{layer}", w))[:, :],
                     scale=HD ** -0.5 if layer else 1.0, bias=bias_q[:, 0:1] if layer else 0.0,
                     part=qparts[:, w, 0, :])

            def maxima(layer, m):
                key = (f"max{layer}T", m)
                move(key, maxT[:, m * MB:(m + 1) * MB, :].rearrange("p b t -> p (b t)"),
                     bank(key)[0:PARTS * H, 0:MB * TOK // 2].bitcast(BF16))

            def squares(src, dst, key, n, p):
                i = norm_no[key]
                for k in range(n):
                    ins = act.activation(dst(k), src(k), ACT.Square, accum_out=sq[0:p, i, k:k + 1])
                ins.then_inc(sem("squares"), 1)

            rounds = [0]

            def round_tiles(dst, src, key, n, p):
                i = norm_no[key]
                rounds[0] += 1
                act.wait_ge(sem("quant_scales"), rounds[0])
                for k in range(n):
                    ins = act.activation(dst(k), src(k), ACT.Identity, scale=comb[0:p, i, k:k + 1],
                                         bias=magic[0:p, 0:1])
                ins.then_inc(sem("rounded"), 1)

            def probs(layer, i):
                n = layer * STEPS + i
                if i < STEPS:
                    key = prob_group(n)
                    if n >= PRING:
                        act.wait_ge(sem("pv_done"), n - PRING + 1)
                    wait_full(act, key)
                    act.activation(p32[n % PRING], bank(key)[0:NK, :], ACT.Exp).then_inc(bank_free(key), 1)
                if 0 < i <= STEPS:
                    wait_read(act, prob_group(n - 1))
                    s = (n - 1) % PRING
                    act.activation(ph[:, s, :], p32[s], ACT.Copy).then_inc(sem("prob_first"), 1)

            def hidden(n):
                if n >= EXPERTS:
                    return
                if n >= AHEAD:
                    wait_full(act, ("y", n - AHEAD))
                for c in range(CK0):
                    wait_full(act, ("h", n, c))
                    act.activation(hT[:, (CK0 * n + c) % 4, :], bank(("h", n, c))[:, :], ACT.Tanh,
                                   scale=0.5).then_inc(sem("tanh_h"), 1)

            def routed(w):
                act.wait_ge(sem("gap"), w + 1)
                act.activation(ediff[:, w, :], gap[:, w, :], ACT.Exp).then_inc(sem("ediff"), 1)

            def weighted(n):
                w, e = n // E0, n % E0
                if e == 0:
                    act.wait_ge(sem("expert_weights"), w + 1)
                    act.wait_ge(sem("v1_split"), 2)
                if n >= 2:
                    act.wait_ge(sem("added"), n - 1)
                wait_full(act, ("y", n))
                for k in range(WB):
                    ins = act.activation(ys[n % 2][:, k * D:(k + 1) * D], bank(("y", n))[:, k * D:(k + 1) * D],
                                         ACT.Copy, scale=cw[:, w, k, e:e + 1])
                ins.then_inc(bank_free(("y", n)), 1)

            def squares_post(w):
                act.wait_ge(sem("centred"), w + 1)
                squares(lambda k: mid[:, w, k, :], lambda k: lin[:, w, k, :], ("rms0", w), WB, 128)

            def round_post(w):
                round_tiles(lambda k: lin[:, w, k, :], lambda k: mid[:, w, k, :], ("rms0", w), WB, 128)

            def ffn_start(w):
                turned("ffnT", w)
                wait_full(act, ("gate", w))
                for k, b in enumerate(batches(w)):
                    ins = act.activation(relu_out[:, k * TOK:(k + 1) * TOK],
                                         bank(("gate", w))[:, k * TOK:(k + 1) * TOK], ACT.Relu,
                                         bias=gatec[:, 0:1], accum_out=hs[:, b:b + 1])
                ins.then_inc(bank_free(("gate", w)), 1)
                wait_read(act, ("gate", w))

            act.wait_ge(sem("loaded_y"), 16)
            squares(lambda k: y[:, k, :], lambda k: yq[:, k, :], "ctx0", B, NK)
            act.wait_ge(sem("loaded_rows"), 16)
            act.activation(tg[:, :], rows[:, 3 * D:3 * D + 4], ACT.Tanh).then_inc(sem("tanh_gates"), 1)
            act.wait_ge(sem("squares"), 1)
            act.wait_ge(sem("constants"), 1)
            round_tiles(lambda k: yq[:, k, :], lambda k: y[:, k, :], "ctx0", B, NK)
            round_tiles(lambda k: lin[:, 0, k, :], lambda k: mid[:, 0, k, :], ("q0", 0), WB, 128)
            turned_context(0)
            turned("q0T", 0)
            keys(0)
            queries(0, 0)
            round_tiles(lambda k: lin[:, 1, k, :], lambda k: mid[:, 1, k, :], ("q0", 1), WB, 128)
            context_values(0, 0)
            turned("q0T", 1)
            queries(0, 1)
            maxima(0, 0)

            def beside_layer0(i):
                if i in TURNS0:
                    maxima(0, TURNS0[i])
                if i == CTX_STEP:
                    turned_context(1)
                if i == CTX_STEP + 1:
                    act.wait_ge(sem("loaded_bias1"), 16)
                    act.activation(bias_q[:, :], bias1[:, 0:1], ACT.Copy, scale=HD ** -0.5).then_inc(
                        sem("scaled_bq"), 1)
                    keys(1)
                if i == CTX_STEP + 7:
                    context_values(1, 0)
                if i == CTX_STEP + 13:
                    context_values(1, 1)
                if i == POST_STEP + 3:
                    squares_post(0)
                if i == POST_STEP + 6:
                    round_post(0)
                if i == POST_STEP + 8:
                    turned("post0T", 0)
                if i == POST_STEP + 13:
                    turned("moeT", 0)

            for i in range(STEPS + LAG):
                probs(0, i)
                beside_layer0(i)
            for n in range(AHEAD):
                hidden(n)
            routed(0)
            for n in range(EXPERTS):
                weighted(n)
                hidden(n + AHEAD)
                if n == 0:
                    squares_post(1)
                if n == 1:
                    round_post(1)
                if n == 2:
                    turned("post0T", 1)
                if n == 4:
                    turned("moeT", 1)
                if n == 6:
                    routed(1)
                if n == E0:
                    turned("q1T", 0)
                if n == E0 + 1:
                    queries(1, 0)
                if n == 14:
                    maxima(1, 0)
            maxima(1, 1)
            act.wait_ge(sem("loaded_gatec"), 16)

            def beside_layer1(i):
                if i == 3:
                    turned("q1T", 1)
                if i == 5:
                    queries(1, 1)
                if i in TURNS1:
                    maxima(1, TURNS1[i])
                if i == POST_STEP:
                    turned("post1T", 0, bias=bias1[:, 2:3])
                if i == POST_STEP + 7:
                    ffn_start(0)

            for i in range(STEPS + LAG):
                probs(1, i)
                beside_layer1(i)
            turned("post1T", 1, bias=bias1[:, 2:3])
            ffn_start(1)
            wait_read(act, "mb1")
            for b in range(B):
                if b >= 2:
                    wait_full(act, ("out", b - 2))
                wait_full(act, ("u", b))
                for c in range(CK1):
                    ins = act.activation(uT[:, b % 2, c, :], bank(("u", b))[:, c * TOK:(c + 1) * TOK],
                                         ACT.Gelu_apprx_tanh, bias=mb1[:, c, b:b + 1])
                ins.then_inc(bank_free(("u", b)), 1)

        @block.vector
        def _(dve):
            count = [0]

            def link(ins):
                count[0] += 1
                ins.then_inc(sem("dve_chain"), 1)
                dve.wait_ge(sem("dve_chain"), count[0])

            def split_rest(src, d0, d1, d2, r, done):
                link(dve.tensor_tensor(r, src, d0, ALU.subtract))
                link(dve.tensor_copy(d1, r))
                dve.tensor_tensor(d2, r, d1, ALU.subtract).then_inc(sem(done), 1)

            given = [0]

            def statistics(key, src):
                i = norm_no[key]
                for k in range(WB):
                    ins = dve.bn_stats(st[:, i, k, :], src(k))
                link(ins)
                for k in range(WB):
                    ins = dve.bn_aggr(mv[:, i, k, :], st[:, i, k, :])
                ins.then_inc(sem("variance"), 1)
                given[0] += 1
                dve.wait_ge(sem("variance"), given[0])

            def quant_scales(key, p, n):
                i = norm_no[key]
                dve.wait_ge(sem("rstd"), i + 1)
                link(dve.tensor_tensor(am1[0:p, 0:n], amax[0:p, i, 0:n], rstd[0:p, i, 0:n], ALU.mult))
                link(dve.tensor_scalar(am1[0:p, 0:n], am1[0:p, 0:n], 1e-5, None, ALU.max))
                link(dve.reciprocal(am2[0:p, 0:n], am1[0:p, 0:n]))
                link(dve.tensor_scalar(inv[0:p, i, 0:n], am1[0:p, 0:n], 1.0 / 127.0, None, ALU.mult))
                dve.scalar_tensor_tensor(out=comb[0:p, i, 0:n], in0=am2[0:p, 0:n], scalar=127.0,
                                         in1=rstd[0:p, i, 0:n], op0=ALU.mult, op1=ALU.mult).then_inc(
                                             sem("quant_scales"), 1)

            rounds = [0]

            def dequantise(tile, key, n, p, done):
                i = norm_no[key]
                rounds[0] += 1
                dve.wait_ge(sem("rounded"), rounds[0])
                for k in range(n):
                    ins = dve.tensor_scalar(tile(k), tile(k), -MAGIC, inv[0:p, i, k:k + 1], ALU.add, ALU.mult)
                ins.then_inc(sem(done), 1)

            def split_keys0():
                for i in range(2):
                    wait_read(dve, ("k0", i))
                n = B * NK
                split_rest(kproj[:, 0:n], *(kparts[:, i, :] for i in range(PARTS)), rest[:, 0:n], "k_split")
                dve.wait_ge(sem("k_split"), 1)

            def split_values0():
                wait_read(dve, ("v0", 0))

                def view(t):
                    return t[0:NK, 0:512].rearrange("s (b h d) -> s b h d", b=B, h=KVH)

                split_rest(view(kproj), *(vst[0][:, :, :, p, 0:HD] for p in range(PARTS)), view(rest), "v_split")
                dve.wait_ge(sem("v_split"), 1)

            def normalise(key, dst, src):
                i = norm_no[key]
                dve.wait_ge(sem("rstd"), i + 1)
                for k in range(WB):
                    ins = dve.tensor_scalar(dst(k), src(k), mv[:, i, k, 0:1], rstd[:, i, k:k + 1],
                                            ALU.subtract, ALU.mult)
                return ins

            def x_tile(w):
                return lambda k: x[:, w * WB + k, :]

            def lin_tile(w):
                return lambda k: lin[:, w, k, :]

            def split_queries(layer, w):
                wait_read(dve, (f"q{layer}", w))
                split_rest(qproj[:, w, :], *(qparts[:, w, i, :] for i in range(PARTS)), rest[:, 0:WT], "q_split")
                dve.wait_ge(sem("q_split"), layer * WAVES + w + 1)

            def maxima(layer, n):
                b, c = n // len(A_SPLIT), n % len(A_SPLIT)
                h0, h1 = A_SPLIT[c]
                key = (f"A{layer}", b, c)
                wait_full(dve, key)
                v = bank(key)[:, 0:(h1 - h0) * NK].rearrange("t (h s) -> t h s", s=NK)
                dve.tensor_reduce(nmax[:, b, h0:h1], v, AX.X, ALU.max, negate=True).then_inc(bank_free(key), 1)

            def split_maxima(layer, m):
                for b in range(m * MB, (m + 1) * MB):
                    for c in range(len(A_SPLIT)):
                        wait_read(dve, (f"A{layer}", b, c))
                v, d = nmax[:, m * MB:(m + 1) * MB, :], mparts[:, m * MB:(m + 1) * MB, :, :]
                link(dve.tensor_copy(d[:, :, 0, :], v))
                split_rest(v, d[:, :, 0, :], d[:, :, 1, :], d[:, :, 2, :], mrest[:, :, :], "max_split")
                dve.wait_ge(sem("max_split"), layer * B // MB + m + 1)

            def outputs(layer, b):
                key = (f"O{layer}", b)
                dve.wait_ge(sem("pv_done"), NG * (layer * B + b + 1))
                v = bank(key)[:, 0:H * PARTS * VW].rearrange("t (h p d) -> t h d p", h=H, p=PARTS)
                dve.tensor_reduce(osum[:, :, :], v, AX.X, ALU.add).then_inc(bank_free(key), 1)
                wait_read(dve, key)
                link(dve.reciprocal(rden[:, :], osum[:, :, HD]))
                dve.tensor_tensor(attn[:, b, :].rearrange("t (h d) -> t h d", h=H), osum[:, :, 0:HD],
                                  rden[:, :].unsqueeze(2).to_broadcast([128, H, HD]), ALU.mult).then_inc(
                                      sem("attn_done"), 1)
                dve.wait_ge(sem("attn_done"), layer * B + b + 1)

            def prob_rest(layer, i):
                n = layer * STEPS + i
                if 0 < i < STEPS and n % 2:
                    n -= 1
                    dve.wait_ge(sem("prob_first"), n + 1)
                    s = n % PRING
                    dve.tensor_tensor(pl[:, s, :], p32[s], ph[:, s, :], ALU.subtract).then_inc(
                        sem("prob_rest"), 1)
                if i >= NG + LAG and (i - LAG) % NG == 0:
                    outputs(layer, (i - LAG) // NG - 1)

            def residual(key, w, gate):
                wait_full(dve, key)
                xs = flat(x[:, w * WB:(w + 1) * WB, :])
                dve.scalar_tensor_tensor(out=xs, in0=bank(key)[:, :], scalar=tg[:, gate:gate + 1], in1=xs,
                                         op0=ALU.mult, op1=ALU.add).then_inc(bank_free(key), 1)
                wait_read(dve, key)

            def post_start(w):
                statistics(("mid0", w), lambda k: attn[:, w * WB + k, :])

            def post_centre(w):
                v = mid[:, w, :, :]
                link(normalise(("mid0", w), lambda k: mid[:, w, k, :], lambda k: attn[:, w * WB + k, :]))
                link(dve.tensor_tensor(v, v, gamma.unsqueeze(1).to_broadcast([128, WB, D]), ALU.mult))
                dve.tensor_tensor(v, v, beta.unsqueeze(1).to_broadcast([128, WB, D]), ALU.add).then_inc(
                    sem("centred"), 1)
                dve.wait_ge(sem("centred"), w + 1)

            def post_maximum(w):
                v = mid[:, w, :, :]
                i = norm_no[("rms0", w)]
                link(dve.tensor_reduce(amax[:, i, 0:WB], v, AX.X, ALU.max, apply_absolute_value=True))

            def post_scales(w):
                quant_scales(("rms0", w), 128, WB)

            def post_quantised(w):
                dequantise(lin_tile(w), ("rms0", w), WB, 128, "lin_post0")

            def wide_e(v):
                return v.unsqueeze(2).to_broadcast([128, WB, E0])

            def experts_statistics(w):
                residual(("post0", w), w, 0)
                statistics(("moe", w), x_tile(w))

            def experts_norm(w):
                normalise(("moe", w), lin_tile(w), x_tile(w)).then_inc(sem("lin_moe"), 1)

            def route(w):
                rk = ("router", w)
                wait_full(dve, rk)
                dve.tensor_copy(logit[:, :, :], bank(rk)[:, 0:WB * E0].rearrange("t (b e) -> t b e", b=WB)).then_inc(
                    bank_free(rk), 1)
                wait_read(dve, rk)
                rank_b = rank.unsqueeze(1).to_broadcast([128, WB, E0])
                for pick, (lg, oh) in enumerate(((logit, oh1), (lg2, oh2))):
                    m, r = mm[:, 2 * pick, :], mm[:, 2 * pick + 1, :]
                    link(dve.tensor_reduce(m, lg[:, :, :], AX.X, ALU.max))
                    link(dve.tensor_tensor(code[:, :, :], lg[:, :, :], wide_e(m), ALU.is_equal))
                    link(dve.tensor_tensor(code[:, :, :], code[:, :, :], rank_b, ALU.mult))
                    link(dve.tensor_reduce(r, code[:, :, :], AX.X, ALU.max))
                    link(dve.tensor_tensor(oh[:, :, :], code[:, :, :], wide_e(r), ALU.is_equal))
                    if pick == 0:
                        link(dve.scalar_tensor_tensor(out=lg2[:, :, :], in0=oh1[:, :, :], scalar=-3.0e38,
                                                      in1=logit[:, :, :], op0=ALU.mult, op1=ALU.add))
                dve.tensor_tensor(gap[:, w, :], mm[:, 2, :], mm[:, 0, :], ALU.subtract).then_inc(sem("gap"), 1)

            def route_weights(w):
                dve.wait_ge(sem("ediff"), w + 1)
                link(dve.tensor_scalar(mm[:, 4, :], ediff[:, w, :], 1.0, None, ALU.add))
                link(dve.reciprocal(mm[:, 5, :], mm[:, 4, :]))
                link(dve.tensor_scalar(mm[:, 5, :], mm[:, 5, :], tg[:, 2:3], 0.5, ALU.mult, ALU.mult))
                link(dve.tensor_tensor(mm[:, 6, :], mm[:, 5, :], ediff[:, w, :], ALU.mult))
                link(dve.tensor_tensor(oh1[:, :, :], oh1[:, :, :], wide_e(mm[:, 5, :]), ALU.mult))
                link(dve.tensor_tensor(oh2[:, :, :], oh2[:, :, :], wide_e(mm[:, 6, :]), ALU.mult))
                dve.tensor_tensor(cw[:, w, :, :], oh1[:, :, :], oh2[:, :, :], ALU.add).then_inc(
                    sem("expert_weights"), 1)

            def hidden(n):
                if n >= EXPERTS:
                    return
                for c in range(CK0):
                    dve.wait_ge(sem("tanh_h"), CK0 * n + c + 1)
                    t = hT[:, (CK0 * n + c) % 4, :]
                    dve.scalar_tensor_tensor(out=t, in0=t, scalar=1.0, in1=bank(("h", n, c))[:, :], op0=ALU.add,
                                             op1=ALU.mult).then_inc(bank_free(("h", n, c)), 1)

            def queries_start(w):
                dve.wait_ge(sem("added"), (w + 1) * E0)
                statistics(("q1", w), x_tile(w))

            def queries_norm(w):
                normalise(("q1", w), lin_tile(w), x_tile(w)).then_inc(sem("lin_q1"), 1)

            def ffn_statistics(w):
                statistics(("ffn1", w), x_tile(w))

            def ffn_norm(w):
                normalise(("ffn1", w), lin_tile(w), x_tile(w)).then_inc(sem("lin_ffn1"), 1)
                dve.wait_ge(sem("lin_ffn1"), w + 1)

            dve.wait_ge(sem("loaded_y"), 16)
            dve.tensor_reduce(amax[0:NK, 0, 0:8], y[:, :, :], AX.X, ALU.max, apply_absolute_value=True)
            dve.wait_ge(sem("loaded_w0"), 16)
            for i, (a, b) in enumerate(w0part):
                ins = dve.tensor_reduce(wsum[:, i:i + 1], w0[:, a:b], AX.X, ALU.add, apply_absolute_value=True)
            ins.then_inc(sem("wsum"), 1)
            dve.wait_ge(sem("wsum"), 1)
            quant_scales("ctx0", NK, 8)
            dve.wait_ge(sem("loaded_x"), 16)
            statistics(("q0", 0), x_tile(0))

            def centre(w):
                i = norm_no[("q0", w)]
                for k in range(WB):
                    ins = dve.tensor_scalar(mid[:, w, k, :], x_tile(w)(k), mv[:, i, k, 0:1], None, ALU.subtract)
                link(ins)
                link(dve.tensor_reduce(amax[:, i, 0:WB], mid[:, w, :, :], AX.X, ALU.max, apply_absolute_value=True))
                quant_scales(("q0", w), 128, WB)

            centre(0)
            wait_full(dve, "wsum")
            dve.tensor_scalar(wsc[:, 0:3], bank("wsum")[:, 0:3], 1.0 / (D * D), 1e-5, ALU.mult, ALU.max)
            dve.tensor_scalar(wsc[:, 3:4], bank("wsum")[:, 3:4], 1.0 / (D * KVH * HD), 1e-5, ALU.mult,
                              ALU.max).then_inc(bank_free("wsum"), 1)
            wait_read(dve, "wsum")
            link(dve.reciprocal(winv[:, :], wsc[:, :]))
            link(dve.tensor_scalar(wsc[:, 0:1], wsc[:, 0:1], HD ** -0.5, None, ALU.mult))
            dequantise(lambda k: yq[:, k, :], "ctx0", B, NK, "yq")
            for i, (a, b) in enumerate(w0part):
                ins = dve.tensor_scalar(w0q[:, a:b], w0[:, a:b], winv[:, i:i + 1], MAGIC, ALU.mult, ALU.add)
            link(ins)
            dequantise(lin_tile(0), ("q0", 0), WB, 128, "lin_q0")
            link(dve.tensor_scalar(w0q[:, :], w0q[:, :], -MAGIC, -1.0, ALU.add, ALU.max))
            for i, (a, b) in enumerate(w0part):
                ins = dve.tensor_scalar(w0q[:, a:b], w0q[:, a:b], 1.0, wsc[:, i:i + 1], ALU.min, ALU.mult)
            ins.then_inc(sem("w0q"), 1)
            statistics(("q0", 1), x_tile(1))
            centre(1)
            split_keys0()
            split_queries(0, 0)
            dequantise(lin_tile(1), ("q0", 1), WB, 128, "lin_q0")
            dve.wait_ge(sem("ones_column"), 2)
            split_values0()
            dve.wait_ge(sem("loaded_const"), 16)
            dve.tensor_copy(identb[:, :], ident).then_inc(sem("identb"), 1)
            for n in range(MB * len(A_SPLIT)):
                maxima(0, n)
            split_maxima(0, 0)
            split_queries(0, 1)
            dve.wait_ge(sem("loaded_rows"), 16)
            dve.wait_ge(sem("tanh_gates"), 1)
            dve.tensor_scalar(tgbo[:, :], bo, tg[:, 1:2], None, ALU.mult).then_inc(sem("tgbo"), 1)

            def beside_layer0(i):
                if i == POST_STEP:
                    post_start(0)
                if i == POST_STEP + 2:
                    post_centre(0)
                if i == POST_STEP + 3:
                    post_maximum(0)
                if i == POST_STEP + 5:
                    post_scales(0)
                if i == POST_STEP + 8:
                    post_quantised(0)
                if i == POST_STEP + 11:
                    experts_statistics(0)
                if i == POST_STEP + 13:
                    experts_norm(0)

            for i in range(STEPS + LAG + 1):
                for j, step in enumerate(CHUNKS0):
                    if i == step + 1:
                        maxima(0, MB * len(A_SPLIT) + j)
                if i in TURNS0:
                    split_maxima(0, TURNS0[i])
                prob_rest(0, i)
                beside_layer0(i)
            for n in range(AHEAD):
                hidden(n)
            route(0)
            route_weights(0)
            post_start(1)
            post_centre(1)
            for n in range(EXPERTS):
                if n in CHUNKS_E:
                    maxima(1, CHUNKS_E.index(n))
                hidden(n + AHEAD)
                if n == 0:
                    post_maximum(1)
                    post_scales(1)
                if n == 2:
                    post_quantised(1)
                if n == 3:
                    experts_statistics(1)
                if n == 4:
                    experts_norm(1)
                if n == 6:
                    route(1)
                if n == 7:
                    route_weights(1)
                if n == E0 - 1:
                    queries_start(0)
                if n == E0:
                    queries_norm(0)
                if n == E0 + 1:
                    split_queries(1, 0)
                if n == 14:
                    split_maxima(1, 0)
                if n in CHUNKS_E:
                    maxima(1, CHUNKS_E.index(n) + 1)
            for j in range(CHUNKS_E.index(EXPERTS), len(CHUNKS_E)):
                maxima(1, j)
            split_maxima(1, 1)
            queries_start(1)

            def beside_layer1(i):
                if i == 2:
                    queries_norm(1)
                if i == 6:
                    split_queries(1, 1)
                if i == POST_STEP + 3:
                    dve.wait_ge(sem("bias_added"), WAVES)
                    residual(("post1", 0), 0, 1)
                if i == POST_STEP + 4:
                    ffn_statistics(0)
                if i == POST_STEP + 6:
                    ffn_norm(0)

            for i in range(STEPS + LAG + 1):
                for j, step in enumerate(CHUNKS1):
                    if i == step + 1:
                        maxima(1, WB * len(A_SPLIT) + j)
                if i in TURNS1:
                    split_maxima(1, TURNS1[i])
                prob_rest(1, i)
                beside_layer1(i)
            residual(("post1", 1), 1, 1)
            ffn_statistics(1)
            ffn_norm(1)
            dve.wait_ge(sem("loaded_gaug_b"), 16)
            wait_full(dve, "gexp")
            dve.tensor_scalar(gexp[:, :], bank("gexp")[:, 0:B], 1.0 / TOK, gatec[:, 1:2], ALU.mult,
                              ALU.add).then_inc(bank_free("gexp"), 1)
            wait_read(dve, "gexp")
            dve.tensor_tensor(gmat[:, :, :], rowsel.unsqueeze(2).to_broadcast([128, R, B]),
                              gexp[:, :].unsqueeze(1).to_broadcast([128, R, B]), ALU.mult).then_inc(sem("gmat"), 1)
            wait_full(dve, "gaug")
            dve.tensor_scalar(gaug[:, :], bank("gaug")[0:E1 + 1, 0:B], 1.0 / TOK, gaug_b[:, 0:1], ALU.mult,
                              ALU.add).then_inc(bank_free("gaug"), 1)
            wait_full(dve, "mb1")
            dve.tensor_copy(mb1[:, :, :], bank("mb1")[:, 0:CK1 * B].rearrange("p (c b) -> p c b", c=CK1)).then_inc(
                bank_free("mb1"), 1)
            for c in range(2 * NJ):
                i, j = c // NJ, c % NJ
                dve.wait_ge(sem(f"loaded_base{i}"), 16)
                if c >= 4:
                    d = c - 4
                    dve.wait_ge(sem(f"regrouped{d % 4}_{d // NJ}"), 16 * ((d % NJ) // 4 + 1))
                wait_full(dve, ("mix", c))
                dve.tensor_tensor(mixed[:, c % 4, :], bank(("mix", c))[:, :], base[i][:, j, :], ALU.add).then_inc(
                    bank_free(("mix", c)), 1)
            for b in range(B):
                wait_full(dve, ("out", b))
                dve.scalar_tensor_tensor(out=x[:, b, :], in0=bank(("out", b))[:, 0:D], scalar=tg[:, 3:4],
                                         in1=x[:, b, :], op0=ALU.mult, op1=ALU.add).then_inc(
                                             bank_free(("out", b)), 1)


def kernel(**inputs):
    import numpy as _np
    import concourse.bacc as _bacc
    from concourse import mybir as _mybir
    from concourse.bass_utils import run_bass_kernel_spmd as _run

    v = {k: _np.asarray(a) for k, a in inputs.items()}
    cat, c = _np.concatenate, _np.ascontiguousarray

    def by_dim(w, rep=1):
        n = w.shape[0] // HD
        w = _np.repeat(w.reshape(n, HD, -1), rep, axis=0)
        return w.transpose(2, 1, 0).reshape(w.shape[2], -1)

    def bias_by_dim(b):
        return b.reshape(H, HD).T.reshape(-1)

    const = _np.zeros((128, 128 + R + 8), _np.float32)
    const[:, :128] = _np.eye(128)
    const[:, 128:128 + R] = _np.tile(_np.eye(R), (E1, 1))
    const[:, 128 + R:] = _np.arange(8, 0, -1)
    one = _np.ones((1, 1), _np.float32)
    tw0 = v["L1_ffn_TW1"].transpose(0, 2, 1).reshape(E1, NJ, R, F1).transpose(0, 2, 1, 3)
    base0 = _np.repeat(v["L1_ffn_W1"].T.reshape(NJ, R, F1).transpose(1, 0, 2), B, axis=0)
    tw1 = v["L1_ffn_TW2"].reshape(E1, D, CK1, NJ, R).transpose(0, 4, 3, 2, 1)
    base1 = _np.repeat(v["L1_ffn_W2"].reshape(D, CK1, NJ, R).transpose(3, 2, 1, 0), B, axis=0)
    g2 = v["L1_ffn_gate_w2"]
    arrays = {
        "x": v["x"], "ctx": v["ctx_1024"], "const": const,
        "rows": cat([v["L0_xattn_ln_gamma"], v["L0_xattn_ln_beta"], v["L1_xattn_bo"], v["g_xattn"], v["g_ffn"]]),
        "w0": cat([by_dim(v["L0_xattn_wq"]), by_dim(v["L0_xattn_wk"], H // KVH), v["L0_xattn_wo"].T,
                   v["L0_xattn_wv"].T], 1),
        "w1": cat([by_dim(v["L1_xattn_Wq"]), by_dim(v["L1_xattn_Wk"]), v["L1_xattn_Wv"].T, v["L1_xattn_Wo"].T], 1),
        "bias1": _np.stack([bias_by_dim(v["L1_xattn_bq"]), bias_by_dim(v["L1_xattn_bk"]), v["L1_xattn_bv"]], 1),
        "router": v["L0_ffn_router_w"],
        "moe1": v["L0_ffn_w1"].transpose(1, 0, 2),
        "moe2": v["L0_ffn_w2"].reshape(E0, CK0, 128, D).transpose(2, 0, 1, 3),
        "gate1": v["L1_ffn_gate_w1"].T,
        "gatec": _np.stack([v["L1_ffn_gate_b1"], _np.repeat(v["L1_ffn_gate_b2"], R)], 1),
        "gate2": cat([_np.repeat(g2.T, R, axis=1), g2.T, _np.zeros((D, 1), _np.float32)], 1),
        "gaug_b": cat([v["L1_ffn_gate_b2"][:, None], one], 0),
        "tb": cat([cat([v["L1_ffn_Tb1"], v["L1_ffn_Tb2"]], 1),
                   cat([v["L1_ffn_b1"], v["L1_ffn_b2"]])[None]], 0),
        "tw0": tw0.reshape(128, NJ, 512), "base0": base0.reshape(128, NJ, 512),
        "tw1": tw1.reshape(128, NJ, 512), "base1": base1.reshape(128, NJ, 512),
    }
    arrays = {k: c(a) for k, a in arrays.items()}
    nc = _bacc.Bacc("TRN2", target_bir_lowering=False, num_devices=1)
    io = {k: nc.dram_tensor("in_" + k, a.shape, _mybir.dt.from_np(a.dtype), kind="ExternalInput").ap()
          for k, a in arrays.items()}
    io["out"] = nc.dram_tensor("out", (B, TOK, D), F32, kind="ExternalOutput").ap()
    build(nc, io)
    r = _run(nc, [{"in_" + k: a for k, a in arrays.items()}], core_ids=[0])
    return r.results[0]["out"]
```

```python
from contextlib import ExitStack

import concourse.bass as bass
from concourse import mybir

F32 = mybir.dt.float32
BF16 = mybir.dt.bfloat16
FP16 = mybir.dt.float16
ACT = mybir.ActivationFunctionType
ALU = mybir.AluOpType
AX = mybir.AxisListType

B, TOK, D = 8, 128, 128
NK = 77
H, HD, KVH = 16, 8, 8
E0, F0 = 8, 256
E1, F1 = 8, 512
R = D // E1
NJ = D // R
CK0, CK1 = F0 // 128, F1 // 128
WAVES = 2
WB = B // WAVES
WT = WB * TOK
PARTS = 3
PAIRS = [(0, 0), (0, 1), (1, 0), (1, 1), (0, 2), (2, 0)]
QK_ROWS = len(PAIRS) * HD
ST_ROWS = QK_ROWS + PARTS
VW = HD + 1
PGROUP = 4
NG = H // PGROUP
STEPS = B * NG
PRING = 7
LAG = 4
MB = 2
EXPERTS = WAVES * E0
AHEAD = 2
CHUNKS0 = list(range(18))
SPLITS0 = {6: 1, 12: 2, 18: 3}
TURNS0 = {7: 1, 13: 2, 19: 3}
CHUNKS_E = [13, 13, 14, 14, 15, 15]
CHUNKS1 = [0, 1, 2, 3, 4, 5, 10, 10, 11, 11, 12, 12, 14, 15, 16, 17, 18, 19]
SPLITS1 = {6: 1, 13: 2, 20: 3}
TURNS1 = {7: 1, 14: 2, 21: 3}
CTX_STEP = 2
POST_STEP = WB * NG + LAG
ENDS1 = [14, 21, 28]
END_FFN = 6
MAGIC = 1.5 * 2.0 ** 23
ROWS = 3 * D + 4
A_SPLIT = [(0, 6), (6, 12), (12, 16)]

NORMS = ["ctx0", ("q0", 0), ("q0", 1), ("mid0", 0), ("rms0", 0), ("moe", 0), ("mid0", 1), ("rms0", 1), ("moe", 1),
         ("q1", 0), ("q1", 1), ("ffn1", 0), ("ffn1", 1), ("ffn1", 2), ("ffn1", 3)]
NORM_FORM = {"ctx0": (1.0 / D, 1e-6), "q0": (1.0 + 1e-6, 1e-11), "mid0": (1.0, 1e-5), "rms0": (1.0 / D, 1e-6),
             "moe": (1.0, 1e-5), "q1": (1.0, 1e-5), "ffn1": (1.0, 1e-5)}


def build(nc, io):
    ctx = ExitStack()
    with ctx:
        def sb(name, shape, dt=F32):
            return ctx.enter_context(nc.sbuf_tensor(name, shape, dt))

        sems = {}

        def sem(name):
            if name not in sems:
                sems[name] = ctx.enter_context(nc.semaphore(name))
            return sems[name]

        rings = {r: [ctx.enter_context(nc.psum_tensor(f"ps_{r}{i}", [128, 512], F32)) for i in range(2)]
                 for r in "taso"}
        place = {}
        taken = {r: 0 for r in rings}
        fulls = {(r, i): 0 for r in rings for i in range(2)}

        def open_bank(pe, key, ring, signalled=True):
            i = taken[ring] % 2
            place[key] = (ring, i, taken[ring] // 2, fulls[ring, i])
            taken[ring] += 1
            fulls[ring, i] += signalled
            if place[key][2]:
                pe.wait_ge(bank_free(key), place[key][2])
            return bank(key)

        def bank(key):
            r, i, _, _ = place[key]
            return rings[r][i]

        def bank_full(key):
            r, i, _, _ = place[key]
            return sem(f"full_{r}{i}")

        def bank_free(key):
            r, i, _, _ = place[key]
            return sem(f"free_{r}{i}")

        def wait_full(eng, key):
            eng.wait_ge(bank_full(key), place[key][3] + 1)

        def wait_read(eng, key):
            eng.wait_ge(bank_free(key), place[key][2] + 1)

        x = sb("x", [128, B, D])
        y = sb("y", [NK, B, D])
        attn = sb("attn", [128, B, D])
        yq = attn[0:NK, :, :]
        yT = sb("yT", [128, B * NK])
        const = sb("const", [128, 128 + R + 8])
        ident, rowsel, rank = const[:, 0:128], const[:, 128:128 + R], const[:, 128 + R:]
        identb = sb("identb", [128, 128], BF16)
        ones = sb("ones", [128, 128])
        onesb = sb("onesb", [PARTS, B * NK], BF16)
        neghalf = sb("neghalf", [128, 8])
        rows = sb("rows", [128, ROWS])
        gamma, beta, bo = (rows[:, i * D:(i + 1) * D] for i in range(3))
        tg = sb("tg", [128, 4])
        w0 = sb("w0", [128, 448])
        w0q = sb("w0q", [128, 448])
        w0part = [(0, 128), (128, 256), (256, 384), (384, 448)]
        wsum = sb("wsum", [128, 4])
        wsc = sb("wsc", [128, 4])
        winv = sb("winv", [128, 4])
        w1 = sb("w1", [128, 512])
        bias1 = sb("bias1", [128, 3])
        router = sb("router", [128, E0])
        moe = sb("moe", [128, 2, E0, F0])
        moe1 = moe[:, 0, :, :]
        moe2 = moe[:, 1, :, :].rearrange("p e (c d) -> p e c d", c=CK0)
        gate1 = sb("gate1", [128, D])
        gatec = sb("gatec", [128, 2])
        gate2 = sb("gate2", [128, 128 + E1 + 1])
        gaug_b = sb("gaug_b", [E1 + 1, 1])
        tb = sb("tb", [E1 + 1, F1 + D])
        tw = [sb(f"tw{i}", [128, NJ, 512]) for i in range(2)]
        keyroom = sb("keyroom", [128, H * B * NK // 2])
        kst = keyroom[0:64, :].bitcast(BF16).rearrange("p (h s) -> p h s", h=H)
        base = [moe[:, :, :, :].rearrange("p a e f -> p (a e f)").rearrange("p (j f) -> p j f", j=NJ),
                keyroom[:, 0:NJ * 512].rearrange("p (j f) -> p j f", j=NJ)]
        mw = sb("mw", [128, 2, B, 512])
        qst = mw[0:64, :, :, :].rearrange("p a b f -> p (a b f)").bitcast(BF16).rearrange("p (h t) -> p h t", h=H)
        vst = [sb(f"vst{i}", [NK, B, n, PARTS, VW], BF16)
               for i, n in enumerate((KVH, H))]
        lin = sb("lin", [128, WAVES, WB, D])
        mid = sb("mid", [128, WAVES, WB, D])
        linT = sb("linT", [128, B * TOK])
        kproj = sb("kproj", [128, 640])
        qproj = sb("qproj", [128, WAVES, WT])
        rest = sb("rest", [128, 640])
        krest = qproj[:, :, :].rearrange("p w t -> p (w t)")
        kparts = sb("kparts", [128, PARTS, B * NK], BF16)
        qparts = sb("qparts", [128, WAVES, PARTS, WT], BF16)
        nmax = sb("nmax", [128, B, H])
        mrest = sb("mrest", [128, MB, H])
        mparts = sb("mparts", [128, B, PARTS, H], BF16)
        maxT = sb("maxT", [PARTS * H, B, TOK], BF16)
        ph = sb("ph", [NK, PRING, 512], FP16)
        pl = sb("pl", [NK, PRING, 512], FP16)
        osum = sb("osum", [128, H, VW])
        rden = sb("rden", [128, H])
        st = sb("st", [128, len(NORMS), WB, 6])
        mv = sb("mv", [128, len(NORMS), WB, 2])
        sq = sb("sq", [128, len(NORMS), 8])
        nin = sb("nin", [128, len(NORMS), 8])
        rstd = sb("rstd", [128, len(NORMS), 8])
        amax = sb("amax", [128, len(NORMS), 8])
        am1 = sb("am1", [128, 8])
        am2 = sb("am2", [128, 8])
        comb = sb("comb", [128, len(NORMS), 8])
        inv = sb("inv", [128, len(NORMS), 8])
        magic = sb("magic", [128, 1])
        logit = sb("logit", [128, WB, E0])
        lg2 = sb("lg2", [128, WB, E0])
        oh1 = sb("oh1", [128, WB, E0])
        oh2 = sb("oh2", [128, WB, E0])
        code = sb("code", [128, WB, E0])
        cw = sb("cw", [128, WAVES, WB, E0])
        mm = sb("mm", [128, 8, WB])
        ediff = sb("ediff", [128, WAVES, WB])
        gap = sb("gap", [128, WAVES, WB])
        hT = sb("hT", [128, 4, WT])
        p32 = [hT[0:NK, i, :] for i in range(4)] + [sb(f"p32_{i}", [NK, 512])[:, :] for i in range(4, PRING)]
        ys = [kproj[:, 0:WT], yT[:, 0:WT]]
        mixed = hT
        hs = sb("hs", [128, B])
        relu_out = mid[:, 0, :, :].rearrange("t b d -> t (b d)")
        tgbo = sb("tgbo", [128, D])
        bias_q = sb("bias_q", [128, 1])
        gexp = sb("gexp", [128, B])
        gmat = sb("gmat", [128, R, B])
        gaug = sb("gaug", [E1 + 1, B])
        gtok = y[0:E1 + 1, :, :]
        mb1 = sb("mb1", [128, CK1, B])
        uT = qproj[:, :, :].rearrange("p w (c t) -> p w c t", c=CK1)

        norm_no = {k: i for i, k in enumerate(NORMS)}
        block = ctx.enter_context(nc.Block())

        def prob_group(n):
            return f"S{n // (B * NG)}", n // NG % B, n % NG

        def batches(w):
            return range(w * WB, (w + 1) * WB)

        def lin_of(b):
            return lin[:, b // WB, b % WB, :]

        def flat(v):
            return v.rearrange("t b d -> t (b d)")

        wide = WB * NK

        @block.tensor
        def _(pe):
            def turn(key, ring, tiles, dt=F32):
                p = open_bank(pe, key, ring)
                for dst, src, n in tiles(p):
                    ins = pe.transpose(dst, src, (identb if dt == BF16 else ident)[0:n, 0:n])
                ins.then_inc(bank_full(key), 1)

            def product(key, ring, terms):
                p = open_bank(pe, key, ring)
                for out, lhsT, rhs in terms(p):
                    ins = pe.matmul(out, lhsT, rhs, start=True, stop=True)
                ins.then_inc(bank_full(key), 1)

            def turn_context(layer):
                src = y if layer else yq
                for i in range(2):
                    turn((f"y{layer}T", i), "t",
                         lambda p: [(p[:, k * NK:(k + 1) * NK], src[:, i * WB + k, :], NK) for k in range(WB)])

            def keys(layer):
                weights = w1 if layer else w0q
                for i in range(2):
                    wait_read(pe, (f"y{layer}T", i))
                    product((f"k{layer}", i), "t",
                            lambda p: [(p[:, 0:wide], weights[:, 128:256], yT[:, i * wide:(i + 1) * wide])])

            def context_values(layer, i):
                wv = w1[:, 256:384] if layer else w0q[:, 384:448]
                n = wv.shape[1]
                tiles = 512 // n
                product((f"v{layer}", i), "t",
                        lambda p: [(p[0:NK, k * n:(k + 1) * n],
                                    yT[:, (i * tiles + k) * NK:(i * tiles + k + 1) * NK], wv)
                                   for k in range(tiles)])

            def turn_wave(key, src, ring="t"):
                turn(key, ring, lambda p: [(p[:, k * TOK:(k + 1) * TOK], src[:, k, :], 128) for k in range(WB)])

            def turn_queries(layer, w, ring="t"):
                pe.wait_ge(sem(f"lin_q{layer}"), w + 1)
                turn_wave((f"q{layer}T", w), lin[:, w, :, :], ring)

            def queries(layer, w, ring="t"):
                wait_read(pe, (f"q{layer}T", w))
                weights = w1 if layer else w0q
                product((f"q{layer}", w), ring,
                        lambda p: [(p[:, :], weights[:, 0:128], linT[:, w * WT:(w + 1) * WT])])

            def scores_for_max(layer, n, ring="a"):
                b, c = n // len(A_SPLIT), n % len(A_SPLIT)
                h0, h1 = A_SPLIT[c]
                pe.wait_ge(sem(f"q_stacked{b // WB}"), 16 * len(PAIRS) * (layer + 1))
                pe.wait_ge(sem("k_stacked"), 16 * len(PAIRS) * (layer + 1))
                product((f"A{layer}", b, c), ring,
                        lambda p: [(p[:, (h - h0) * NK:(h - h0 + 1) * NK],
                                    qst[0:QK_ROWS, h, b * TOK:(b + 1) * TOK],
                                    kst[0:QK_ROWS, h, b * NK:(b + 1) * NK]) for h in range(h0, h1)])

            def turn_maxima(layer, m, ring="t"):
                pe.wait_ge(sem("max_split"), layer * B // MB + m + 1)
                turn((f"max{layer}T", m), ring,
                     lambda p: [(p[0:PARTS * H, k * TOK // 2:(k + 1) * TOK // 2].bitcast(BF16),
                                 mparts[:, m * MB + k, :, :].rearrange("t p h -> t (p h)"), 128)
                                for k in range(MB)], BF16)

            def scores(layer, b, g):
                pe.wait_ge(sem(f"max_stacked{b // MB}"), 16 * (layer + 1))
                pe.wait_ge(sem("ones_stacked"), 16)
                product((f"S{layer}", b, g), "s",
                        lambda p: [(p[0:NK, k * TOK:(k + 1) * TOK],
                                    kst[0:ST_ROWS, g * PGROUP + k, b * NK:(b + 1) * NK],
                                    qst[0:ST_ROWS, g * PGROUP + k, b * TOK:(b + 1) * TOK]) for k in range(PGROUP)])

            def values(layer, b, g):
                n = (layer * B + b) * NG + g
                key = (f"O{layer}", b)
                if g == 0:
                    open_bank(pe, key, "o", signalled=False)
                pe.wait_ge(sem("prob_rest_pool" if n % 2 else "prob_rest"), n // 2 + 1)
                o, s = bank(key), n % PRING
                for k in range(PGROUP):
                    h = g * PGROUP + k
                    col = h * PARTS * VW
                    v = vst[layer][:, b, h if layer else h // 2, :, :].rearrange("s p d -> s (p d)")
                    pe.matmul(o[:, col:col + PARTS * VW], ph[:, s, k * TOK:(k + 1) * TOK], v, start=True, stop=False,
                              skip_group_check=True)
                    ins = pe.matmul(o[:, col:col + 2 * VW], pl[:, s, k * TOK:(k + 1) * TOK], v[:, 0:2 * VW],
                                    start=False, stop=True, skip_group_check=True)
                ins.then_inc(sem("pv_done"), 1)

            def attention(layer, beside):
                pe.wait_ge(sem("v_split" if layer == 0 else "v1_split"), layer + 1)
                for i in range(STEPS + LAG):
                    if i < STEPS:
                        scores(layer, i // NG, i % NG)
                    beside(i)
                    if i >= LAG:
                        values(layer, (i - LAG) // NG, (i - LAG) % NG)

            def turn_post0(w, ring="t"):
                pe.wait_ge(sem("lin_post0"), w + 1)
                turn_wave(("post0T", w), lin[:, w, :, :], ring)

            def post0(w, ring="t"):
                wait_read(pe, ("post0T", w))
                product(("post0", w), ring,
                        lambda p: [(p[:, k * TOK:(k + 1) * TOK], linT[:, b * TOK:(b + 1) * TOK], w0q[:, 256:384])
                                   for k, b in enumerate(batches(w))])

            def turn_post1(m):
                pe.wait_ge(sem("attn_done"), B + (m + 1) * MB)
                turn(("post1T", m), "t",
                     lambda p: [(p[:, k * TOK:(k + 1) * TOK], attn[:, m * MB + k, :], 128) for k in range(MB)])

            def post1(m):
                wait_read(pe, ("post1T", m))
                product(("post1", m), "t",
                        lambda p: [(p[:, k * TOK:(k + 1) * TOK],
                                    linT[:, (m * MB + k) * TOK:(m * MB + k + 1) * TOK], w1[:, 384:512])
                                   for k in range(MB)])

            def turn_experts(w, ring="t"):
                pe.wait_ge(sem("lin_moe"), w + 1)
                turn_wave(("moeT", w), lin[:, w, :, :], ring)

            def route(w):
                product(("router", w), "a",
                        lambda p: [(p[:, k * E0:(k + 1) * E0],
                                    linT[:, (w * WB + k) * TOK:(w * WB + k + 1) * TOK], router[:, :])
                                   for k in range(WB)])

            def hidden(n):
                w, e = n // E0, n % E0
                if e == 0:
                    wait_read(pe, ("moeT", w))
                for c in range(CK0):
                    product(("h", n, c), "ts"[n % 2],
                            lambda p: [(p[:, :], moe1[:, e, c * 128:(c + 1) * 128], linT[:, w * WT:(w + 1) * WT])])

            def expert_out(n):
                for c in range(CK0):
                    wait_read(pe, ("h", n, c))
                p = open_bank(pe, ("y", n), "a")
                for k in range(WB):
                    for c in range(CK0):
                        ins = pe.matmul(p[:, k * D:(k + 1) * D], hT[:, (CK0 * n + c) % 4, k * TOK:(k + 1) * TOK],
                                        moe2[:, n % E0, c, :], start=(c == 0), stop=(c == CK0 - 1))
                ins.then_inc(bank_full(("y", n)), 1)

            def turn_ffn(m):
                pe.wait_ge(sem("lin_ffn1"), m + 1)
                turn(("ffnT", m), "t",
                     lambda p: [(p[:, k * TOK:(k + 1) * TOK], lin_of(m * MB + k), 128) for k in range(MB)])

            def ffn_gate(m):
                wait_read(pe, ("ffnT", m))
                product(("gate", m), "t", lambda p: [(p[:, 0:MB * TOK], gate1[:, :],
                                                      linT[:, m * MB * TOK:(m + 1) * MB * TOK])])

            pe.wait_ge(sem("constants"), 1)
            pe.wait_ge(sem("wsum"), 1)
            product("wsum", "t", lambda p: [(p[:, 0:4], ones[:, :], wsum[:, :])])
            pe.wait_ge(sem("loaded_const"), 16)
            pe.wait_ge(sem("yq"), 1)
            turn_context(0)
            turn_queries(0, 0)
            pe.wait_ge(sem("w0q"), 1)
            keys(0)
            queries(0, 0)
            context_values(0, 0)
            turn_queries(0, 1)
            queries(0, 1)
            pe.wait_ge(sem("identb"), 1)
            for n in range(MB * len(A_SPLIT)):
                scores_for_max(0, n)
            turn_maxima(0, 0)

            def beside_layer0(i):
                for j, step in enumerate(CHUNKS0):
                    if i == step:
                        scores_for_max(0, MB * len(A_SPLIT) + j)
                if i in TURNS0:
                    turn_maxima(0, TURNS0[i])
                if i == CTX_STEP:
                    turn_context(1)
                if i == CTX_STEP + 1:
                    pe.wait_ge(sem("loaded_w1"), 16)
                    keys(1)
                if i == CTX_STEP + 4:
                    context_values(1, 0)
                if i == CTX_STEP + 10:
                    context_values(1, 1)
                if i == POST_STEP + 8:
                    turn_post0(0)
                if i == POST_STEP + 9:
                    post0(0)
                if i == POST_STEP + 13:
                    turn_experts(0)

            attention(0, beside_layer0)
            for name in ("router", "moe1", "moe2"):
                pe.wait_ge(sem("loaded_" + name), 16)
            hidden(0)
            route(0)
            hidden(1)
            for n in range(EXPERTS):
                if n in CHUNKS_E:
                    scores_for_max(1, CHUNKS_E.index(n), "o")
                expert_out(n)
                if n + AHEAD < EXPERTS:
                    hidden(n + AHEAD)
                if n == 3:
                    turn_post0(1, "o")
                if n == 4:
                    post0(1, "o")
                if n == 5:
                    turn_experts(1, "o")
                if n == 6:
                    route(1)
                if n == E0 + 1:
                    turn_queries(1, 0, "o")
                if n == E0 + 2:
                    queries(1, 0, "o")
                if n in CHUNKS_E:
                    scores_for_max(1, CHUNKS_E.index(n) + 1, "o")
            turn_maxima(1, 0)
            for name in ("gate1", "gate2", "tb"):
                pe.wait_ge(sem("loaded_" + name), 16)

            def beside_layer1(i):
                if i == 4:
                    turn_queries(1, 1)
                if i == 5:
                    queries(1, 1)
                for j, step in enumerate(CHUNKS1):
                    if i == step:
                        scores_for_max(1, MB * len(A_SPLIT) + j)
                if i in TURNS1:
                    turn_maxima(1, TURNS1[i])
                for m, step in enumerate(ENDS1):
                    if i == step:
                        turn_post1(m)
                    if i == step + 1:
                        post1(m)
                    if i == step + END_FFN:
                        turn_ffn(m)
                    if i == step + END_FFN + 1:
                        ffn_gate(m)

            attention(1, beside_layer1)
            m = len(ENDS1)
            turn_post1(m)
            post1(m)
            turn_ffn(m)
            ffn_gate(m)
            for m in range(B // MB):
                wait_read(pe, ("gate", m))
            product("gexp", "t", lambda p: [(p[:, 0:B], gate2[:, 0:128], hs[:, :])])
            product("gaug", "t", lambda p: [(p[0:E1 + 1, 0:B], gate2[:, 128:], hs[:, :])])
            pe.wait_ge(sem("gmat"), 1)
            for c in range(2 * NJ):
                i, j = c // NJ, c % NJ
                pe.wait_ge(sem(f"loaded_tw{i}"), 16)
                product(("mix", c), "as"[c // 2 % 2],
                        lambda p: [(p[:, :], gmat[:, :, :].rearrange("p r b -> p (r b)"), tw[i][:, j, :])])
                if c == NJ:
                    wait_read(pe, "gaug")
                    product("mb1", "t", lambda p: [(p[:, q * B:(q + 1) * B], tb[:, q * 128:(q + 1) * 128], gaug[:, :])
                                                   for q in range(CK1)])

            def ffn_up(b):
                product(("u", b), "sa"[b // 2 % 2],
                        lambda p: [(p[:, c * TOK:(c + 1) * TOK], mw[:, 0, b, c * 128:(c + 1) * 128],
                                    linT[:, b * TOK:(b + 1) * TOK]) for c in range(CK1)])

            def regrouped(i):
                for q in range(4):
                    pe.wait_ge(sem(f"regrouped{q}_{i}"), 16 * NJ // 4)

            regrouped(0)
            ffn_up(0)
            ffn_up(1)
            pe.wait_ge(sem("gtok"), 1)
            for b in range(B):
                if b + 2 < B:
                    ffn_up(b + 2)
                wait_read(pe, ("u", b))
                if b == 0:
                    regrouped(1)
                p = open_bank(pe, ("out", b), "t")
                for c in range(CK1):
                    pe.matmul(p[:, 0:D], uT[:, b % 2, c, :], mw[:, 1, b, c * D:(c + 1) * D], start=(c == 0), stop=False)
                pe.matmul(p[:, 0:D], gtok[:, b, :], tb[:, F1:F1 + D], start=False, stop=True).then_inc(
                    bank_full(("out", b)), 1)

        @block.sync
        def _(sp):
            def load(name, dst, src):
                sp.dma_start(dst, src).then_inc(sem("loaded_" + name), 16)

            load("y", y[:, :, :], io["ctx"].rearrange("b s d -> s b d"))
            load("w0", w0[:, :], io["w0"])
            load("x", x[:, :, :], io["x"].rearrange("b t d -> t b d"))
            load("const", const[:, :], io["const"])
            load("rows", rows[:, :], io["rows"].partition_broadcast(128))
            load("w1", w1[:, :], io["w1"])
            load("bias1", bias1[:, :], io["bias1"])
            sp.wait_ge(sem("constants"), 1)
            sp.dma_start(kst[QK_ROWS:ST_ROWS, :, :],
                         onesb[:, :].unsqueeze(1).to_broadcast([PARTS, H, B * NK])).then_inc(sem("ones_stacked"), 16)

            def stack_keys(layer, first):
                if first:
                    for i in range(2):
                        wait_read(sp, (f"k{layer}", i))
                else:
                    sp.wait_ge(sem("k1_split" if layer else "k_split"), 1)
                if layer:
                    sp.wait_ge(sem("attn_done"), B)
                for r, (_, kp) in enumerate(PAIRS):
                    if (kp == 0) == first:
                        sp.dma_start(kst[HD * r:HD * (r + 1), :, :], kparts[:, kp, :]).then_inc(sem("k_stacked"), 16)

            def stack_queries(layer, w, first):
                if first:
                    wait_read(sp, (f"q{layer}", w))
                else:
                    sp.wait_ge(sem("q_split"), layer * WAVES + w + 1)
                for r, (qp, _) in enumerate(PAIRS):
                    if (qp == 0) == first:
                        sp.dma_start(qst[HD * r:HD * (r + 1), :, w * WT:(w + 1) * WT],
                                     qparts[:, w, qp, :]).then_inc(sem(f"q_stacked{w}"), 16)

            def stack_maxima(layer, m):
                wait_read(sp, (f"max{layer}T", m))
                sp.dma_start(qst[QK_ROWS:ST_ROWS, :, m * MB * TOK:(m + 1) * MB * TOK],
                             maxT[:, m * MB:(m + 1) * MB, :]).then_inc(sem(f"max_stacked{m}"), 16)

            stack_keys(0, True)
            stack_queries(0, 0, True)
            stack_keys(0, False)
            stack_queries(0, 0, False)
            stack_queries(0, 1, True)
            stack_maxima(0, 0)
            stack_queries(0, 1, False)
            load("router", router[:, :], io["router"])
            load("moe1", moe1[:, :, :], io["moe1"])
            load("moe2", moe2[:, :, :, :], io["moe2"])
            for m in range(1, B // MB):
                stack_maxima(0, m)
            load("gate1", gate1[:, :], io["gate1"])
            load("gatec", gatec[:, :], io["gatec"])
            load("gate2", gate2[:, :], io["gate2"])
            load("gaug_b", gaug_b[:, :], io["gaug_b"])
            load("tb", tb[:, :], io["tb"])
            load("tw0", tw[0][:, :, :], io["tw0"])
            load("tw1", tw[1][:, :, :], io["tw1"])
            stack_keys(1, True)
            stack_keys(1, False)
            stack_queries(1, 0, True)
            stack_queries(1, 0, False)
            stack_maxima(1, 0)
            stack_queries(1, 1, True)
            stack_maxima(1, 1)
            stack_queries(1, 1, False)
            wait_full(sp, ("y", EXPERTS - 2))
            wait_full(sp, ("y", EXPERTS - 1))
            load("base0", base[0][:, :, :], io["base0"])
            for m in range(WB // MB, B // MB):
                stack_maxima(1, m)
            sp.wait_ge(sem("attn_done"), 2 * B)
            load("base1", base[1][:, :, :], io["base1"])
            for c in range(2 * NJ):
                i, j = c // NJ, c % NJ
                wait_read(sp, ("mix", c))
                sp.dma_start(mw[R * j:R * (j + 1), i, :, :], mixed[:, c % 4, :]).then_inc(
                    sem(f"regrouped{c % 4}_{i}"), 16)
            for b in range(B):
                wait_read(sp, ("out", b))
                sp.dma_start(io["out"][b], x[:, b, :]).then_inc(sem("stored"), 16)
            sp.wait_ge(sem("stored"), 16 * B)

        @block.gpsimd
        def _(pool):
            count = [0]

            def link(ins):
                count[0] += 1
                ins.then_inc(sem("pool_chain"), 1)
                pool.wait_ge(sem("pool_chain"), count[0])

            given = {k: n + 1 for n, k in enumerate(k for k in NORMS if k[0] not in ("c", "rms0"))}

            def inverse_root(key):
                i = norm_no[key]
                kind = key if isinstance(key, str) else key[0]
                scale, eps = NORM_FORM[kind]
                n, p = (8, NK) if kind == "ctx0" else (MB if kind == "ffn1" else WB, 128)
                if kind in ("ctx0", "rms0"):
                    pool.wait_ge(sem("squares"), 1 if kind == "ctx0" else 2 + key[1])
                    src = sq[0:p, i, 0:n]
                else:
                    pool.wait_ge(sem("variance"), given[key])
                    src = mv[0:p, i, 0:n, 1]
                link(pool.tensor_scalar(nin[0:p, i, 0:n], src, scale, eps, ALU.mult, ALU.add))
                pool.tensor_tensor(rstd[0:p, i, 0:n], nin[0:p, i, 0:n], neghalf[0:p, 0:n],
                                   ALU.pow).then_inc(sem("rstd"), 1)

            def prob_rests(layer, beside):
                for i in range(STEPS + LAG):
                    n = layer * STEPS + i
                    if i < STEPS and n % 2:
                        pool.wait_ge(sem("prob_first"), n + 1)
                        s = n % PRING
                        pool.tensor_tensor(pl[:, s, :], p32[s], ph[:, s, :], ALU.subtract).then_inc(
                            sem("prob_rest_pool"), 1)
                    beside(i)

            def split_rest(step, src, d0, d1, d2, r, done, times):
                if step == 0:
                    link(pool.tensor_tensor(r, src, d0, ALU.subtract))
                if step == 1:
                    link(pool.tensor_copy(d1, r))
                if step == 2:
                    pool.tensor_tensor(d2, r, d1, ALU.subtract).then_inc(sem(done), 1)
                    pool.wait_ge(sem(done), times)

            def split_keys1(step):
                if step == 0:
                    pool.wait_ge(sem("q_split"), WAVES)
                    for i in range(2):
                        wait_read(pool, ("k1", i))
                n = B * NK
                split_rest(step, kproj[:, 0:n], *(kparts[:, i, :] for i in range(PARTS)), krest[:, 0:n],
                           "k1_split", 1)

            def split_values1(step, i):
                if step == 0:
                    wait_read(pool, ("v1", i))

                def view(t):
                    return t[0:NK, 0:512].rearrange("s (b h d) -> s b h d", b=WB, h=H)

                split_rest(step, view(kproj), *(vst[1][:, i * WB:(i + 1) * WB, :, p, 0:HD] for p in range(PARTS)),
                           view(krest), "v1_split", i + 1)

            def add_expert(n):
                w = n // E0
                if n % E0 == 0:
                    pool.wait_ge(sem("lin_moe"), w + 1)
                wait_read(pool, ("y", n))
                xw = x[:, w * WB:(w + 1) * WB, :]
                pool.tensor_tensor(xw, xw, ys[n % 2].rearrange("t (b d) -> t b d", b=WB), ALU.add).then_inc(
                    sem("added"), 1)
                pool.wait_ge(sem("added"), n + 1)

            def add_bias(w):
                pool.wait_ge(sem("lin_q1"), w + 1)
                pool.wait_ge(sem("tgbo"), 1)
                xw = x[:, w * WB:(w + 1) * WB, :]
                pool.tensor_tensor(xw, xw, tgbo[:, :].unsqueeze(1).to_broadcast([128, WB, D]), ALU.add).then_inc(
                    sem("bias_added"), 1)

            pool.memset(magic[:, :], MAGIC)
            pool.memset(neghalf[:, :], -0.5)
            pool.memset(onesb[:, :], 1.0)
            pool.memset(ones[:, :], 1.0).then_inc(sem("constants"), 1)
            pool.wait_ge(sem("constants"), 1)
            inverse_root("ctx0")
            inverse_root(("q0", 0))
            inverse_root(("q0", 1))
            for v in vst:
                link(pool.memset(v[:, :, :, 0, HD:VW], 1.0))
                pool.memset(v[:, :, :, 1:PARTS, HD:VW], 0.0).then_inc(sem("ones_column"), 1)

            def beside_layer0(i):
                c = i - CTX_STEP - 2
                if c >= 0 and c % 2 == 0:
                    if c // 2 < 3:
                        split_keys1(c // 2)
                    elif c // 2 < 9:
                        split_values1(c // 2 % 3, c // 2 // 3 - 1)
                if i == POST_STEP + 1:
                    inverse_root(("mid0", 0))
                if i == POST_STEP + 4:
                    inverse_root(("rms0", 0))
                if i == POST_STEP + 12:
                    inverse_root(("moe", 0))

            prob_rests(0, beside_layer0)
            inverse_root(("mid0", 1))
            for n in range(EXPERTS):
                add_expert(n)
                if n == 1:
                    inverse_root(("rms0", 1))
                if n == 4:
                    inverse_root(("moe", 1))
                if n == E0 - 1:
                    inverse_root(("q1", 0))
                if n == E0 + 4:
                    add_bias(0)
            inverse_root(("q1", 1))

            def beside_layer1(i):
                if i == 4:
                    add_bias(1)
                for m, step in enumerate(ENDS1):
                    if i == step + 2:
                        inverse_root(("ffn1", m))

            prob_rests(1, beside_layer1)
            inverse_root(("ffn1", len(ENDS1)))
            wait_read(pool, "gaug")
            pool.tensor_copy(gtok[:, :, :], gaug[:, :].unsqueeze(2).to_broadcast([E1 + 1, B, TOK])).then_inc(
                sem("gtok"), 1)

        @block.scalar
        def _(act):
            def move(key, dst, src, scale=1.0, bias=0.0, part=None):
                wait_full(act, key)
                ins = act.activation(dst, src, ACT.Identity, bias=bias, scale=scale)
                if part is not None:
                    ins = act.activation(part, src, ACT.Identity, bias=bias, scale=scale)
                ins.then_inc(bank_free(key), 1)

            def turned_context(layer):
                for i in range(2):
                    move((f"y{layer}T", i), yT[:, i * wide:(i + 1) * wide], bank((f"y{layer}T", i))[:, 0:wide])

            def keys(layer):
                if layer:
                    act.wait_ge(sem("v_split"), 1)
                    act.wait_ge(sem("k_stacked"), 16 * len(PAIRS))
                for i in range(2):
                    cols = slice(i * wide, (i + 1) * wide)
                    move((f"k{layer}", i), kproj[:, cols], bank((f"k{layer}", i))[:, 0:wide],
                         bias=bias1[:, 1:2] if layer else 0.0, part=kparts[:, 0, cols])

            def value_view(layer, i, t):
                shape = dict(b=WB, h=H) if layer else dict(b=B, h=KVH)
                return t[0:NK, 0:512].rearrange("s (b h d) -> s b h d", **shape)

            def context_values(layer, i):
                key = (f"v{layer}", i)
                if layer:
                    act.wait_ge(sem("v1_split" if i else "k1_split"), 1)
                    dst = vst[1][:, i * WB:(i + 1) * WB, :, 0, 0:HD]
                else:
                    act.wait_ge(sem("k_split"), 1)
                    dst = vst[0][:, :, :, 0, 0:HD]
                wait_full(act, key)
                act.activation(kproj[0:NK, 0:512], bank(key)[0:NK, :], ACT.Identity)
                act.activation(dst, value_view(layer, i, bank(key)), ACT.Identity).then_inc(bank_free(key), 1)

            def turned(key, w, bias=0.0):
                move((key, w), linT[:, w * WT:(w + 1) * WT], bank((key, w))[:, :], bias=bias)

            def queries(layer, w):
                if layer:
                    act.wait_ge(sem("scaled_bq"), 1)
                    act.wait_ge(sem("v1_split"), 2)
                move((f"q{layer}", w), qproj[:, w, :], bank((f"q{layer}", w))[:, :],
                     scale=HD ** -0.5 if layer else 1.0, bias=bias_q[:, 0:1] if layer else 0.0,
                     part=qparts[:, w, 0, :])

            def maxima(layer, m):
                key = (f"max{layer}T", m)
                move(key, maxT[:, m * MB:(m + 1) * MB, :].rearrange("p b t -> p (b t)"),
                     bank(key)[0:PARTS * H, 0:MB * TOK // 2].bitcast(BF16))

            def squares(src, dst, key, n, p):
                i = norm_no[key]
                for k in range(n):
                    ins = act.activation(dst(k), src(k), ACT.Square, accum_out=sq[0:p, i, k:k + 1])
                ins.then_inc(sem("squares"), 1)

            rounds = [0]

            def round_tiles(dst, src, key, n, p):
                i = norm_no[key]
                rounds[0] += 1
                act.wait_ge(sem("quant_scales"), rounds[0])
                for k in range(n):
                    ins = act.activation(dst(k), src(k), ACT.Identity, scale=comb[0:p, i, k:k + 1],
                                         bias=magic[0:p, 0:1])
                ins.then_inc(sem("rounded"), 1)

            def probs(layer, i):
                n = layer * STEPS + i
                if i < STEPS:
                    key = prob_group(n)
                    if n >= PRING:
                        act.wait_ge(sem("pv_done"), n - PRING + 1)
                    wait_full(act, key)
                    act.activation(p32[n % PRING], bank(key)[0:NK, :], ACT.Exp).then_inc(bank_free(key), 1)
                if 0 < i <= STEPS:
                    wait_read(act, prob_group(n - 1))
                    s = (n - 1) % PRING
                    act.activation(ph[:, s, :], p32[s], ACT.Copy).then_inc(sem("prob_first"), 1)

            def hidden(n):
                if n >= EXPERTS:
                    return
                if n >= AHEAD:
                    wait_full(act, ("y", n - AHEAD))
                for c in range(CK0):
                    wait_full(act, ("h", n, c))
                    act.activation(hT[:, (CK0 * n + c) % 4, :], bank(("h", n, c))[:, :], ACT.Tanh,
                                   scale=0.5).then_inc(sem("tanh_h"), 1)

            def routed(w):
                act.wait_ge(sem("gap"), w + 1)
                act.activation(ediff[:, w, :], gap[:, w, :], ACT.Exp).then_inc(sem("ediff"), 1)

            def weighted(n):
                w, e = n // E0, n % E0
                if e == 0:
                    act.wait_ge(sem("expert_weights"), w + 1)
                    act.wait_ge(sem("v1_split"), 2)
                if n >= 2:
                    act.wait_ge(sem("added"), n - 1)
                wait_full(act, ("y", n))
                for k in range(WB):
                    ins = act.activation(ys[n % 2][:, k * D:(k + 1) * D], bank(("y", n))[:, k * D:(k + 1) * D],
                                         ACT.Copy, scale=cw[:, w, k, e:e + 1])
                ins.then_inc(bank_free(("y", n)), 1)

            def squares_post(w):
                act.wait_ge(sem("centred"), w + 1)
                squares(lambda k: mid[:, w, k, :], lambda k: lin[:, w, k, :], ("rms0", w), WB, 128)

            def round_post(w):
                round_tiles(lambda k: lin[:, w, k, :], lambda k: mid[:, w, k, :], ("rms0", w), WB, 128)

            def turned_group(key, m, bias=0.0):
                move((key, m), linT[:, m * MB * TOK:(m + 1) * MB * TOK], bank((key, m))[:, 0:MB * TOK], bias=bias)

            def ffn_gate(m):
                key = ("gate", m)
                wait_full(act, key)
                for k in range(MB):
                    b = m * MB + k
                    ins = act.activation(relu_out[:, k * TOK:(k + 1) * TOK], bank(key)[:, k * TOK:(k + 1) * TOK],
                                         ACT.Relu, bias=gatec[:, 0:1], accum_out=hs[:, b:b + 1])
                ins.then_inc(bank_free(key), 1)
                wait_read(act, key)

            act.wait_ge(sem("loaded_y"), 16)
            squares(lambda k: y[:, k, :], lambda k: yq[:, k, :], "ctx0", B, NK)
            act.wait_ge(sem("loaded_rows"), 16)
            act.activation(tg[:, :], rows[:, 3 * D:3 * D + 4], ACT.Tanh).then_inc(sem("tanh_gates"), 1)
            act.wait_ge(sem("squares"), 1)
            act.wait_ge(sem("constants"), 1)
            round_tiles(lambda k: yq[:, k, :], lambda k: y[:, k, :], "ctx0", B, NK)
            round_tiles(lambda k: lin[:, 0, k, :], lambda k: mid[:, 0, k, :], ("q0", 0), WB, 128)
            turned_context(0)
            turned("q0T", 0)
            keys(0)
            queries(0, 0)
            round_tiles(lambda k: lin[:, 1, k, :], lambda k: mid[:, 1, k, :], ("q0", 1), WB, 128)
            context_values(0, 0)
            turned("q0T", 1)
            queries(0, 1)
            maxima(0, 0)

            def beside_layer0(i):
                if i in TURNS0:
                    maxima(0, TURNS0[i])
                if i == CTX_STEP:
                    turned_context(1)
                if i == CTX_STEP + 1:
                    act.wait_ge(sem("loaded_bias1"), 16)
                    act.activation(bias_q[:, :], bias1[:, 0:1], ACT.Copy, scale=HD ** -0.5).then_inc(
                        sem("scaled_bq"), 1)
                    keys(1)
                if i == CTX_STEP + 7:
                    context_values(1, 0)
                if i == CTX_STEP + 13:
                    context_values(1, 1)
                if i == POST_STEP + 3:
                    squares_post(0)
                if i == POST_STEP + 6:
                    round_post(0)
                if i == POST_STEP + 8:
                    turned("post0T", 0)
                if i == POST_STEP + 13:
                    turned("moeT", 0)

            for i in range(STEPS + LAG):
                probs(0, i)
                beside_layer0(i)
            for n in range(AHEAD + 1):
                hidden(n)
            routed(0)
            for n in range(EXPERTS):
                if n == 1:
                    squares_post(1)
                weighted(n)
                if n:
                    hidden(n + AHEAD)
                if n == 2:
                    round_post(1)
                if n == 3:
                    turned("post0T", 1)
                if n == 5:
                    turned("moeT", 1)
                if n == 6:
                    routed(1)
                if n == E0 + 1:
                    turned("q1T", 0)
                if n == E0 + 2:
                    queries(1, 0)
            maxima(1, 0)
            act.wait_ge(sem("loaded_gatec"), 16)

            def beside_layer1(i):
                if i == 4:
                    turned("q1T", 1)
                if i == 5:
                    queries(1, 1)
                if i in TURNS1:
                    maxima(1, TURNS1[i])
                for m, step in enumerate(ENDS1):
                    if i == step:
                        turned_group("post1T", m, bias=bias1[:, 2:3])
                    if i == step + END_FFN:
                        turned_group("ffnT", m)
                    if i == step + END_FFN + 1:
                        ffn_gate(m)

            for i in range(STEPS + LAG):
                probs(1, i)
                beside_layer1(i)
            turned_group("post1T", len(ENDS1), bias=bias1[:, 2:3])
            turned_group("ffnT", len(ENDS1))
            ffn_gate(len(ENDS1))
            act.activation(bias_q[:, :], magic[:, :], ACT.Gelu_apprx_tanh)
            wait_read(act, "mb1")
            for b in range(B):
                if b >= 2:
                    wait_full(act, ("out", b - 2))
                wait_full(act, ("u", b))
                for c in range(CK1):
                    ins = act.activation(uT[:, b % 2, c, :], bank(("u", b))[:, c * TOK:(c + 1) * TOK],
                                         ACT.Gelu_apprx_tanh, bias=mb1[:, c, b:b + 1])
                ins.then_inc(bank_free(("u", b)), 1)

        @block.vector
        def _(dve):
            count = [0]

            def link(ins):
                count[0] += 1
                ins.then_inc(sem("dve_chain"), 1)
                dve.wait_ge(sem("dve_chain"), count[0])

            def split_rest(src, d0, d1, d2, r, done):
                link(dve.tensor_tensor(r, src, d0, ALU.subtract))
                link(dve.tensor_copy(d1, r))
                dve.tensor_tensor(d2, r, d1, ALU.subtract).then_inc(sem(done), 1)

            given = [0]

            def statistics(key, src, n=WB):
                i = norm_no[key]
                for k in range(n):
                    ins = dve.bn_stats(st[:, i, k, :], src(k))
                link(ins)
                for k in range(n):
                    ins = dve.bn_aggr(mv[:, i, k, :], st[:, i, k, :])
                ins.then_inc(sem("variance"), 1)
                given[0] += 1
                dve.wait_ge(sem("variance"), given[0])

            def quant_scales(key, p, n):
                i = norm_no[key]
                dve.wait_ge(sem("rstd"), i + 1)
                link(dve.tensor_tensor(am1[0:p, 0:n], amax[0:p, i, 0:n], rstd[0:p, i, 0:n], ALU.mult))
                link(dve.tensor_scalar(am1[0:p, 0:n], am1[0:p, 0:n], 1e-5, None, ALU.max))
                link(dve.reciprocal(am2[0:p, 0:n], am1[0:p, 0:n]))
                link(dve.tensor_scalar(inv[0:p, i, 0:n], am1[0:p, 0:n], 1.0 / 127.0, None, ALU.mult))
                dve.scalar_tensor_tensor(out=comb[0:p, i, 0:n], in0=am2[0:p, 0:n], scalar=127.0,
                                         in1=rstd[0:p, i, 0:n], op0=ALU.mult, op1=ALU.mult).then_inc(
                                             sem("quant_scales"), 1)

            rounds = [0]

            def dequantise(tile, key, n, p, done):
                i = norm_no[key]
                rounds[0] += 1
                dve.wait_ge(sem("rounded"), rounds[0])
                for k in range(n):
                    ins = dve.tensor_scalar(tile(k), tile(k), -MAGIC, inv[0:p, i, k:k + 1], ALU.add, ALU.mult)
                ins.then_inc(sem(done), 1)

            def split_keys0():
                for i in range(2):
                    wait_read(dve, ("k0", i))
                n = B * NK
                split_rest(kproj[:, 0:n], *(kparts[:, i, :] for i in range(PARTS)), rest[:, 0:n], "k_split")
                dve.wait_ge(sem("k_split"), 1)

            def split_values0():
                wait_read(dve, ("v0", 0))

                def view(t):
                    return t[0:NK, 0:512].rearrange("s (b h d) -> s b h d", b=B, h=KVH)

                split_rest(view(kproj), *(vst[0][:, :, :, p, 0:HD] for p in range(PARTS)), view(rest), "v_split")
                dve.wait_ge(sem("v_split"), 1)

            def normalise(key, dst, src, n=WB):
                i = norm_no[key]
                dve.wait_ge(sem("rstd"), i + 1)
                for k in range(n):
                    ins = dve.tensor_scalar(dst(k), src(k), mv[:, i, k, 0:1], rstd[:, i, k:k + 1],
                                            ALU.subtract, ALU.mult)
                return ins

            def x_tile(w):
                return lambda k: x[:, w * WB + k, :]

            def lin_tile(w):
                return lambda k: lin[:, w, k, :]

            def split_queries(layer, w):
                wait_read(dve, (f"q{layer}", w))
                split_rest(qproj[:, w, :], *(qparts[:, w, i, :] for i in range(PARTS)), rest[:, 0:WT], "q_split")
                dve.wait_ge(sem("q_split"), layer * WAVES + w + 1)

            def maxima(layer, n):
                b, c = n // len(A_SPLIT), n % len(A_SPLIT)
                h0, h1 = A_SPLIT[c]
                key = (f"A{layer}", b, c)
                wait_full(dve, key)
                v = bank(key)[:, 0:(h1 - h0) * NK].rearrange("t (h s) -> t h s", s=NK)
                dve.tensor_reduce(nmax[:, b, h0:h1], v, AX.X, ALU.max, negate=True).then_inc(bank_free(key), 1)

            def split_maxima(layer, m):
                for b in range(m * MB, (m + 1) * MB):
                    for c in range(len(A_SPLIT)):
                        wait_read(dve, (f"A{layer}", b, c))
                v, d = nmax[:, m * MB:(m + 1) * MB, :], mparts[:, m * MB:(m + 1) * MB, :, :]
                link(dve.tensor_copy(d[:, :, 0, :], v))
                split_rest(v, d[:, :, 0, :], d[:, :, 1, :], d[:, :, 2, :], mrest[:, :, :], "max_split")
                dve.wait_ge(sem("max_split"), layer * B // MB + m + 1)

            def outputs(layer, b):
                key = (f"O{layer}", b)
                dve.wait_ge(sem("pv_done"), NG * (layer * B + b + 1))
                v = bank(key)[:, 0:H * PARTS * VW].rearrange("t (h p d) -> t h d p", h=H, p=PARTS)
                dve.tensor_reduce(osum[:, :, :], v, AX.X, ALU.add).then_inc(bank_free(key), 1)
                wait_read(dve, key)
                link(dve.reciprocal(rden[:, :], osum[:, :, HD]))
                dve.tensor_tensor(attn[:, b, :].rearrange("t (h d) -> t h d", h=H), osum[:, :, 0:HD],
                                  rden[:, :].unsqueeze(2).to_broadcast([128, H, HD]), ALU.mult).then_inc(
                                      sem("attn_done"), 1)
                dve.wait_ge(sem("attn_done"), layer * B + b + 1)

            def prob_rest(layer, i):
                n = layer * STEPS + i
                if 0 < i < STEPS and n % 2:
                    n -= 1
                    dve.wait_ge(sem("prob_first"), n + 1)
                    s = n % PRING
                    dve.tensor_tensor(pl[:, s, :], p32[s], ph[:, s, :], ALU.subtract).then_inc(
                        sem("prob_rest"), 1)
                if i >= NG + LAG and (i - LAG) % NG == 0:
                    outputs(layer, (i - LAG) // NG - 1)

            def residual(key, first, n, gate):
                wait_full(dve, key)
                xs = flat(x[:, first:first + n, :])
                dve.scalar_tensor_tensor(out=xs, in0=bank(key)[:, 0:n * D], scalar=tg[:, gate:gate + 1], in1=xs,
                                         op0=ALU.mult, op1=ALU.add).then_inc(bank_free(key), 1)
                wait_read(dve, key)

            def post_start(w):
                statistics(("mid0", w), lambda k: attn[:, w * WB + k, :])

            def post_centre(w):
                v = mid[:, w, :, :]
                link(normalise(("mid0", w), lambda k: mid[:, w, k, :], lambda k: attn[:, w * WB + k, :]))
                link(dve.tensor_tensor(v, v, gamma.unsqueeze(1).to_broadcast([128, WB, D]), ALU.mult))
                dve.tensor_tensor(v, v, beta.unsqueeze(1).to_broadcast([128, WB, D]), ALU.add).then_inc(
                    sem("centred"), 1)
                dve.wait_ge(sem("centred"), w + 1)

            def post_maximum(w):
                v = mid[:, w, :, :]
                i = norm_no[("rms0", w)]
                link(dve.tensor_reduce(amax[:, i, 0:WB], v, AX.X, ALU.max, apply_absolute_value=True))

            def post_scales(w):
                quant_scales(("rms0", w), 128, WB)

            def post_quantised(w):
                dequantise(lin_tile(w), ("rms0", w), WB, 128, "lin_post0")

            def wide_e(v):
                return v.unsqueeze(2).to_broadcast([128, WB, E0])

            def experts_statistics(w):
                residual(("post0", w), w * WB, WB, 0)
                statistics(("moe", w), x_tile(w))

            def experts_norm(w):
                normalise(("moe", w), lin_tile(w), x_tile(w)).then_inc(sem("lin_moe"), 1)

            def route(w):
                rk = ("router", w)
                wait_full(dve, rk)
                dve.tensor_copy(logit[:, :, :], bank(rk)[:, 0:WB * E0].rearrange("t (b e) -> t b e", b=WB)).then_inc(
                    bank_free(rk), 1)
                wait_read(dve, rk)
                rank_b = rank.unsqueeze(1).to_broadcast([128, WB, E0])
                for pick, (lg, oh) in enumerate(((logit, oh1), (lg2, oh2))):
                    m, r = mm[:, 2 * pick, :], mm[:, 2 * pick + 1, :]
                    link(dve.tensor_reduce(m, lg[:, :, :], AX.X, ALU.max))
                    link(dve.tensor_tensor(code[:, :, :], lg[:, :, :], wide_e(m), ALU.is_equal))
                    link(dve.tensor_tensor(code[:, :, :], code[:, :, :], rank_b, ALU.mult))
                    link(dve.tensor_reduce(r, code[:, :, :], AX.X, ALU.max))
                    link(dve.tensor_tensor(oh[:, :, :], code[:, :, :], wide_e(r), ALU.is_equal))
                    if pick == 0:
                        link(dve.scalar_tensor_tensor(out=lg2[:, :, :], in0=oh1[:, :, :], scalar=-3.0e38,
                                                      in1=logit[:, :, :], op0=ALU.mult, op1=ALU.add))
                dve.tensor_tensor(gap[:, w, :], mm[:, 2, :], mm[:, 0, :], ALU.subtract).then_inc(sem("gap"), 1)

            def route_weights(w):
                dve.wait_ge(sem("ediff"), w + 1)
                link(dve.tensor_scalar(mm[:, 4, :], ediff[:, w, :], 1.0, None, ALU.add))
                link(dve.reciprocal(mm[:, 5, :], mm[:, 4, :]))
                link(dve.tensor_scalar(mm[:, 5, :], mm[:, 5, :], tg[:, 2:3], 0.5, ALU.mult, ALU.mult))
                link(dve.tensor_tensor(mm[:, 6, :], mm[:, 5, :], ediff[:, w, :], ALU.mult))
                link(dve.tensor_tensor(oh1[:, :, :], oh1[:, :, :], wide_e(mm[:, 5, :]), ALU.mult))
                link(dve.tensor_tensor(oh2[:, :, :], oh2[:, :, :], wide_e(mm[:, 6, :]), ALU.mult))
                dve.tensor_tensor(cw[:, w, :, :], oh1[:, :, :], oh2[:, :, :], ALU.add).then_inc(
                    sem("expert_weights"), 1)

            def hidden(n):
                if n >= EXPERTS:
                    return
                for c in range(CK0):
                    dve.wait_ge(sem("tanh_h"), CK0 * n + c + 1)
                    t = hT[:, (CK0 * n + c) % 4, :]
                    dve.scalar_tensor_tensor(out=t, in0=t, scalar=1.0, in1=bank(("h", n, c))[:, :], op0=ALU.add,
                                             op1=ALU.mult).then_inc(bank_free(("h", n, c)), 1)

            def queries_start(w):
                dve.wait_ge(sem("added"), (w + 1) * E0)
                statistics(("q1", w), x_tile(w))

            def queries_norm(w):
                normalise(("q1", w), lin_tile(w), x_tile(w)).then_inc(sem("lin_q1"), 1)

            def ffn_statistics(m):
                residual(("post1", m), m * MB, MB, 1)
                statistics(("ffn1", m), lambda k: x[:, m * MB + k, :], MB)

            def ffn_norm(m):
                normalise(("ffn1", m), lambda k: lin_of(m * MB + k), lambda k: x[:, m * MB + k, :], MB).then_inc(
                    sem("lin_ffn1"), 1)

            dve.wait_ge(sem("loaded_y"), 16)
            dve.tensor_reduce(amax[0:NK, 0, 0:8], y[:, :, :], AX.X, ALU.max, apply_absolute_value=True)
            dve.wait_ge(sem("loaded_w0"), 16)
            for i, (a, b) in enumerate(w0part):
                ins = dve.tensor_reduce(wsum[:, i:i + 1], w0[:, a:b], AX.X, ALU.add, apply_absolute_value=True)
            ins.then_inc(sem("wsum"), 1)
            dve.wait_ge(sem("wsum"), 1)
            quant_scales("ctx0", NK, 8)
            dve.wait_ge(sem("loaded_x"), 16)
            statistics(("q0", 0), x_tile(0))

            def centre(w):
                i = norm_no[("q0", w)]
                for k in range(WB):
                    ins = dve.tensor_scalar(mid[:, w, k, :], x_tile(w)(k), mv[:, i, k, 0:1], None, ALU.subtract)
                link(ins)
                link(dve.tensor_reduce(amax[:, i, 0:WB], mid[:, w, :, :], AX.X, ALU.max, apply_absolute_value=True))
                quant_scales(("q0", w), 128, WB)

            centre(0)
            wait_full(dve, "wsum")
            dve.tensor_scalar(wsc[:, 0:3], bank("wsum")[:, 0:3], 1.0 / (D * D), 1e-5, ALU.mult, ALU.max)
            dve.tensor_scalar(wsc[:, 3:4], bank("wsum")[:, 3:4], 1.0 / (D * KVH * HD), 1e-5, ALU.mult,
                              ALU.max).then_inc(bank_free("wsum"), 1)
            wait_read(dve, "wsum")
            link(dve.reciprocal(winv[:, :], wsc[:, :]))
            link(dve.tensor_scalar(wsc[:, 0:1], wsc[:, 0:1], HD ** -0.5, None, ALU.mult))
            dequantise(lambda k: yq[:, k, :], "ctx0", B, NK, "yq")
            for i, (a, b) in enumerate(w0part):
                ins = dve.tensor_scalar(w0q[:, a:b], w0[:, a:b], winv[:, i:i + 1], MAGIC, ALU.mult, ALU.add)
            link(ins)
            dequantise(lin_tile(0), ("q0", 0), WB, 128, "lin_q0")
            link(dve.tensor_scalar(w0q[:, :], w0q[:, :], -MAGIC, -1.0, ALU.add, ALU.max))
            for i, (a, b) in enumerate(w0part):
                ins = dve.tensor_scalar(w0q[:, a:b], w0q[:, a:b], 1.0, wsc[:, i:i + 1], ALU.min, ALU.mult)
            ins.then_inc(sem("w0q"), 1)
            statistics(("q0", 1), x_tile(1))
            centre(1)
            split_keys0()
            split_queries(0, 0)
            dequantise(lin_tile(1), ("q0", 1), WB, 128, "lin_q0")
            dve.wait_ge(sem("ones_column"), 2)
            split_values0()
            dve.wait_ge(sem("loaded_const"), 16)
            dve.tensor_copy(identb[:, :], ident).then_inc(sem("identb"), 1)
            for n in range(MB * len(A_SPLIT)):
                maxima(0, n)
            split_maxima(0, 0)
            split_queries(0, 1)
            dve.wait_ge(sem("loaded_rows"), 16)
            dve.wait_ge(sem("tanh_gates"), 1)
            dve.tensor_scalar(tgbo[:, :], bo, tg[:, 1:2], None, ALU.mult).then_inc(sem("tgbo"), 1)

            def beside_layer0(i):
                if i == POST_STEP:
                    post_start(0)
                if i == POST_STEP + 2:
                    post_centre(0)
                if i == POST_STEP + 3:
                    post_maximum(0)
                if i == POST_STEP + 5:
                    post_scales(0)
                if i == POST_STEP + 8:
                    post_quantised(0)
                if i == POST_STEP + 11:
                    experts_statistics(0)
                if i == POST_STEP + 13:
                    experts_norm(0)

            for i in range(STEPS + LAG + 1):
                for j, step in enumerate(CHUNKS0):
                    if i == step + 1:
                        maxima(0, MB * len(A_SPLIT) + j)
                if i in SPLITS0:
                    split_maxima(0, SPLITS0[i])
                prob_rest(0, i)
                beside_layer0(i)
            post_start(1)
            for n in range(AHEAD):
                hidden(n)
            post_centre(1)
            post_maximum(1)
            route(0)
            hidden(AHEAD)
            route_weights(0)
            for n in range(EXPERTS):
                if n in CHUNKS_E:
                    maxima(1, CHUNKS_E.index(n))
                if n == 2:
                    post_scales(1)
                if n == 3:
                    post_quantised(1)
                if n == 5:
                    experts_norm(1)
                if n == E0 + 3:
                    split_queries(1, 0)
                if n:
                    hidden(n + AHEAD)
                if n == 4:
                    experts_statistics(1)
                if n == 6:
                    route(1)
                if n == 7:
                    route_weights(1)
                if n == E0 - 1:
                    queries_start(0)
                if n == E0:
                    queries_norm(0)
                if n in CHUNKS_E:
                    maxima(1, CHUNKS_E.index(n) + 1)
            split_maxima(1, 0)
            queries_start(1)

            def beside_layer1(i):
                if i == 2:
                    queries_norm(1)
                if i == 6:
                    split_queries(1, 1)
                for m, step in enumerate(ENDS1):
                    if i == step + 2:
                        if m == 0:
                            dve.wait_ge(sem("bias_added"), WAVES)
                        ffn_statistics(m)
                    if i == step + END_FFN - 1:
                        ffn_norm(m)

            for i in range(STEPS + LAG + 1):
                for j, step in enumerate(CHUNKS1):
                    if i == step + 1:
                        maxima(1, MB * len(A_SPLIT) + j)
                if i in SPLITS1:
                    split_maxima(1, SPLITS1[i])
                prob_rest(1, i)
                beside_layer1(i)
            ffn_statistics(len(ENDS1))
            ffn_norm(len(ENDS1))
            dve.wait_ge(sem("loaded_gaug_b"), 16)
            wait_full(dve, "gexp")
            dve.tensor_scalar(gexp[:, :], bank("gexp")[:, 0:B], 1.0 / TOK, gatec[:, 1:2], ALU.mult,
                              ALU.add).then_inc(bank_free("gexp"), 1)
            wait_read(dve, "gexp")
            dve.tensor_tensor(gmat[:, :, :], rowsel.unsqueeze(2).to_broadcast([128, R, B]),
                              gexp[:, :].unsqueeze(1).to_broadcast([128, R, B]), ALU.mult).then_inc(sem("gmat"), 1)
            wait_full(dve, "gaug")
            dve.tensor_scalar(gaug[:, :], bank("gaug")[0:E1 + 1, 0:B], 1.0 / TOK, gaug_b[:, 0:1], ALU.mult,
                              ALU.add).then_inc(bank_free("gaug"), 1)
            for c in range(2 * NJ):
                i, j = c // NJ, c % NJ
                dve.wait_ge(sem(f"loaded_base{i}"), 16)
                if c >= 4:
                    d = c - 4
                    dve.wait_ge(sem(f"regrouped{d % 4}_{d // NJ}"), 16 * ((d % NJ) // 4 + 1))
                if c == NJ + 2:
                    wait_full(dve, "mb1")
                    dve.tensor_copy(mb1[:, :, :], bank("mb1")[:, 0:CK1 * B].rearrange(
                        "p (c b) -> p c b", c=CK1)).then_inc(bank_free("mb1"), 1)
                wait_full(dve, ("mix", c))
                dve.tensor_tensor(mixed[:, c % 4, :], bank(("mix", c))[:, :], base[i][:, j, :], ALU.add).then_inc(
                    bank_free(("mix", c)), 1)
            for b in range(B):
                wait_full(dve, ("out", b))
                dve.scalar_tensor_tensor(out=x[:, b, :], in0=bank(("out", b))[:, 0:D], scalar=tg[:, 3:4],
                                         in1=x[:, b, :], op0=ALU.mult, op1=ALU.add).then_inc(
                                             bank_free(("out", b)), 1)


def kernel(**inputs):
    import numpy as _np
    import concourse.bacc as _bacc
    from concourse import mybir as _mybir
    from concourse.bass_utils import run_bass_kernel_spmd as _run

    v = {k: _np.asarray(a) for k, a in inputs.items()}
    cat, c = _np.concatenate, _np.ascontiguousarray

    def by_dim(w, rep=1):
        n = w.shape[0] // HD
        w = _np.repeat(w.reshape(n, HD, -1), rep, axis=0)
        return w.transpose(2, 1, 0).reshape(w.shape[2], -1)

    def bias_by_dim(b):
        return b.reshape(H, HD).T.reshape(-1)

    const = _np.zeros((128, 128 + R + 8), _np.float32)
    const[:, :128] = _np.eye(128)
    const[:, 128:128 + R] = _np.tile(_np.eye(R), (E1, 1))
    const[:, 128 + R:] = _np.arange(8, 0, -1)
    one = _np.ones((1, 1), _np.float32)
    tw0 = v["L1_ffn_TW1"].transpose(0, 2, 1).reshape(E1, NJ, R, F1).transpose(0, 2, 1, 3)
    base0 = _np.repeat(v["L1_ffn_W1"].T.reshape(NJ, R, F1).transpose(1, 0, 2), B, axis=0)
    tw1 = v["L1_ffn_TW2"].reshape(E1, D, CK1, NJ, R).transpose(0, 4, 3, 2, 1)
    base1 = _np.repeat(v["L1_ffn_W2"].reshape(D, CK1, NJ, R).transpose(3, 2, 1, 0), B, axis=0)
    g2 = v["L1_ffn_gate_w2"]
    arrays = {
        "x": v["x"], "ctx": v["ctx_1024"], "const": const,
        "rows": cat([v["L0_xattn_ln_gamma"], v["L0_xattn_ln_beta"], v["L1_xattn_bo"], v["g_xattn"], v["g_ffn"]]),
        "w0": cat([by_dim(v["L0_xattn_wq"]), by_dim(v["L0_xattn_wk"], H // KVH), v["L0_xattn_wo"].T,
                   v["L0_xattn_wv"].T], 1),
        "w1": cat([by_dim(v["L1_xattn_Wq"]), by_dim(v["L1_xattn_Wk"]), v["L1_xattn_Wv"].T, v["L1_xattn_Wo"].T], 1),
        "bias1": _np.stack([bias_by_dim(v["L1_xattn_bq"]), bias_by_dim(v["L1_xattn_bk"]), v["L1_xattn_bv"]], 1),
        "router": v["L0_ffn_router_w"],
        "moe1": v["L0_ffn_w1"].transpose(1, 0, 2),
        "moe2": v["L0_ffn_w2"].reshape(E0, CK0, 128, D).transpose(2, 0, 1, 3),
        "gate1": v["L1_ffn_gate_w1"].T,
        "gatec": _np.stack([v["L1_ffn_gate_b1"], _np.repeat(v["L1_ffn_gate_b2"], R)], 1),
        "gate2": cat([_np.repeat(g2.T, R, axis=1), g2.T, _np.zeros((D, 1), _np.float32)], 1),
        "gaug_b": cat([v["L1_ffn_gate_b2"][:, None], one], 0),
        "tb": cat([cat([v["L1_ffn_Tb1"], v["L1_ffn_Tb2"]], 1),
                   cat([v["L1_ffn_b1"], v["L1_ffn_b2"]])[None]], 0),
        "tw0": tw0.reshape(128, NJ, 512), "base0": base0.reshape(128, NJ, 512),
        "tw1": tw1.reshape(128, NJ, 512), "base1": base1.reshape(128, NJ, 512),
    }
    arrays = {k: c(a) for k, a in arrays.items()}
    nc = _bacc.Bacc("TRN2", target_bir_lowering=False, num_devices=1)
    io = {k: nc.dram_tensor("in_" + k, a.shape, _mybir.dt.from_np(a.dtype), kind="ExternalInput").ap()
          for k, a in arrays.items()}
    io["out"] = nc.dram_tensor("out", (B, TOK, D), F32, kind="ExternalOutput").ap()
    build(nc, io)
    r = _run(nc, [{"in_" + k: a for k, a in arrays.items()}], core_ids=[0])
    return r.results[0]["out"]
```
